# Optimizing a Trainium2 kernel written in Bass

```python
import numpy as np
import jax
import jax.numpy as jnp

def _softmax(x, axis=-1):
    return jax.nn.softmax(x, axis=axis)

def _gelu(x):
    return jax.nn.gelu(x, approximate=True)

def _silu(x):
    return jax.nn.silu(x)

def _sigmoid(x):
    return jax.nn.sigmoid(x)

def _layernorm(x, axis=-1, eps=1e-05):
    m = jnp.mean(x, axis=axis, keepdims=True)
    v = jnp.var(x, axis=axis, keepdims=True)
    return (x - m) / jnp.sqrt(v + eps)

def _scatter_add(tgt, idx, src, axis=0):
    return tgt.at[idx].add(src)

def _segment_sum(src, seg, n):
    return jax.ops.segment_sum(src, seg, n)
kernel_name = 'mk_hybrid_d1_jaxref_r4_beceff'

def setup_inputs(seed: int=0):
    np.random.seed(seed)
    _w = jnp.asarray

    def _L0_attn_a_setup():
        import jax, jax.numpy as jnp
        import numpy as np
        import math
        _OFFSETS = list(range(41)) + [128, 96, 384]
        key = jax.random.key(seed)
        B, T, C, H = (1, 512, 256, 16)
        HD = C // H
        J = len(_OFFSETS)
        k0, k1, k2, k3 = jax.random.split(key, 4)
        x = jax.random.normal(k0, (B, T, C), jnp.float32)
        w_qkv = jax.random.normal(k1, (C, 3 * C), jnp.float32) / math.sqrt(C)
        w_out = jax.random.normal(k2, (C, C), jnp.float32) / math.sqrt(C)
        delta_vals = jnp.log1p(jnp.asarray(_OFFSETS, jnp.float32))
        alphas = jnp.concatenate([jnp.linspace(0.2, 2.0, H - 1) * 1.5, jnp.array([1.0], jnp.float32)])
        pos_bias = -delta_vals[:, None] * alphas[None, :]
        scale_embed = 0.05 * jax.random.normal(k3, (J, HD), jnp.float32)
        if_gain = jnp.ones((H,), jnp.float32)
        return {'x': x, 'w_qkv': w_qkv, 'w_out': w_out, 'pos_bias': pos_bias, 'scale_embed': scale_embed, 'if_gain': if_gain}
    _L0_attn_a_in = _L0_attn_a_setup()

    def _L0_attn_b_setup():
        import jax, jax.numpy as jnp
        import numpy as np
        B, L, D = (2, 512, 256)
        H = 16
        DH = D // H

        def rope_tables(seq_len, dim):
            inv_freq = 1.0 / 10000.0 ** (jnp.arange(0, dim, 2, dtype=jnp.float32) / dim)
            t = jnp.arange(seq_len, dtype=jnp.float32)
            freqs = jnp.outer(t, inv_freq)
            emb = jnp.concatenate([freqs, freqs], -1)
            return (jnp.cos(emb), jnp.sin(emb))

        def rotate_half(x):
            x1, x2 = (x[..., :x.shape[-1] // 2], x[..., x.shape[-1] // 2:])
            return jnp.concatenate([-x2, x1], axis=-1)
        key = jax.random.key(seed)
        k1, k2, k3 = jax.random.split(key, 3)
        x = jax.random.normal(k1, (B, L, D), dtype=jnp.float32)
        Wqkv = jax.random.normal(k2, (D, 3 * D), dtype=jnp.float32) / np.sqrt(D)
        Wo = jax.random.normal(k3, (D, D), dtype=jnp.float32) / np.sqrt(D)
        return {'x': x, 'Wqkv': Wqkv, 'Wo': Wo}
    _L0_attn_b_in = _L0_attn_b_setup()

    def _L0_ffn_setup():
        import jax, jax.numpy as jnp
        import numpy as np
        NUM_GEMMS = 8
        HIDDEN = 256
        INTER = 1024
        key = jax.random.key(seed)
        k_x, k_w1, k_b1, k_w2, k_b2 = jax.random.split(key, 5)
        x = jax.random.normal(k_x, (8, 512, HIDDEN), dtype=jnp.float32)
        s1 = 1.0 / np.sqrt(HIDDEN)
        s2 = 1.0 / np.sqrt(INTER)
        W1 = jax.random.uniform(k_w1, (NUM_GEMMS, INTER, HIDDEN), jnp.float32, -s1, s1)
        b1 = jax.random.uniform(k_b1, (NUM_GEMMS, INTER), jnp.float32, -s1, s1)
        W2 = jax.random.uniform(k_w2, (NUM_GEMMS, HIDDEN, INTER), jnp.float32, -s2, s2)
        b2 = jax.random.uniform(k_b2, (NUM_GEMMS, HIDDEN), jnp.float32, -s2, s2)
        return {'x': x, 'W1': W1, 'b1': b1, 'W2': W2, 'b2': b2}
    _L0_ffn_in = _L0_ffn_setup()
    _d = {'L0_attn_a_x': _L0_attn_a_in['x'], 'L0_attn_a_w_qkv': _L0_attn_a_in['w_qkv'], 'L0_attn_a_w_out': _L0_attn_a_in['w_out'], 'L0_attn_a_pos_bias': _L0_attn_a_in['pos_bias'], 'L0_attn_a_scale_embed': _L0_attn_a_in['scale_embed'], 'L0_attn_a_if_gain': _L0_attn_a_in['if_gain'], 'L0_attn_b_Wqkv': _L0_attn_b_in['Wqkv'], 'L0_attn_b_Wo': _L0_attn_b_in['Wo'], 'L0_ffn_W1': _L0_ffn_in['W1'], 'L0_ffn_b1': _L0_ffn_in['b1'], 'L0_ffn_W2': _L0_ffn_in['W2'], 'L0_ffn_b2': _L0_ffn_in['b2']}
    _x0 = _d['L0_attn_a_x']
    _d['L0_attn_a_x'] = jax.random.normal(jax.random.fold_in(jax.random.key(seed), 1), (2, 2048, 256), dtype=_x0.dtype)
    del _x0
    return _d

def reference(L0_attn_a_x, L0_attn_a_w_qkv, L0_attn_a_w_out, L0_attn_a_pos_bias, L0_attn_a_scale_embed, L0_attn_a_if_gain, L0_attn_b_Wqkv, L0_attn_b_Wo, L0_ffn_W1, L0_ffn_b1, L0_ffn_W2, L0_ffn_b2):

    def _L0_attn_a_ref(x, w_qkv, w_out, pos_bias, scale_embed, if_gain):
        import jax, jax.numpy as jnp
        import numpy as np
        import math
        _OFFSETS = list(range(41)) + [128, 96, 384]
        B, T, C = x.shape
        H = if_gain.shape[0]
        HD = C // H
        deltas = jnp.asarray(_OFFSETS)
        qkv = x @ w_qkv
        q, k, v = jnp.split(qkv, 3, axis=-1)
        q = q.reshape(B, T, H, HD).transpose(0, 2, 1, 3)
        k = k.reshape(B, T, H, HD).transpose(0, 2, 1, 3)
        v = v.reshape(B, T, H, HD).transpose(0, 2, 1, 3)
        idx = jnp.arange(T)[:, None] - deltas[None, :]
        valid = idx >= 0
        idxc = jnp.maximum(idx, 0)
        k_g = k[:, :, idxc]
        v_g = v[:, :, idxc]
        k_mod = k_g * (1.0 + scale_embed)
        scale = 1.0 / math.sqrt(HD)
        scores = jnp.einsum('bhtd,bhtjd->bhtj', q, k_mod) * scale
        scores = scores + pos_bias.T[None, :, None, :]
        scores = jnp.where(valid[None, None], scores, jnp.finfo(scores.dtype).min)
        attn = jax.nn.softmax(scores, axis=-1)
        out = jnp.einsum('bhtj,bhtjd->bhtd', attn, v_g)
        out = out * if_gain[None, :, None, None]
        out = out.transpose(0, 2, 1, 3).reshape(B, T, C)
        return out @ w_out

    def _L0_attn_b_ref(x, Wqkv, Wo):
        import jax, jax.numpy as jnp
        import numpy as np
        B, L, D = (2, 512, 256)
        H = 16
        DH = D // H

        def rope_tables(seq_len, dim):
            inv_freq = 1.0 / 10000.0 ** (jnp.arange(0, dim, 2, dtype=jnp.float32) / dim)
            t = jnp.arange(seq_len, dtype=jnp.float32)
            freqs = jnp.outer(t, inv_freq)
            emb = jnp.concatenate([freqs, freqs], -1)
            return (jnp.cos(emb), jnp.sin(emb))

        def rotate_half(x):
            x1, x2 = (x[..., :x.shape[-1] // 2], x[..., x.shape[-1] // 2:])
            return jnp.concatenate([-x2, x1], axis=-1)
        b, l, d = x.shape
        qkv = (x @ Wqkv).reshape(b, l, 3, H, DH)
        q, k, v = (qkv[:, :, 0], qkv[:, :, 1], qkv[:, :, 2])
        cos, sin = rope_tables(l, DH)
        cos = cos[:, None, :]
        sin = sin[:, None, :]
        q = q * cos + rotate_half(q) * sin
        k = k * cos + rotate_half(k) * sin
        scale = DH ** (-0.5)
        scores = jnp.einsum('bqhd,bkhd->bhqk', q, k) * scale
        attn = jax.nn.softmax(scores, axis=-1)
        out = jnp.einsum('bhqk,bkhd->bqhd', attn, v)
        out = out.reshape(b, l, d)
        return out @ Wo

    def _L0_ffn_ref(x, W1, b1, W2, b2):
        import jax, jax.numpy as jnp
        import numpy as np
        NUM_GEMMS = 8
        HIDDEN = 256
        INTER = 1024
        orig_shape = x.shape
        token_num = int(np.prod(orig_shape[:-1]))
        m = token_num // NUM_GEMMS
        xg = x.reshape(NUM_GEMMS, m, HIDDEN)
        h1 = jnp.einsum('gmh,goh->gmo', xg, W1) + b1[:, None, :]
        h2 = jnp.einsum('gmo,gho->gmh', h1, W2) + b2[:, None, :]
        return h2.reshape(orig_shape)
    x = L0_attn_a_x
    x = x + _L0_attn_a_ref(_layernorm(x, axis=-1), L0_attn_a_w_qkv, L0_attn_a_w_out, L0_attn_a_pos_bias, L0_attn_a_scale_embed, L0_attn_a_if_gain)
    x = x + _L0_ffn_ref(_layernorm(x, axis=-1), L0_ffn_W1, L0_ffn_b1, L0_ffn_W2, L0_ffn_b2)
    x = x + _L0_attn_b_ref(_layernorm(x, axis=-1), L0_attn_b_Wqkv, L0_attn_b_Wo)
    x = x + _L0_ffn_ref(_layernorm(x, axis=-1), L0_ffn_W1, L0_ffn_b1, L0_ffn_W2, L0_ffn_b2)
    return x

_drawn_inputs = setup_inputs


def setup_inputs(seed=0):
    import zlib

    import numpy as np

    out = dict(_drawn_inputs(seed))
    spreads = {'L0_attn_a_if_gain': (1.0, 0.2)}
    factors = {'L0_attn_a_scale_embed': 3.544}
    for name, (base, spread) in spreads.items():
        noise = np.random.default_rng([zlib.crc32(name.encode()), seed]).standard_normal(out[name].shape)
        drawn = base * np.exp(spread * noise) if base else spread * noise
        out[name] = jnp.asarray(drawn.astype(out[name].dtype))
    for name, factor in factors.items():
        out[name] = (out[name] * factor).astype(out[name].dtype)
    return out
```

```python
from contextlib import ExitStack

import numpy as np
import concourse.bass as bass
from concourse import mybir

F32 = mybir.dt.float32
BF16 = mybir.dt.bfloat16
ALU = mybir.AluOpType
ACT = mybir.ActivationFunctionType
AX_X = mybir.AxisListType.X

P = 128
BATCH, T, C = 2, 2048, 256
H, HD = 16, 16
KC = C // P
CH = 512
NCH = T // CH
TILES = CH // P
OFFSETS = list(range(41)) + [128, 96, 384]
J = len(OFFSETS)
NEAR = 41
PAD = 384
GRP, HG = 4, H // 4
SLOT = 32
INTER = 1024
NG = 8
EPS = 1e-5
PARTS = 3
BANK_J = 16
BANKS = [min(BANK_J, J - BANK_J * k) for k in range((J + BANK_J - 1) // BANK_J)]
EBW = 3 * P - 1
Q_STACK = [0, 0, 0, 1, 1, 2]
K_STACK = [0, 1, 2, 0, 1, 0]
KROWS = 6 * HD


PRODUCTS = [(c, bank, r, g) for c in range(KC) for bank in range(len(BANKS)) for r in range(4)
            for g in range(BANKS[bank] // 4)]
ON_POOL = [(k * 29) % 88 < 29 for k in range(len(PRODUCTS))]
N_DVE, N_POOL = ON_POOL.count(False), ON_POOL.count(True)
RING = 4
SUMMED = []
for _unit in range(KC * len(BANKS)):
    _n = sum(1 for c, bank, _, _ in PRODUCTS if c * len(BANKS) + bank <= _unit)
    SUMMED.append((ON_POOL[:_n].count(False), ON_POOL[:_n].count(True)))


def fold_ffn(nc, W1, W2T, b1, b2, mt_d, bc_d):
    OC = INTER // P
    with ExitStack() as ctx:
        sb = lambda n, s, d: ctx.enter_context(nc.sbuf_tensor(n, s, d))
        sem = lambda n: ctx.enter_context(nc.semaphore(n))
        w1 = sb("w1", [P, 2, OC, C], F32)
        w2 = sb("w2", [P, 2, OC, C], F32)
        b1s = sb("b1s", [P, 2, OC], F32)
        b2s = sb("b2s", [1, 2, C], F32)
        mt = sb("mt", [P, 2, KC, C], F32)
        bc = sb("bc", [1, 2, C], F32)
        ps = ctx.enter_context(nc.psum_tensor("fold_ps", [P, 2, 4, CH], F32))
        loaded = [sem("fold_loaded0"), sem("fold_loaded1")]
        mm_done, evac, stored = sem("fold_mm"), sem("fold_evac"), sem("fold_stored")
        start = sem("fold_start")
        block = ctx.enter_context(nc.Block())

        @block.sync
        def _(sp):
            with sp.Fori(0, NG // 2) as i:
                for s in range(2):
                    g = i * 2 + s
                    sp.wait_ge(evac, i * 2 + s + 1)
                    sp.dma_start(w1[:, s], W1[g].rearrange("(k p) n -> p k n", p=P)).then_inc(loaded[s], 16)
                    sp.dma_start(w2[:, s], W2T[g].rearrange("(k p) n -> p k n", p=P)).then_inc(loaded[s], 16)
                    sp.dma_start(b1s[:, s], b1[g]).then_inc(loaded[s], 16)
                    sp.dma_start(b2s[:, s], b2[g].unsqueeze(0)).then_inc(loaded[s], 16)

        @block.tensor
        def _(pe):
            pe.wait_ge(start, 1)
            pe.sem_inc(mm_done, 2)
            with pe.Fori(0, NG // 2) as i:
                for s in range(2):
                    pe.wait_ge(loaded[s], i * 64 + 64)
                    pe.wait_ge(evac, i * 2 + s + 1)
                    for m in range(KC):
                        for k in range(OC):
                            pe.matmul(ps[:, s, m, 0:C], w1[:, s, k, m * P:(m + 1) * P], w2[:, s, k, :],
                                      start=(k == 0), stop=(k == OC - 1))
                    for k in range(OC):
                        last = pe.matmul(ps[0:1, s, 2, 0:C], b1s[:, s, k:k + 1], w2[:, s, k, :],
                                         start=(k == 0), stop=(k == OC - 1))
                    last.then_inc(mm_done, 1)

        @block.vector
        def _(dve):
            dve.sem_inc(start, 1)
            dve.sem_inc(evac, 2)
            dve.sem_inc(stored, 64)
            with dve.Fori(0, NG // 2) as i:
                for s in range(2):
                    dve.wait_ge(mm_done, i * 2 + s + 3)
                    dve.wait_ge(stored, i * 64 + 64)
                    dve.tensor_copy(mt[:, s], ps[:, s, 0:KC, 0:C])
                    dve.tensor_tensor(bc[:, s], ps[0:1, s, 2, 0:C], b2s[:, s], ALU.add).then_inc(evac, 1)

        @block.scalar
        def _(act):
            with act.Fori(0, NG // 2) as i:
                for s in range(2):
                    g = i * 2 + s
                    act.wait_ge(evac, i * 2 + s + 3)
                    act.dma_start(mt_d[g].rearrange("(k p) n -> p k n", p=P), mt[:, s]).then_inc(stored, 16)
                    act.dma_start(bc_d[g].unsqueeze(0), bc[:, s]).then_inc(stored, 16)
            act.wait_ge(stored, 64 + 32 * NG)


def layer_norm(nc, ctx, sb, sem, PS, mean_bank, var_bank, ones, eps, xc, per_chunk):
    xm = sb("xm", [P, KC, CH], F32)
    sq = sb("sq", [P, KC, CH], F32)
    sd = sb("sd", [P, CH], F32)
    rs = sb("rs", [P, CH], F32)
    xn = sb("xn", [P, KC, CH], F32)
    mean_ps, centered, squared, var_ps, sd_ready, rs_ready, xn_ready = (
        sem(n) for n in ("mean_ps", "centered", "squared", "var_ps", "sd_ready", "rs_ready", "xn_ready"))
    wide = lambda v: v.unsqueeze(1).broadcast_to([P, KC, CH])

    def on_pe(pe, it, l):
        n = it * per_chunk + (l + 1)
        for k in range(KC):
            mm = pe.matmul(PS[:, mean_bank, :], ones[:, :], xc[:, k, :], start=(k == 0), stop=(k == KC - 1))
        mm.then_inc(mean_ps, 1)
        pe.wait_ge(squared, n)
        for k in range(KC):
            mm = pe.matmul(PS[:, var_bank, :], ones[:, :], sq[:, k, :], start=(k == 0), stop=(k == KC - 1))
        mm.then_inc(var_ps, 1)
        pe.wait_ge(xn_ready, n)

    def on_act(act, it, l):
        n = it * per_chunk + (l + 1)
        act.wait_ge(centered, n)
        act.activation(sq[:, :, :], xm[:, :, :], ACT.Square).then_inc(squared, 1)
        act.wait_ge(var_ps, n)
        act.activation(sd[:, :], PS[:, var_bank, :], ACT.Sqrt, bias=eps[:, 0:1]).then_inc(sd_ready, 1)

    def on_dve(dve, it, l):
        n = it * per_chunk + (l + 1)
        dve.wait_ge(mean_ps, n)
        dve.tensor_tensor(xm[:, :, :], xc[:, :, :], wide(PS[:, mean_bank, :]), ALU.subtract).then_inc(centered, 1)
        dve.wait_ge(sd_ready, n)
        dve.reciprocal(rs[:, :], sd[:, :]).then_inc(rs_ready, 1)
        dve.wait_ge(rs_ready, n)
        dve.tensor_tensor(xn[:, :, :], xm[:, :, :], wide(rs[:, :]), ALU.mult).then_inc(xn_ready, 1)

    return xn, on_pe, on_act, on_dve


def local_stage(nc, I, D):
    with ExitStack() as ctx:
        sb = lambda n, s, d: ctx.enter_context(nc.sbuf_tensor(n, s, d))
        sem = lambda n: ctx.enter_context(nc.semaphore(n))
        PS = ctx.enter_context(nc.psum_tensor("PSa", [P, 8, CH], F32))
        TP = PS[:, 3, :].bitcast(BF16).rearrange("p (h t) -> p h t", h=8)

        ones = sb("ones", [P, P], F32)
        eps = sb("eps", [P, 1], F32)
        ident = sb("ident", [P, P], F32)
        identb = sb("identb", [P, P], BF16)
        band = sb("band", [PARTS * NEAR, EBW], BF16)
        wqkv = sb("wqkv", [P, KC, 3 * C], F32)
        wo = sb("wo", [P, HG, C], F32)
        wqkv_b = sb("wqkv_b", [P, KC, 3 * C], F32)
        wrot = sb("wrot", [P, KC, 2 * C], F32)
        hmask = sb("hmask", [P, 8], F32)
        se_t = sb("se_t", [P, J], F32)
        se_w = sb("se_w", [P, J], F32)
        sj = sb("sj", [P, J, SLOT], F32)
        pbias = sb("pbias", [P, KC, J, 8], F32)
        vmask = sb("vmask", [P, T // P, J], F32)
        gain = sb("gain", [P, H], F32)
        xc = sb("xc", [P, KC, CH], F32)
        cosc = sb("cosc", [P, CH], F32)
        sinc = sb("sinc", [P, CH], F32)
        mtc = sb("mtc", [P, KC, C], F32)
        bcc = sb("bcc", [P, KC], F32)
        qT = sb("qT", [P, KC, CH], F32)
        kT = sb("kT", [P, KC, PAD + T], F32)
        prod_d = sb("prod_d", [P, RING, CH], F32)
        prod_p = sb("prod_p", [P, RING, CH], F32)
        sc = sb("sc", [P, 2 * len(BANKS), CH], F32)
        lg = sb("lg", [P, KC, J, 8], F32)
        red = sb("red", [P, 4, H], F32)
        attn = sb("attn", [P, H, J], F32)
        rest = sb("rest", [P, H, NEAR], F32)
        parts = sb("parts", [P, H, PARTS, NEAR], BF16)
        parts_t = sb("parts_t", [PARTS * NEAR, H, P], BF16)
        a0 = sb("a0", [P, H, P], F32)
        a1 = sb("a1", [P, H, NEAR - 1], F32)
        vnew = sb("vnew", [P, TILES, H, SLOT], F32)
        v7 = sb("v7", [P, TILES + 3, H, SLOT], F32)
        v96 = sb("v96", [P, TILES, H, SLOT], F32)
        far = sb("far", [P, H, SLOT], F32)
        fart = sb("fart", [P, H, HD], F32)
        oT = sb("oT", [P, HG, CH], F32)
        rope_a = sb("rope_a", [P, CH], F32)
        rope_b = sb("rope_b", [P, CH], F32)
        rope_q = sb("rope_q", [P, CH], F32)
        rope_r = sb("rope_r", [P, CH], F32)
        qparts = sb("qparts", [P, PARTS, CH], BF16)
        vb = sb("vb", [P, TILES, H, SLOT], F32)

        const_ld, filled, made = sem("const_ld"), sem("filled"), sem("made")
        stored = sem("stored")
        chunk_ld, v_stored, v_ld = sem("chunk_ld"), sem("v_stored"), sem("v_ld")
        qk_ps, qk_sb, v_ps, v_sb = sem("qk_ps"), sem("qk_sb"), sem("v_ps"), sem("v_sb")
        prod_d_ready, prod_d_used = sem("prod_d_ready"), sem("prod_d_used")
        prod_p_ready, prod_p_used = sem("prod_p_ready"), sem("prod_p_used")
        sc_sb, l_ps, lg_ready = sem("sc_sb"), sem("l_ps"), sem("lg_ready")
        lg_shifted, exp_ready, attn_ready = sem("lg_shifted"), sem("exp_ready"), sem("attn_ready")
        part_cast, rest_ready, parts_ready = sem("part_cast"), sem("rest_ready"), sem("parts_ready")
        tp_ps, tp_sb, sp_ps, a_sb = sem("tp_ps"), sem("tp_sb"), sem("sp_ps"), sem("a_sb")
        far_step, far_ready, pv_ps, o_sb = sem("far_step"), sem("far_ready"), sem("pv_ps"), sem("o_sb")
        y_ps, ffn_ps, x_updated, dve_step = sem("y_ps"), sem("ffn_ps"), sem("x_updated"), sem("dve_step")
        qkb_ps, qkb_read, rope_cast, rope_rest, qparts_ready = (
            sem("qkb_ps"), sem("qkb_read"), sem("rope_cast"), sem("rope_rest"), sem("qparts_ready"))
        qparts_stored, vb_ps, vb_sb = sem("qparts_stored"), sem("vb_ps"), sem("vb_sb")

        xn, ln_pe, ln_act, ln_dve = layer_norm(nc, ctx, sb, sem, PS, 4, 5, ones, eps, xc, 3)
        block = ctx.enter_context(nc.Block())
        PAD_STORES = 2
        STORES = 2
        N_CONST = 11 + 8 + GRP * HG
        QKD = [D["q_d"], D["k_d"]]

        def chunk_start(eng, it):
            eng.wait_ge(stored, it * (16 * STORES) + 16 * PAD_STORES)

        def chunks(eng):
            return eng.Fori(0, BATCH), eng.Fori(0, NCH)

        @block.sync
        def _(sp):
            def const(dst, src):
                sp.dma_start(dst, src).then_inc(const_ld, 16)
            const(ident[:, :], I["ident"])
            const(identb[:, :], I["identb"])
            const(band[:, :], I["band"])
            const(wqkv[:, :, :], I["wqkv"].rearrange("(k p) n -> p k n", p=P))
            const(wqkv_b[:, :, :], I["wqkv_b"].rearrange("(k p) n -> p k n", p=P))
            const(wrot[:, :, :], I["wrot"].rearrange("(k p) n -> p k n", p=P))
            const(hmask[:, :], I["hmask"])
            const(vmask[:, :, :], I["vmask"])
            const(gain[:, :], I["gain"].partition_broadcast(P))
            for c in range(KC):
                const(pbias[:, c], I["pos_bias"][:, 8 * c:8 * c + 8].partition_broadcast(P))
            sp.wait_ge(filled, 1)
            for h in range(8):
                const(se_t[HD * h:HD * (h + 1), :], I["se_t"])
            for j in range(GRP):
                for g in range(HG):
                    const(wo[SLOT * j:SLOT * j + HD, g, :],
                          I["wo"][HD * (GRP * g + j):HD * (GRP * g + j + 1), :])
            sp.wait_ge(filled, 2)
            for b in range(BATCH):
                sp.dma_start(D["v_d"][b, 0:PAD, :].rearrange("(k p) n -> p k n", p=P),
                             vnew[:, 0:3].rearrange("p k h d -> p k (h d)")).then_inc(stored, 16)
            fb, fn = chunks(sp)
            with fb as b:
                with sp.Fori(0, NCH) as n:
                    it = b * NCH + n
                    chunk_start(sp, it)
                    cols = bass.ds(it * CH, CH)
                    sp.dma_start(xc[:, :, :], I["xT"][:, cols].rearrange("(k p) t -> p k t", p=P)).then_inc(chunk_ld, 16)
                    sp.dma_start(cosc[:, :], I["cosT"][:, bass.ds(n * CH, CH)]).then_inc(chunk_ld, 16)
                    sp.dma_start(sinc[:, :], I["sinT"][:, bass.ds(n * CH, CH)]).then_inc(chunk_ld, 16)
                    sp.dma_start(mtc[:, :, :], D["mt_d"][it].rearrange("(k p) n -> p k n", p=P)).then_inc(chunk_ld, 16)
                    sp.dma_start(bcc[:, :], D["bc_d"][it].rearrange("(k p) -> p k", p=P),
                                 allow_slow_non_contiguous=True).then_inc(chunk_ld, 16)
                    sp.wait_ge(v_sb, it * 2 + 2)
                    sp.dma_start(D["v_d"][b, bass.ds(n * CH + PAD, CH), :].rearrange("(k p) n -> p k n", p=P),
                                 vnew[:, :, :, :].rearrange("p k h d -> p k (h d)")).then_inc(v_stored, 16)
                    sp.wait_ge(v_stored, it * 16 + 16)
                    sp.dma_start(v7[:, :, :, :].rearrange("p k h d -> p k (h d)"),
                                 D["v_d"][b, bass.ds(n * CH, CH + PAD), :].rearrange("(k p) n -> p k n", p=P)).then_inc(v_ld, 16)
                    sp.dma_start(v96[:, :, :, :].rearrange("p k h d -> p k (h d)"),
                                 D["v_d"][b, bass.ds(n * CH + PAD - 96, CH), :].rearrange("(k p) n -> p k n", p=P)).then_inc(v_ld, 16)
                    sp.wait_ge(x_updated, it * 2 + 2)
                    sp.dma_start(D["x_d"][:, cols].rearrange("(k p) t -> p k t", p=P), xc[:, :, :]).then_inc(stored, 16)
                    for u in range(4):
                        sp.wait_ge(qparts_ready, it * 4 + u + 1)
                        dst = QKD[u // 2][b, :, (u % 2) * P:(u % 2 + 1) * P, bass.ds(n * CH, CH)]
                        sp.dma_start(dst.rearrange("s p t -> p s t"), qparts[:, :, :]).then_inc(qparts_stored, 16)
                    sp.wait_ge(vb_sb, it * 2 + 2)
                    sp.wait_ge(qparts_stored, it * 64 + 64)
                    sp.dma_start(D["vb_d"][b, bass.ds(n * CH, CH), :].rearrange("(k p) n -> p k n", p=P),
                                 vb[:, :, :, :].rearrange("p k h d -> p k (h d)")).then_inc(stored, 16)
            sp.wait_ge(stored, 16 * PAD_STORES + 16 * STORES * NG)

        @block.gpsimd
        def _(pool):
            pool.memset(wo[:, :, :], 0.0)
            pool.memset(ones[:, :], 1.0 / C).then_inc(filled, 1)
            pool.memset(vnew[:, :, :, :], 0.0).then_inc(filled, 1)
            pool.memset(kT[:, :, 0:PAD], 0.0)
            pool.memset(eps[:, :], EPS)
            pool.memset(far[:, :, :], 0.0)
            pool.memset(sj[:, :, :], 0.0).then_inc(filled, 1)
            pool.memset(vb[:, :, :, :], 0.0).then_inc(filled, 1)
            pool.wait_ge(filled, 4)
            pool.memset(vb[:, :, :, HD:HD + 1], 1.0).then_inc(filled, 1)
            pool.wait_ge(const_ld, 16 * N_CONST)
            pool.tensor_scalar(se_w[:, :], se_t[:, :], HD ** -0.5, HD ** -0.5, ALU.mult, ALU.add).then_inc(made, 1)
            pool.wait_ge(made, 1)
            for r in range(4):
                view = sj[:, :, :].rearrange("p (a r) (s h) -> p a r s h", r=4, s=4)[:, :, r, r, :]
                w = se_w[:, :].rearrange("p (a r) -> p a r", r=4)[:, :, r]
                pool.tensor_tensor(view, w.unsqueeze(2).broadcast_to([P, J // 4, 8]),
                                   hmask[:, :].unsqueeze(1).broadcast_to([P, J // 4, 8]), ALU.mult).then_inc(made, 1)
            with pool.Fori(0, BATCH) as b:
                with pool.Fori(0, NCH) as n:
                    it = b * NCH + n
                    chunk_start(pool, it)
                    pool.wait_ge(qk_sb, it * 4 + 4)
                    k = 0
                    for m, (c, bank, r, g) in enumerate(PRODUCTS):
                        if ON_POOL[m]:
                            if k >= RING:
                                pool.wait_ge(prod_p_used, it * N_POOL + (k - RING + 1))
                            off = OFFSETS[BANK_J * bank + 4 * g + r]
                            pool.tensor_tensor(prod_p[:, k % RING, :], qT[:, c, :],
                                               kT[:, c, bass.ds(n * CH + (PAD - off), CH)], ALU.mult).then_inc(prod_p_ready, 1)
                            k += 1
                    pool.wait_ge(v_ld, it * 32 + 32)
                    for u in range(TILES):
                        t = it * TILES + u
                        pool.wait_ge(attn_ready, t + 1)
                        if u:
                            pool.wait_ge(pv_ps, t)
                        for f, src in enumerate((v7[:, u + 2], v96[:, u], v7[:, u])):
                            w = attn[:, :, NEAR + f:NEAR + f + 1].broadcast_to([P, H, HD])
                            dst = far[:, :, 0:HD] if f == 0 else fart[:, :, :]
                            pool.tensor_tensor(dst, w, src[:, :, 0:HD], ALU.mult).then_inc(far_step, 1)
                            if f:
                                pool.wait_ge(far_step, t * 5 + 2 * f)
                                i = pool.tensor_tensor(far[:, :, 0:HD], far[:, :, 0:HD], fart[:, :, :], ALU.add)
                                i.then_inc(far_step, 1)
                                pool.wait_ge(far_step, t * 5 + 2 * f + 1)
                        pool.sem_inc(far_ready, 1)

        @block.tensor
        def _(pe):
            pe.wait_ge(filled, 5)
            pe.wait_ge(const_ld, 16 * N_CONST)
            pe.wait_ge(made, 5)
            with pe.Fori(0, BATCH) as b:
                with pe.Fori(0, NCH) as n:
                    it = b * NCH + n
                    chunk_start(pe, it)
                    pe.wait_ge(chunk_ld, it * 80 + 80)
                    ln_pe(pe, it, 0)
                    for u in range(4):
                        for k in range(KC):
                            mm = pe.matmul(PS[:, u, :], wqkv[:, k, u * P:(u + 1) * P], xn[:, k, :],
                                           start=(k == 0), stop=(k == KC - 1))
                        mm.then_inc(qk_ps, 1)
                    for s in range(TILES):
                        for k in range(KC):
                            mm = pe.matmul(PS[:, 6 + s // 2, (s % 2) * C:(s % 2 + 1) * C], xn[:, k, s * P:(s + 1) * P],
                                           wqkv[:, k, 2 * C:3 * C], start=(k == 0), stop=(k == KC - 1))
                        mm.then_inc(v_ps, 1)
                    kd = kp = 0
                    for m, (c, bank, r, g) in enumerate(PRODUCTS):
                        unit = c * len(BANKS) + bank
                        if r == 0 and g == 0 and unit >= 2:
                            pe.wait_ge(sc_sb, it * 6 + (unit - 1))
                        if ON_POOL[m]:
                            pe.wait_ge(prod_p_ready, it * N_POOL + (kp + 1))
                            rhs, used = prod_p[:, kp % RING, :], prod_p_used
                            kp += 1
                        else:
                            pe.wait_ge(prod_d_ready, it * N_DVE + (kd + 1))
                            rhs, used = prod_d[:, kd % RING, :], prod_d_used
                            kd += 1
                        j = BANK_J * bank + 4 * g + r
                        pe.matmul(PS[SLOT * g:SLOT * (g + 1), unit % 2, :], sj[:, j, :], rhs,
                                  start=(r == 0), stop=(r == 3)).then_inc(used, 1)
                    for u in range(TILES):
                        t = it * TILES + u
                        for c in range(KC):
                            pe.wait_ge(sc_sb, it * 6 + 3 * (c + 1))
                            if u or c:
                                pe.wait_ge(lg_ready, t * 2 + c)
                            for bank, nj in enumerate(BANKS):
                                mrows = 8 * nj
                                tr = pe.transpose(PS[:, 2, bank * P:bank * P + mrows],
                                                  sc[0:mrows, 3 * c + bank, u * P:(u + 1) * P], ident[0:mrows, 0:mrows])
                            tr.then_inc(l_ps, 1)
                        pe.wait_ge(parts_ready, t + 1)
                        for half in range(2):
                            if u or half:
                                pe.wait_ge(tp_sb, t * 2 + half)
                            for h in range(8):
                                tr = pe.transpose(TP[0:PARTS * NEAR, h, :],
                                                  parts[:, 8 * half + h].rearrange("p s j -> p (s j)"), identb[:, :])
                            tr.then_inc(tp_ps, 1)
                        pe.wait_ge(tp_sb, t * 2 + 2)
                        for q in range(6):
                            if q >= 3:
                                pe.wait_ge(a_sb, t * 6 + (q - 2))
                            first = 32 * q if q < 4 else 32 * (q - 4)
                            for tt in range(first, min(first + 32, P if q < 4 else NEAR - 1)):
                                a = (2 * P - 1 - tt) if q < 4 else (P - 1 - tt)
                                mm = pe.matmul(PS[:, 4 + q % 3, (tt - first) * H:(tt - first + 1) * H],
                                               band[:, a:a + P], parts_t[:, :, tt], start=True, stop=True)
                            mm.then_inc(sp_ps, 1)
                        pe.wait_ge(a_sb, t * 6 + 6)
                        pe.wait_ge(v_ld, it * 32 + 32)
                        pe.wait_ge(far_ready, t + 1)
                        if u:
                            pe.wait_ge(o_sb, t)
                        for g in range(HG):
                            for step in range(3):
                                for jh in range(GRP):
                                    h = GRP * g + jh
                                    out = PS[SLOT * jh:SLOT * (jh + 1), 7, g * P:(g + 1) * P]
                                    if step == 0:
                                        pe.matmul(out, v7[:, u + 3, h, :], a0[:, h, :], start=True, stop=False)
                                    elif step == 1:
                                        pe.matmul(out[:, 0:NEAR - 1], v7[:, u + 2, h, :], a1[:, h, :], start=False, stop=False)
                                    else:
                                        mm = pe.matmul(out, far[:, h, :], ident[:, :], start=False, stop=True)
                        mm.then_inc(pv_ps, 1)
                    pe.wait_ge(o_sb, it * TILES + TILES)
                    for m in range(KC):
                        for g in range(HG):
                            mm = pe.matmul(PS[:, m, :], wo[:, g, m * P:(m + 1) * P], oT[:, g, :],
                                           start=(g == 0), stop=(g == HG - 1))
                        mm.then_inc(y_ps, 1)
                    pe.wait_ge(x_updated, it * 2 + 1)
                    ln_pe(pe, it, 1)
                    for m in range(KC):
                        for k in range(KC):
                            mm = pe.matmul(PS[:, 2 + m, :], mtc[:, k, m * P:(m + 1) * P], xn[:, k, :],
                                           start=(k == 0), stop=(k == KC - 1))
                        mm.then_inc(ffn_ps, 1)
                    pe.wait_ge(x_updated, it * 2 + 2)
                    ln_pe(pe, it, 2)
                    for u in range(4):
                        if u >= 2:
                            pe.wait_ge(qkb_read, it * 4 + (u - 1))
                        for w, bank in ((wqkv_b, 2 * (u % 2)), (wrot, 2 * (u % 2) + 1)):
                            for k in range(KC):
                                mm = pe.matmul(PS[:, bank, :], w[:, k, u * P:(u + 1) * P], xn[:, k, :],
                                               start=(k == 0), stop=(k == KC - 1))
                        mm.then_inc(qkb_ps, 1)
                    for s in range(TILES):
                        for k in range(KC):
                            mm = pe.matmul(PS[:, 6 + s // 2, (s % 2) * C:(s % 2 + 1) * C], xn[:, k, s * P:(s + 1) * P],
                                           wqkv_b[:, k, 2 * C:3 * C], start=(k == 0), stop=(k == KC - 1))
                        mm.then_inc(vb_ps, 1)

        @block.scalar
        def _(act):
            act.wait_ge(filled, 5)
            with act.Fori(0, BATCH) as b:
                with act.Fori(0, NCH) as n:
                    it = b * NCH + n
                    chunk_start(act, it)
                    ln_act(act, it, 0)
                    for u in range(4):
                        act.wait_ge(qk_ps, it * 4 + (u + 1))
                        dst = qT[:, u, :] if u < 2 else kT[:, u - 2, bass.ds(n * CH + PAD, CH)]
                        act.copy(dst, PS[:, u, :]).then_inc(qk_sb, 1)
                    for s in range(2):
                        act.wait_ge(v_ps, it * 4 + (2 * s + 2))
                        act.copy(vnew[:, 2 * s:2 * s + 2, :, 0:HD],
                                 PS[:, 6 + s, :].rearrange("p (s h d) -> p s h d", s=2, d=HD)).then_inc(v_sb, 1)
                    for unit in range(2 * len(BANKS)):
                        act.wait_ge(prod_d_used, it * N_DVE + SUMMED[unit][0])
                        act.wait_ge(prod_p_used, it * N_POOL + SUMMED[unit][1])
                        rows = 8 * BANKS[unit % 3]
                        act.copy(sc[0:rows, unit, :], PS[0:rows, unit % 2, :]).then_inc(sc_sb, 1)
                    for u in range(TILES):
                        t = it * TILES + u
                        act.wait_ge(lg_shifted, t + 1)
                        for c in range(KC):
                            e = act.activation(attn[:, 8 * c:8 * c + 8, :], lg[:, c].rearrange("p j h -> p h j"), ACT.Exp)
                        e.then_inc(exp_ready, 1)
                        act.wait_ge(attn_ready, t + 1)
                        act.copy(parts[:, :, 0, :], attn[:, :, 0:NEAR]).then_inc(part_cast, 1)
                        act.wait_ge(rest_ready, t + 1)
                        act.copy(parts[:, :, 1, :], rest[:, :, :]).then_inc(part_cast, 1)
                        for q in range(6):
                            act.wait_ge(sp_ps, t * 6 + (q + 1))
                            nt = 32 if q < 5 else NEAR - 1 - 32
                            dst = a0[:, :, 32 * q:32 * q + 32] if q < 4 else a1[:, :, 32 * (q - 4):32 * (q - 4) + nt]
                            act.copy(dst, PS[:, 4 + q % 3, 0:nt * H].rearrange("p (t h) -> p h t", h=H)).then_inc(a_sb, 1)
                    ln_act(act, it, 1)
                    ln_act(act, it, 2)
                    for u in range(4):
                        act.wait_ge(rope_rest, it * 8 + 2 * u + 1)
                        act.copy(qparts[:, 0, :], rope_q[:, :]).then_inc(rope_cast, 1)
                        act.wait_ge(rope_rest, it * 8 + 2 * u + 2)
                        act.copy(qparts[:, 1, :], rope_r[:, :]).then_inc(rope_cast, 1)
                    for s in range(2):
                        act.wait_ge(vb_ps, it * 4 + (2 * s + 2))
                        act.copy(vb[:, 2 * s:2 * s + 2, :, 0:HD],
                                 PS[:, 6 + s, :].rearrange("p (s h d) -> p s h d", s=2, d=HD)).then_inc(vb_sb, 1)

        STEPS = TILES * 6 + 4 * 2

        @block.vector
        def _(dve):
            dve.wait_ge(filled, 5)
            dve.wait_ge(const_ld, 16 * N_CONST)
            with dve.Fori(0, BATCH) as b:
                with dve.Fori(0, NCH) as n:
                    it = b * NCH + n
                    count = [0]

                    def then(ins):
                        count[0] += 1
                        ins.then_inc(dve_step, 1)
                        dve.wait_ge(dve_step, it * STEPS + count[0])

                    chunk_start(dve, it)
                    dve.wait_ge(chunk_ld, it * 80 + 80)
                    ln_dve(dve, it, 0)
                    dve.wait_ge(qk_sb, it * 4 + 4)
                    k = 0
                    for m, (c, bank, r, g) in enumerate(PRODUCTS):
                        if not ON_POOL[m]:
                            if k >= RING:
                                dve.wait_ge(prod_d_used, it * N_DVE + (k - RING + 1))
                            off = OFFSETS[BANK_J * bank + 4 * g + r]
                            dve.tensor_tensor(prod_d[:, k % RING, :], qT[:, c, :],
                                              kT[:, c, bass.ds(n * CH + (PAD - off), CH)], ALU.mult).then_inc(prod_d_ready, 1)
                            k += 1
                    for u in range(TILES):
                        t = it * TILES + u
                        for c in range(KC):
                            dve.wait_ge(l_ps, t * 2 + (c + 1))
                            dve.tensor_tensor(lg[:, c].rearrange("p j h -> p (j h)"), PS[:, 2, 0:8 * J],
                                              pbias[:, c].rearrange("p j h -> p (j h)"), ALU.add).then_inc(lg_ready, 1)
                        dve.wait_ge(lg_ready, t * 2 + 2)
                        mask = vmask[:, bass.ds(n * TILES + u, 1), :].rearrange("p a j -> p (a j)") \
                            .unsqueeze(2).broadcast_to([P, J, 8])
                        for c in range(KC):
                            i = dve.tensor_tensor(lg[:, c], lg[:, c], mask, ALU.add)
                        then(i)
                        for c in range(KC):
                            i = dve.tensor_reduce(red[:, 0, 8 * c:8 * c + 8], lg[:, c].rearrange("p j h -> p h j"), AX_X, ALU.max)
                        then(i)
                        for c in range(KC):
                            i = dve.tensor_tensor(lg[:, c], lg[:, c],
                                                  red[:, 0, 8 * c:8 * c + 8].unsqueeze(1).broadcast_to([P, J, 8]), ALU.subtract)
                        i.then_inc(lg_shifted, 1)
                        dve.wait_ge(exp_ready, t + 1)
                        then(dve.tensor_reduce(red[:, 1, :], attn[:, :, :], AX_X, ALU.add))
                        then(dve.reciprocal(red[:, 2, :], red[:, 1, :]))
                        then(dve.tensor_tensor(red[:, 3, :], red[:, 2, :], gain[:, :], ALU.mult))
                        i = dve.tensor_tensor(attn[:, :, :], attn[:, :, :], red[:, 3, :].unsqueeze(2).broadcast_to([P, H, J]), ALU.mult)
                        i.then_inc(attn_ready, 1)
                        dve.wait_ge(part_cast, t * 2 + 1)
                        dve.tensor_tensor(rest[:, :, :], attn[:, :, 0:NEAR], parts[:, :, 0, :], ALU.subtract).then_inc(rest_ready, 1)
                        dve.wait_ge(part_cast, t * 2 + 2)
                        dve.tensor_tensor(parts[:, :, 2, :], rest[:, :, :], parts[:, :, 1, :], ALU.subtract).then_inc(parts_ready, 1)
                        for half in range(2):
                            dve.wait_ge(tp_ps, t * 2 + (half + 1))
                            dve.tensor_copy(parts_t[:, 8 * half:8 * half + 8, :], TP[0:PARTS * NEAR]).then_inc(tp_sb, 1)
                        dve.wait_ge(pv_ps, t + 1)
                        dve.tensor_copy(oT[:, :, u * P:(u + 1) * P],
                                        PS[:, 7, :].rearrange("p (g t) -> p g t", g=HG)).then_inc(o_sb, 1)
                        then(dve.engine_nop())
                    dve.wait_ge(y_ps, it * 2 + 2)
                    dve.tensor_tensor(xc[:, :, :], xc[:, :, :], PS[:, 0:KC, :], ALU.add).then_inc(x_updated, 1)
                    ln_dve(dve, it, 1)
                    dve.wait_ge(ffn_ps, it * 2 + 2)
                    for m in range(KC):
                        i = dve.scalar_tensor_tensor(out=xc[:, m, :], in0=PS[:, 2 + m, :], scalar=bcc[:, m:m + 1],
                                                     in1=xc[:, m, :], op0=ALU.add, op1=ALU.add)
                    i.then_inc(x_updated, 1)
                    ln_dve(dve, it, 2)
                    for u in range(4):
                        dve.wait_ge(qkb_ps, it * 4 + (u + 1))
                        dve.tensor_tensor(rope_a[:, :], PS[:, 2 * (u % 2), :], cosc[:, :], ALU.mult)
                        i = dve.tensor_tensor(rope_b[:, :], PS[:, 2 * (u % 2) + 1, :], sinc[:, :], ALU.mult)
                        i.then_inc(qkb_read, 1)
                        dve.wait_ge(qkb_read, it * 4 + (u + 1))
                        dve.tensor_tensor(rope_q[:, :], rope_a[:, :], rope_b[:, :], ALU.add).then_inc(dve_step, 1)
                        count[0] += 1
                        dve.wait_ge(dve_step, it * STEPS + count[0])
                        if u:
                            dve.wait_ge(qparts_stored, it * 64 + 16 * u)
                        dve.sem_inc(rope_rest, 1)
                        dve.wait_ge(rope_cast, it * 8 + (2 * u + 1))
                        dve.tensor_tensor(rope_r[:, :], rope_q[:, :], qparts[:, 0, :], ALU.subtract).then_inc(rope_rest, 1)
                        dve.wait_ge(rope_cast, it * 8 + (2 * u + 2))
                        dve.tensor_tensor(qparts[:, 2, :], rope_r[:, :], qparts[:, 1, :], ALU.subtract).then_inc(qparts_ready, 1)
                        then(dve.engine_nop())
                    assert count[0] == STEPS, count


def full_attention(nc, D):
    KT = T // P
    NGROUP = BATCH * HG
    ITERS = NGROUP * NCH
    MAXU = GRP * TILES * NCH
    UNITS = MAXU + 2
    PER_STEP = 5
    QK_LOADS = 16 * 6 * (1 + NCH)
    SUM_AT = 2
    with ExitStack() as ctx:
        sb = lambda n, s, d: ctx.enter_context(nc.sbuf_tensor(n, s, d))
        sem = lambda n: ctx.enter_context(nc.semaphore(n))
        ps_s = ctx.enter_context(nc.psum_tensor("ps_s", [P, 2, 2, CH], F32))
        ps_m = ctx.enter_context(nc.psum_tensor("ps_m", [P, 3, CH], F32))
        ps_o = ctx.enter_context(nc.psum_tensor("ps_o", [P, CH], F32))
        qs = sb("qs", [KROWS + PARTS, HG * NCH, GRP, CH], BF16)
        ks = sb("ks", [KROWS + PARTS, HG, GRP, T], BF16)
        vg = sb("vg", [P, KT, GRP, SLOT], F32)
        pr = sb("pr", [P, 2, GRP, CH], F32)
        mx = sb("mx", [P, GRP * TILES, NCH], F32)
        nm = sb("nm", [P, GRP * TILES], F32)
        nmr = sb("nmr", [P, GRP * TILES], F32)
        nmp = sb("nmp", [P, P // 16, GRP * TILES], BF16)
        nmt = sb("nmt", [PARTS * GRP * TILES, P], BF16)
        identb = sb("identb2", [P, P], BF16)
        sel = sb("sel", [P, P], F32)
        ou = sb("ou", [P, CH], F32)
        orc = sb("orc", [P, CH], F32)
        on = sb("on", [P, CH], F32)
        (const_ld, filled, qk_ld, va_ld, vb_ld, vc_ld, s_ps, p_ready, pv_done, m_ps, m_read, nm_step,
         nmp_ready, nmt_sb, neg_ld, o_ps, o_sb, orc_ready, on_ready, o_stored) = (sem("c_" + n) for n in (
             "const_ld", "filled", "qk_ld", "va_ld", "vb_ld", "vc_ld", "s_ps", "p_ready", "pv_done", "m_ps",
             "m_read", "nm_step", "nmp_ready", "nmt_sb", "neg_ld", "o_ps", "o_sb", "orc_ready", "on_ready",
             "o_stored"))
        block = ctx.enter_context(nc.Block())

        def units_of(step):
            return range(min(step * PER_STEP, MAXU), min((step + 1) * PER_STEP, MAXU))

        def unit_place(u):
            return u // (TILES * NCH), u // NCH % TILES, u % NCH

        @block.sync
        def _(sp):
            sp.dma_start(identb[:, :], D["identb"]).then_inc(const_ld, 16)
            sp.dma_start(sel[:, :], D["sel"]).then_inc(const_ld, 16)
            sp.wait_ge(filled, 4)

            def load_qk(G):
                b, g = G // HG, G % HG
                rows = slice(g * GRP * HD, (g + 1) * GRP * HD)
                for i in range(6):
                    r = slice(HD * i, HD * (i + 1))
                    sp.dma_start(ks[r, g, :, :],
                                 D["k_d"][b, K_STACK[i], rows, :].rearrange("(j d) t -> d j t", d=HD)).then_inc(qk_ld, 16)
                    for n in range(NCH):
                        sp.dma_start(qs[r, g * NCH + n, :, :],
                                     D["q_d"][b, Q_STACK[i], rows, n * CH:(n + 1) * CH].rearrange("(j d) t -> d j t", d=HD)
                                     ).then_inc(qk_ld, 16)
                sp.wait_ge(qk_ld, QK_LOADS * (G + 1))

            def load_v(G, first, last, loaded):
                b, g = G // HG, G % HG
                sp.dma_start(vg[:, first:last, :, :].rearrange("p k j d -> p k (j d)"),
                             D["vb_d"][b, first * P:last * P, g * GRP * SLOT:(g + 1) * GRP * SLOT]
                             .rearrange("(k p) n -> p k n", p=P)).then_inc(loaded, 16)

            for G in range(NGROUP):
                if G == 0:
                    load_qk(0)
                for first, last, loaded in ((0, 8, va_ld), (8, KT - 1, vb_ld), (KT - 1, KT, vc_ld)):
                    if G:
                        sp.wait_ge(pv_done, (G - 1) * NCH * KT + (NCH - 1) * KT + (last - 1) + 3)
                    load_v(G, first, last, loaded)
                if G == 0:
                    load_qk(1)
                    load_qk(2)
                if G + 3 < NGROUP:
                    load_qk(G + 3)
            sp.wait_ge(o_stored, 16 * (ITERS + 2))

        @block.gpsimd
        def _(pool):
            pool.memset(ks[KROWS:KROWS + PARTS, :, :, :], 1.0).then_inc(filled, 1)
            pool.wait_ge(filled, 1)
            pool.memset(ou[:, :], 1.0).then_inc(filled, 1)
            pool.memset(pr[:, 1, :, :], 1.0).then_inc(filled, 1)
            pool.memset(nmp[:, :, :], 0.0).then_inc(filled, 1)
            def rows(x, nq):
                pool.wait_ge(nmt_sb, x + 1)
                for part in range(PARTS):
                    pool.dma_start(qs[KROWS + part:KROWS + part + 1, bass.ds(nq, 1), :, :]
                                   .rearrange("a n j t -> a (n j t)"),
                                   nmt[16 * part:16 * part + 16, :]).then_inc(neg_ld, 16)

            def outs(x):
                pool.wait_ge(on_ready, x + 1)
                pool.dma_start(D["o_d"][x], on[:, :]).then_inc(o_stored, 16)

            outs(0)
            rows(0, 0)
            with pool.Fori(1, ITERS) as x:
                outs(x)
                nq = pool.snap(x % (HG * NCH))
                rows(x, nq)
            outs(ITERS)
            outs(ITERS + 1)

        @block.tensor
        def _(pe):
            pe.wait_ge(const_ld, 32)
            pe.wait_ge(filled, 4)
            pe.sem_inc(pv_done, 1)

            def bank_free(x, u):
                pe.wait_ge(m_read, x * UNITS + (u + 1))

            def max_unit(x, u, pos, nq, nslot):
                j, qt, kc = unit_place(u)
                bank_free(x, pos)
                pe.matmul(ps_m[:, pos % 3, :], qs[0:KROWS, bass.ds(nq, 1), j, qt * P:(qt + 1) * P].rearrange("p a t -> p (a t)"),
                          ks[0:KROWS, bass.ds(nslot, 1), j, kc * CH:(kc + 1) * CH].rearrange("p a t -> p (a t)"),
                          start=True, stop=True).then_inc(m_ps, 1)

            def sums(x, pos):
                bank_free(x, pos)
                pe.wait_ge(o_sb, x + 1)
                pe.matmul(ps_m[:, pos % 3, :], sel[:, :], ou[:, :], start=True, stop=True).then_inc(m_ps, 1)

            def max_rows(x):
                bank_free(x, UNITS - 1)
                pe.wait_ge(nmp_ready, x + 1)
                pe.transpose(ps_m[:, (UNITS - 1) % 3, 0:P // 2].bitcast(BF16),
                             nmp[:, :, :].rearrange("p s n -> p (s n)"), identb[:, :]).then_inc(m_ps, 1)

            def weigh(kt, ready):
                pe.wait_ge(p_ready, ready)
                for j in range(GRP):
                    mm = pe.matmul(ps_o[SLOT * j:SLOT * (j + 1), :], vg[:, kt, j, :], pr[:, kt % 2, j, :],
                                   start=(kt == 0), stop=(kt == KT - 1), skip_group_check=True)
                mm.then_inc(pv_done, 1)
                return mm

            def iteration(x, cur_q, slot, nq, nslot, G):
                pos = 0
                pe.wait_ge(neg_ld, x * (16 * PARTS))
                if nq is not None:
                    pe.wait_ge(qk_ld, G[1] * QK_LOADS + QK_LOADS)
                for kk in range(KT):
                    for pair in range(2):
                        pe.wait_ge(p_ready, x * (2 * KT) + (2 * kk + pair + 1 - 2 * KT))
                        for jj in range(2):
                            j = 2 * pair + jj
                            mm = pe.matmul(ps_s[:, pair, jj, :],
                                           ks[:, bass.ds(slot, 1), j, kk * P:(kk + 1) * P].rearrange("p a t -> p (a t)"),
                                           qs[:, bass.ds(cur_q, 1), j, :].rearrange("p a t -> p (a t)"),
                                           start=True, stop=True)
                        mm.then_inc(s_ps, 1)
                    if kk == 1:
                        pe.wait_ge(va_ld, G[0] * 16 + 16)
                        pe.wait_ge(o_sb, x + 1)
                    if kk == 9:
                        pe.wait_ge(vb_ld, G[0] * 16 + 16)
                    if kk == KT - 1:
                        pe.wait_ge(vc_ld, G[0] * 16 + 16)
                    weigh((kk - 1) % KT, x * (2 * KT) + (2 * kk + 2 - 2 * KT))
                    if nq is not None:
                        for u in units_of(kk):
                            max_unit(x, u, pos, nq, nslot)
                            pos += 1
                    if kk == SUM_AT:
                        sums(x, pos)
                        pos += 1
                if nq is not None:
                    max_rows(x)

            pe.wait_ge(qk_ld, QK_LOADS)
            pos = 0
            for kk in range(KT):
                for u in units_of(kk):
                    max_unit(0, u, pos, 0, 0)
                    pos += 1
                if kk == SUM_AT:
                    sums(0, pos)
                    pos += 1
            max_rows(0)
            pe.wait_ge(vc_ld, 16)
            for j in range(GRP):
                pe.matmul(ps_o[SLOT * j:SLOT * (j + 1), :], vg[:, KT - 1, j, :], pr[:, 1, j, :],
                          start=True, stop=False, skip_group_check=True)
            with pe.Fori(1, ITERS) as x:
                G = pe.snap((x - 1) // NCH)
                NGp = pe.snap(x // NCH)
                iteration(x, pe.snap((x - 1) % (HG * NCH)), pe.snap(G % HG), pe.snap(x % (HG * NCH)),
                          pe.snap(NGp % HG), (G, NGp))
            iteration(ITERS, HG * NCH - 1, HG - 1, None, None, (NGROUP - 1, None))
            weigh(KT - 1, 2 * KT * ITERS + 2)
            sums(ITERS + 1, 1 - UNITS)

        @block.scalar
        def _(act):
            act.wait_ge(filled, 4)
            act.sem_inc(p_ready, 2)
            with act.Fori(0, ITERS) as i:
                for kk in range(KT):
                    act.wait_ge(pv_done, i * KT + (kk + 1))
                    for pair in range(2):
                        act.wait_ge(s_ps, i * (2 * KT) + (2 * kk + pair + 1))
                        act.activation(pr[:, kk % 2, 2 * pair:2 * pair + 2, :], ps_s[:, pair, :, :], ACT.Exp,
                                       scale=HD ** -0.5).then_inc(p_ready, 1)

        @block.vector
        def _(dve):
            dve.wait_ge(filled, 4)
            dve.sem_inc(m_read, 3)
            dve.sem_inc(o_sb, 1)

            def max_unit(x, u, pos):
                dve.wait_ge(m_ps, x * UNITS + (pos + 1))
                j, qt, kc = unit_place(u)
                return dve.tensor_reduce(mx[:, j * TILES + qt, kc:kc + 1], ps_m[:, pos % 3, :], AX_X, ALU.max).then_inc(m_read, 1)

            def sums(x, pos):
                dve.wait_ge(m_ps, x * UNITS + (pos + 1))
                dve.reciprocal(orc[:, :], ps_m[:, pos % 3, :]).then_inc(m_read, 1)
                dve.wait_ge(m_read, x * UNITS + (pos + 4))
                if isinstance(x, int) and x == 0:
                    pass
                else:
                    dve.wait_ge(o_stored, x * 16)
                dve.tensor_tensor(on[:, :], ou[:, :], orc[:, :], ALU.mult).then_inc(on_ready, 1)

            def max_rows(x):
                dve.wait_ge(m_read, x * UNITS + (UNITS - 1 + 3))
                NS = 5
                dve.tensor_reduce(nm[:, :], mx[:, :, :], AX_X, ALU.max, negate=True).then_inc(nm_step, 1)
                dve.wait_ge(nm_step, x * NS + 1)
                dve.tensor_copy(nmp[:, 0, :], nm[:, :]).then_inc(nm_step, 1)
                dve.wait_ge(nm_step, x * NS + 2)
                dve.tensor_tensor(nmr[:, :], nm[:, :], nmp[:, 0, :], ALU.subtract).then_inc(nm_step, 1)
                dve.wait_ge(nm_step, x * NS + 3)
                dve.tensor_copy(nmp[:, 1, :], nmr[:, :]).then_inc(nm_step, 1)
                dve.wait_ge(nm_step, x * NS + 4)
                dve.tensor_tensor(nmp[:, 2, :], nmr[:, :], nmp[:, 1, :], ALU.subtract).then_inc(nm_step, 1)
                dve.wait_ge(nm_step, x * NS + 5)
                dve.sem_inc(nmp_ready, 1)
                dve.wait_ge(m_ps, x * UNITS + UNITS)
                if not (isinstance(x, int) and x == 0):
                    dve.wait_ge(neg_ld, x * (16 * PARTS))
                dve.tensor_copy(nmt[:, :], ps_m[0:PARTS * 16, (UNITS - 1) % 3, 0:P // 2].bitcast(BF16)).then_inc(m_read, 1)
                dve.wait_ge(m_read, x * UNITS + (UNITS + 3))
                dve.sem_inc(nmt_sb, 1)

            def take_output(x):
                dve.wait_ge(pv_done, x * KT + (2 - KT))
                if not (isinstance(x, int) and x == 0):
                    dve.wait_ge(on_ready, x)
                dve.tensor_copy(ou[:, :], ps_o[:, :]).then_inc(o_sb, 1)

            def iteration(x, maxima):
                pos = 0
                for kk in range(KT):
                    if maxima:
                        for u in units_of(kk):
                            max_unit(x, u, pos)
                            pos += 1
                    if kk == 0 and not (isinstance(x, int) and x == 0):
                        take_output(x)
                    if kk == SUM_AT:
                        sums(x, pos)
                        pos += 1
                if maxima:
                    max_rows(x)

            iteration(0, True)
            with dve.Fori(1, ITERS) as x:
                iteration(x, True)
            iteration(ITERS, False)
            take_output(ITERS + 1)
            sums(ITERS + 1, 1 - UNITS)


def final_stage(nc, I, D, out):
    with ExitStack() as ctx:
        sb = lambda n, s, d: ctx.enter_context(nc.sbuf_tensor(n, s, d))
        sem = lambda n: ctx.enter_context(nc.semaphore("f_" + n))
        PS = ctx.enter_context(nc.psum_tensor("PSf", [P, 8, CH], F32))
        ones = sb("f_ones", [P, P], F32)
        eps = sb("f_eps", [P, 1], F32)
        wo = sb("f_wo", [P, HG, C], F32)
        xc = sb("f_xc", [P, KC, CH], F32)
        oT = sb("f_oT", [P, HG, CH], F32)
        mtc = sb("f_mtc", [P, KC, C], F32)
        bcc = sb("f_bcc", [P, KC], F32)
        filled, const_ld, chunk_ld, y_ps, ffn_ps, x_updated, stored = (
            sem(n) for n in ("filled", "const_ld", "chunk_ld", "y_ps", "ffn_ps", "x_updated", "stored"))
        fsb = lambda n, s, d: sb("f_" + n, s, d)
        xn, ln_pe, ln_act, ln_dve = layer_norm(nc, ctx, fsb, sem, PS, 4, 5, ones, eps, xc, 1)
        block = ctx.enter_context(nc.Block())
        LOADS = 16 * (HG + 3)

        @block.sync
        def _(sp):
            sp.wait_ge(filled, 2)
            for j in range(GRP):
                for g in range(HG):
                    sp.dma_start(wo[SLOT * j:SLOT * j + HD, g, :],
                                 I["wo_b"][HD * (GRP * g + j):HD * (GRP * g + j + 1), :]).then_inc(const_ld, 16)
            with sp.Fori(0, BATCH) as b:
                with sp.Fori(0, NCH) as n:
                    it = b * NCH + n
                    sp.wait_ge(stored, it * 16 + 16)
                    cols = bass.ds(it * CH, CH)
                    for g in range(HG):
                        sp.dma_start(oT[:, g, :], D["o_d"][b * (HG * NCH) + n + (2 + g * NCH)]).then_inc(chunk_ld, 16)
                    sp.dma_start(xc[:, :, :], D["x_d"][:, cols].rearrange("(k p) t -> p k t", p=P)).then_inc(chunk_ld, 16)
                    sp.dma_start(mtc[:, :, :], D["mt_d"][it].rearrange("(k p) n -> p k n", p=P)).then_inc(chunk_ld, 16)
                    sp.dma_start(bcc[:, :], D["bc_d"][it].rearrange("(k p) -> p k", p=P),
                                 allow_slow_non_contiguous=True).then_inc(chunk_ld, 16)
                    sp.wait_ge(x_updated, it * 2 + 2)
                    sp.dma_start(out[:, cols].rearrange("(k p) t -> p k t", p=P), xc[:, :, :]).then_inc(stored, 16)
            sp.wait_ge(stored, 16 * NG + 16)

        @block.gpsimd
        def _(pool):
            pool.memset(wo[:, :, :], 0.0).then_inc(filled, 1)
            pool.memset(eps[:, :], EPS).then_inc(filled, 1)
            pool.memset(ones[:, :], 1.0 / C).then_inc(filled, 1)
            pool.sem_inc(stored, 16)

        @block.tensor
        def _(pe):
            pe.wait_ge(filled, 3)
            pe.wait_ge(const_ld, 16 * GRP * HG)
            with pe.Fori(0, NG) as it:
                pe.wait_ge(chunk_ld, it * LOADS + LOADS)
                for m in range(KC):
                    for g in range(HG):
                        mm = pe.matmul(PS[:, m, :], wo[:, g, m * P:(m + 1) * P], oT[:, g, :],
                                       start=(g == 0), stop=(g == HG - 1))
                    mm.then_inc(y_ps, 1)
                pe.wait_ge(x_updated, it * 2 + 1)
                ln_pe(pe, it, 0)
                for m in range(KC):
                    for k in range(KC):
                        mm = pe.matmul(PS[:, 2 + m, :], mtc[:, k, m * P:(m + 1) * P], xn[:, k, :],
                                       start=(k == 0), stop=(k == KC - 1))
                    mm.then_inc(ffn_ps, 1)

        @block.scalar
        def _(act):
            act.wait_ge(filled, 3)
            with act.Fori(0, NG) as it:
                ln_act(act, it, 0)

        @block.vector
        def _(dve):
            with dve.Fori(0, NG) as it:
                dve.wait_ge(chunk_ld, it * LOADS + LOADS)
                dve.wait_ge(y_ps, it * 2 + 2)
                dve.tensor_tensor(xc[:, :, :], xc[:, :, :], PS[:, 0:KC, :], ALU.add).then_inc(x_updated, 1)
                dve.wait_ge(x_updated, it * 2 + 1)
                ln_dve(dve, it, 0)
                dve.wait_ge(ffn_ps, it * 2 + 2)
                for m in range(KC):
                    i = dve.scalar_tensor_tensor(out=xc[:, m, :], in0=PS[:, 2 + m, :], scalar=bcc[:, m:m + 1],
                                                 in1=xc[:, m, :], op0=ALU.add, op1=ALU.add)
                i.then_inc(x_updated, 1)


def build(nc, I, out):
    dram = lambda n, s, d: nc.dram_tensor(n, s, d, kind="Internal").ap()
    D = {
        "mt_d": dram("mt_d", (NG, C, C), F32),
        "bc_d": dram("bc_d", (NG, C), F32),
        "v_d": dram("v_d", (BATCH, PAD + T, H * SLOT), F32),
        "vb_d": dram("vb_d", (BATCH, T, H * SLOT), F32),
        "x_d": dram("x_d", (C, BATCH * T), F32),
        "q_d": dram("q_d", (BATCH, PARTS, C, T), BF16),
        "k_d": dram("k_d", (BATCH, PARTS, C, T), BF16),
        "o_d": dram("o_d", (2 + BATCH * HG * NCH, P, CH), F32),
        "identb": I["identb"],
        "sel": I["sel"],
    }
    fold_ffn(nc, I["W1"], I["W2T"], I["b1"], I["b2"], D["mt_d"], D["bc_d"])
    local_stage(nc, I, D)
    full_attention(nc, D)
    final_stage(nc, I, D, out)


def constants():
    bf = mybir.dt.np(BF16)
    f = np.float32
    inv = (f(1.0) / f(10000.0) ** (np.arange(0, HD, 2, dtype=f) / f(HD))).astype(f)
    ang = np.outer(np.arange(T, dtype=f), inv).astype(f)
    d = np.arange(P) % HD
    sign = np.where(d < HD // 2, -1.0, 1.0).astype(f)[:, None]
    cosT = np.cos(ang).astype(f).T[d % (HD // 2)]
    sinT = np.sin(ang).astype(f).T[d % (HD // 2)] * sign
    t = np.arange(T).reshape(T // P, P)
    vmask = np.where(t.T[:, :, None] >= np.array(OFFSETS)[None, None, :], f(0), np.finfo(f).min).astype(f)
    j = np.tile(np.arange(NEAR), PARTS)
    band = (np.arange(EBW)[None, :] == (2 * P - 1 - j)[:, None]).astype(bf)
    p = np.arange(P)
    return {
        "cosT": np.ascontiguousarray(cosT), "sinT": np.ascontiguousarray(sinT.astype(f)), "vmask": vmask,
        "band": band, "ident": np.eye(P, dtype=f), "identb": np.eye(P).astype(bf),
        "hmask": (p[:, None] // HD == np.arange(8)[None, :]).astype(f),
        "sel": (p[:, None] == (p[None, :] // SLOT * SLOT + HD)).astype(f),
    }


def kernel(**inputs):
    import concourse.bacc as bacc
    from concourse.bass_utils import run_bass_kernel_spmd

    a = {k[3:]: np.asarray(v) for k, v in inputs.items()}
    tokens = BATCH * T
    wqkv_b = a["attn_b_Wqkv"]
    turned = (np.arange(2 * C) // HD) * HD + (np.arange(2 * C) + HD // 2) % HD
    arrays = {
        "xT": a["attn_a_x"].reshape(tokens, C).T,
        "wqkv": a["attn_a_w_qkv"], "wo": a["attn_a_w_out"], "pos_bias": a["attn_a_pos_bias"],
        "se_t": a["attn_a_scale_embed"].T, "gain": a["attn_a_if_gain"],
        "wqkv_b": wqkv_b, "wrot": wqkv_b[:, turned], "wo_b": a["attn_b_Wo"],
        "W1": a["ffn_W1"], "W2T": a["ffn_W2"].transpose(0, 2, 1), "b1": a["ffn_b1"].reshape(NG, INTER // P, P).transpose(0, 2, 1), "b2": a["ffn_b2"],
        **constants(),
    }
    arrays = {n: np.ascontiguousarray(v) for n, v in arrays.items()}
    nc = bacc.Bacc("TRN2", target_bir_lowering=False, num_devices=1)
    I = {n: nc.dram_tensor("in_" + n, v.shape, mybir.dt.from_np(v.dtype), kind="ExternalInput").ap()
         for n, v in arrays.items()}
    out = nc.dram_tensor("out_T", (C, tokens), F32, kind="ExternalOutput").ap()
    build(nc, I, out)
    r = run_bass_kernel_spmd(nc, [{"in_" + n: v for n, v in arrays.items()}], core_ids=[0])
    return r.results[0]["out_T"].T.reshape(BATCH, T, C)
```

```python
from contextlib import ExitStack

import numpy as np
import concourse.bass as bass
from concourse import mybir

F32 = mybir.dt.float32
BF16 = mybir.dt.bfloat16
ALU = mybir.AluOpType
ACT = mybir.ActivationFunctionType
AX_X = mybir.AxisListType.X

P = 128
BATCH, T, C = 2, 2048, 256
H, HD = 16, 16
KC = C // P
CH = 512
NCH = T // CH
TILES = CH // P
OFFSETS = list(range(41)) + [128, 96, 384]
J = len(OFFSETS)
NEAR = 41
PAD = 384
GRP, HG = 4, H // 4
SLOT = 32
INTER = 1024
NG = 8
EPS = 1e-5
PARTS = 3
BANK_J = 16
BANKS = [min(BANK_J, J - BANK_J * k) for k in range((J + BANK_J - 1) // BANK_J)]
EBW = 3 * P - 1
Q_STACK = [0, 0, 0, 1, 1, 2]
K_STACK = [0, 1, 2, 0, 1, 0]
KROWS = 6 * HD


PRODUCTS = [(c, bank, r, g) for c in range(KC) for bank in range(len(BANKS)) for r in range(4)
            for g in range(BANKS[bank] // 4)]
ON_POOL = [(k * 29) % 88 < 29 for k in range(len(PRODUCTS))]
N_DVE, N_POOL = ON_POOL.count(False), ON_POOL.count(True)
RING = 4
SUMMED = []
for _unit in range(KC * len(BANKS)):
    _n = sum(1 for c, bank, _, _ in PRODUCTS if c * len(BANKS) + bank <= _unit)
    SUMMED.append((ON_POOL[:_n].count(False), ON_POOL[:_n].count(True)))


def fold_ffn(nc, W1, W2T, b1, b2, mt_d, bc_d):
    OC = INTER // P
    with ExitStack() as ctx:
        sb = lambda n, s, d: ctx.enter_context(nc.sbuf_tensor(n, s, d))
        sem = lambda n: ctx.enter_context(nc.semaphore(n))
        w1 = sb("w1", [P, 2, OC, C], F32)
        w2 = sb("w2", [P, 2, OC, C], F32)
        b1s = sb("b1s", [P, 2, OC], F32)
        b2s = sb("b2s", [1, 2, C], F32)
        mt = sb("mt", [P, 2, KC, C], F32)
        bc = sb("bc", [1, 2, C], F32)
        ps = ctx.enter_context(nc.psum_tensor("fold_ps", [P, 2, 4, CH], F32))
        loaded = [sem("fold_loaded0"), sem("fold_loaded1")]
        mm_done, evac, stored = sem("fold_mm"), sem("fold_evac"), sem("fold_stored")
        start = sem("fold_start")
        block = ctx.enter_context(nc.Block())

        @block.sync
        def _(sp):
            with sp.Fori(0, NG // 2) as i:
                for s in range(2):
                    g = i * 2 + s
                    sp.wait_ge(evac, i * 2 + s + 1)
                    sp.dma_start(w1[:, s], W1[g].rearrange("(k p) n -> p k n", p=P)).then_inc(loaded[s], 16)
                    sp.dma_start(w2[:, s], W2T[g].rearrange("(k p) n -> p k n", p=P)).then_inc(loaded[s], 16)
                    sp.dma_start(b1s[:, s], b1[g]).then_inc(loaded[s], 16)
                    sp.dma_start(b2s[:, s], b2[g].unsqueeze(0)).then_inc(loaded[s], 16)

        @block.tensor
        def _(pe):
            pe.wait_ge(start, 1)
            pe.sem_inc(mm_done, 2)
            with pe.Fori(0, NG // 2) as i:
                for s in range(2):
                    pe.wait_ge(loaded[s], i * 64 + 64)
                    pe.wait_ge(evac, i * 2 + s + 1)
                    for m in range(KC):
                        for k in range(OC):
                            pe.matmul(ps[:, s, m, 0:C], w1[:, s, k, m * P:(m + 1) * P], w2[:, s, k, :],
                                      start=(k == 0), stop=(k == OC - 1))
                    for k in range(OC):
                        last = pe.matmul(ps[0:1, s, 2, 0:C], b1s[:, s, k:k + 1], w2[:, s, k, :],
                                         start=(k == 0), stop=(k == OC - 1))
                    last.then_inc(mm_done, 1)

        @block.vector
        def _(dve):
            dve.sem_inc(start, 1)
            dve.sem_inc(evac, 2)
            dve.sem_inc(stored, 64)
            with dve.Fori(0, NG // 2) as i:
                for s in range(2):
                    dve.wait_ge(mm_done, i * 2 + s + 3)
                    dve.wait_ge(stored, i * 64 + 64)
                    dve.tensor_copy(mt[:, s], ps[:, s, 0:KC, 0:C])
                    dve.tensor_tensor(bc[:, s], ps[0:1, s, 2, 0:C], b2s[:, s], ALU.add).then_inc(evac, 1)

        @block.scalar
        def _(act):
            with act.Fori(0, NG // 2) as i:
                for s in range(2):
                    g = i * 2 + s
                    act.wait_ge(evac, i * 2 + s + 3)
                    act.dma_start(mt_d[g].rearrange("(k p) n -> p k n", p=P), mt[:, s]).then_inc(stored, 16)
                    act.dma_start(bc_d[g].unsqueeze(0), bc[:, s]).then_inc(stored, 16)
            act.wait_ge(stored, 64 + 32 * NG)


def layer_norm(nc, ctx, sb, sem, PS, mean_bank, var_bank, ones, spread, eps, xc, per_chunk):
    xm = sb("xm", [P, KC, CH], F32)
    sq = sb("sq", [P, KC, CH], F32)
    sd = sb("sd", [P, P], F32)
    rs = sb("rs", [P, P], F32)
    xn = sb("xn", [P, KC, CH], F32)
    mean_ps, centered, squared, var_ps, sd_ready, rs_ready, rs_ps, xn_ready = (
        sem(n) for n in ("mean_ps", "centered", "squared", "var_ps", "sd_ready", "rs_ready", "rs_ps", "xn_ready"))
    wide = lambda v: v.unsqueeze(1).broadcast_to([P, KC, CH])

    def on_pe(pe, it, l):
        n = it * per_chunk + (l + 1)
        for k in range(KC):
            mm = pe.matmul(PS[:, mean_bank, :], ones[:, :], xc[:, k, :], start=(k == 0), stop=(k == KC - 1))
        mm.then_inc(mean_ps, 1)
        pe.wait_ge(squared, n)
        for k in range(KC):
            for q in range(TILES):
                mm = pe.matmul(PS[SLOT * q:SLOT * (q + 1), var_bank, 0:P], ones[:, 0:SLOT],
                               sq[:, k, q * P:(q + 1) * P], start=(k == 0), stop=(k == KC - 1))
        mm.then_inc(var_ps, 1)
        pe.wait_ge(rs_ready, n)
        for q in range(TILES):
            mm = pe.matmul(PS[:, mean_bank, q * P:(q + 1) * P], spread[:, q, :], rs[:, :], start=True, stop=True)
        mm.then_inc(rs_ps, 1)

    def on_act(act, it, l):
        n = it * per_chunk + (l + 1)
        act.wait_ge(centered, n)
        act.activation(sq[:, :, :], xm[:, :, :], ACT.Square).then_inc(squared, 1)
        act.wait_ge(var_ps, n)
        act.activation(sd[:, :], PS[:, var_bank, 0:P], ACT.Sqrt, bias=eps[:, 0:1]).then_inc(sd_ready, 1)

    def on_dve(dve, it, l):
        n = it * per_chunk + (l + 1)
        dve.wait_ge(mean_ps, n)
        dve.tensor_tensor(xm[:, :, :], xc[:, :, :], wide(PS[:, mean_bank, :]), ALU.subtract).then_inc(centered, 1)
        dve.wait_ge(sd_ready, n)
        dve.reciprocal(rs[:, :], sd[:, :]).then_inc(rs_ready, 1)
        dve.wait_ge(rs_ps, n)
        dve.tensor_tensor(xn[:, :, :], xm[:, :, :], wide(PS[:, mean_bank, :]), ALU.mult).then_inc(xn_ready, 1)

    def xn_on_pe(pe, it, l):
        pe.wait_ge(xn_ready, it * per_chunk + (l + 1))

    return xn, on_pe, on_act, on_dve, xn_on_pe


def local_stage(nc, I, D):
    with ExitStack() as ctx:
        sb = lambda n, s, d: ctx.enter_context(nc.sbuf_tensor(n, s, d))
        sem = lambda n: ctx.enter_context(nc.semaphore(n))
        PS = ctx.enter_context(nc.psum_tensor("PSa", [P, 8, CH], F32))
        TP = PS[:, 3, :].bitcast(BF16).rearrange("p (h t) -> p h t", h=8)

        ones = sb("ones", [P, P], F32)
        spread = sb("spread", [P, TILES, P], F32)
        eps = sb("eps", [P, 1], F32)
        ident = sb("ident", [P, P], F32)
        identb = sb("identb", [P, P], BF16)
        band = sb("band", [PARTS * NEAR, EBW], BF16)
        wqkv = sb("wqkv", [P, KC, 3 * C], F32)
        wo = sb("wo", [P, HG, C], F32)
        wqkv_b = sb("wqkv_b", [P, KC, 3 * C], F32)
        wrot = sb("wrot", [P, KC, 2 * C], F32)
        hmask = sb("hmask", [P, 8], F32)
        se_t = sb("se_t", [P, J], F32)
        se_w = sb("se_w", [P, J], F32)
        sj = sb("sj", [P, J, SLOT], F32)
        pbias = sb("pbias", [P, KC, J, 8], F32)
        vmask = sb("vmask", [P, T // P, J], F32)
        gain = sb("gain", [P, H], F32)
        xc = sb("xc", [P, KC, CH], F32)
        cosc = sb("cosc", [P, CH], F32)
        sinc = sb("sinc", [P, CH], F32)
        mtc = sb("mtc", [P, KC, C], F32)
        bcc = sb("bcc", [P, KC], F32)
        qT = sb("qT", [P, KC, CH], F32)
        kT = sb("kT", [P, KC, PAD + T], F32)
        prod_d = sb("prod_d", [P, RING, CH], F32)
        prod_p = sb("prod_p", [P, RING, CH], F32)
        sc = sb("sc", [P, 2 * len(BANKS), CH], F32)
        lg = sb("lg", [P, KC, J, 8], F32)
        red = sb("red", [P, 4, H], F32)
        attn = sb("attn", [P, H, J], F32)
        rest = sb("rest", [P, H, NEAR], F32)
        parts = sb("parts", [P, H, PARTS, NEAR], BF16)
        parts_t = sb("parts_t", [PARTS * NEAR, H, P], BF16)
        a0 = sb("a0", [P, H, P], F32)
        a1 = sb("a1", [P, H, NEAR - 1], F32)
        vnew = sb("vnew", [P, TILES, H, SLOT], F32)
        v7 = sb("v7", [P, TILES + 3, H, SLOT], F32)
        v96 = sb("v96", [P, TILES, H, SLOT], F32)
        far = sb("far", [P, H, SLOT], F32)
        fart = sb("fart", [P, H, HD], F32)
        oT = sb("oT", [P, HG, CH], F32)
        rope_a = sb("rope_a", [P, CH], F32)
        rope_b = sb("rope_b", [P, CH], F32)
        rope_q = sb("rope_q", [P, CH], F32)
        rope_r = sb("rope_r", [P, CH], F32)
        qparts = sb("qparts", [P, PARTS, CH], BF16)
        vb = sb("vb", [P, TILES, H, SLOT], F32)

        const_ld, filled, made = sem("const_ld"), sem("filled"), sem("made")
        stored = sem("stored")
        chunk_ld, v_stored, v_ld = sem("chunk_ld"), sem("v_stored"), sem("v_ld")
        qk_ps, qk_sb, v_ps, v_sb = sem("qk_ps"), sem("qk_sb"), sem("v_ps"), sem("v_sb")
        prod_d_ready, prod_d_used = sem("prod_d_ready"), sem("prod_d_used")
        prod_p_ready, prod_p_used = sem("prod_p_ready"), sem("prod_p_used")
        sc_sb, l_ps, lg_ready = sem("sc_sb"), sem("l_ps"), sem("lg_ready")
        lg_shifted, exp_ready, attn_ready = sem("lg_shifted"), sem("exp_ready"), sem("attn_ready")
        part_cast, rest_ready, parts_ready = sem("part_cast"), sem("rest_ready"), sem("parts_ready")
        tp_ps, tp_sb, sp_ps, a_sb = sem("tp_ps"), sem("tp_sb"), sem("sp_ps"), sem("a_sb")
        far_step, far_ready, pv_ps, o_sb = sem("far_step"), sem("far_ready"), sem("pv_ps"), sem("o_sb")
        y_ps, ffn_ps, x_updated, dve_step = sem("y_ps"), sem("ffn_ps"), sem("x_updated"), sem("dve_step")
        qkb_ps, qkb_read, rope_cast, rope_rest, qparts_ready = (
            sem("qkb_ps"), sem("qkb_read"), sem("rope_cast"), sem("rope_rest"), sem("qparts_ready"))
        qparts_stored, vb_ps, vb_sb = sem("qparts_stored"), sem("vb_ps"), sem("vb_sb")

        xn, ln_pe, ln_act, ln_dve, xn_pe = layer_norm(nc, ctx, sb, sem, PS, 4, 5, ones, spread, eps, xc, 3)
        block = ctx.enter_context(nc.Block())
        PAD_STORES = 2
        STORES = 2
        N_CONST = 12 + 8 + GRP * HG
        QKD = [D["q_d"], D["k_d"]]

        def chunk_start(eng, it):
            eng.wait_ge(stored, it * (16 * STORES) + 16 * PAD_STORES)

        def chunks(eng):
            return eng.Fori(0, BATCH), eng.Fori(0, NCH)

        @block.sync
        def _(sp):
            def const(dst, src):
                sp.dma_start(dst, src).then_inc(const_ld, 16)
            const(ident[:, :], I["ident"])
            const(spread[:, :, :], I["spread"])
            const(identb[:, :], I["identb"])
            const(band[:, :], I["band"])
            const(wqkv[:, :, :], I["wqkv"].rearrange("(k p) n -> p k n", p=P))
            const(wqkv_b[:, :, :], I["wqkv_b"].rearrange("(k p) n -> p k n", p=P))
            const(wrot[:, :, :], I["wrot"].rearrange("(k p) n -> p k n", p=P))
            const(hmask[:, :], I["hmask"])
            const(vmask[:, :, :], I["vmask"])
            const(gain[:, :], I["gain"].partition_broadcast(P))
            for c in range(KC):
                const(pbias[:, c], I["pos_bias"][:, 8 * c:8 * c + 8].partition_broadcast(P))
            sp.wait_ge(filled, 1)
            for h in range(8):
                const(se_t[HD * h:HD * (h + 1), :], I["se_t"])
            for j in range(GRP):
                for g in range(HG):
                    const(wo[SLOT * j:SLOT * j + HD, g, :],
                          I["wo"][HD * (GRP * g + j):HD * (GRP * g + j + 1), :])
            sp.wait_ge(filled, 2)
            for b in range(BATCH):
                sp.dma_start(D["v_d"][b, 0:PAD, :].rearrange("(k p) n -> p k n", p=P),
                             vnew[:, 0:3].rearrange("p k h d -> p k (h d)")).then_inc(stored, 16)
            fb, fn = chunks(sp)
            with fb as b:
                with sp.Fori(0, NCH) as n:
                    it = b * NCH + n
                    chunk_start(sp, it)
                    cols = bass.ds(it * CH, CH)
                    sp.dma_start(xc[:, :, :], I["xT"][:, cols].rearrange("(k p) t -> p k t", p=P)).then_inc(chunk_ld, 16)
                    sp.dma_start(cosc[:, :], I["cosT"][:, bass.ds(n * CH, CH)]).then_inc(chunk_ld, 16)
                    sp.dma_start(sinc[:, :], I["sinT"][:, bass.ds(n * CH, CH)]).then_inc(chunk_ld, 16)
                    sp.dma_start(mtc[:, :, :], D["mt_d"][it].rearrange("(k p) n -> p k n", p=P)).then_inc(chunk_ld, 16)
                    sp.dma_start(bcc[:, :], D["bc_d"][it].rearrange("(k p) -> p k", p=P),
                                 allow_slow_non_contiguous=True).then_inc(chunk_ld, 16)
                    sp.wait_ge(v_sb, it * 2 + 2)
                    sp.dma_start(D["v_d"][b, bass.ds(n * CH + PAD, CH), :].rearrange("(k p) n -> p k n", p=P),
                                 vnew[:, :, :, :].rearrange("p k h d -> p k (h d)")).then_inc(v_stored, 16)
                    sp.wait_ge(v_stored, it * 16 + 16)
                    sp.dma_start(v7[:, :, :, :].rearrange("p k h d -> p k (h d)"),
                                 D["v_d"][b, bass.ds(n * CH, CH + PAD), :].rearrange("(k p) n -> p k n", p=P)).then_inc(v_ld, 16)
                    sp.dma_start(v96[:, :, :, :].rearrange("p k h d -> p k (h d)"),
                                 D["v_d"][b, bass.ds(n * CH + PAD - 96, CH), :].rearrange("(k p) n -> p k n", p=P)).then_inc(v_ld, 16)
                    sp.wait_ge(x_updated, it * 2 + 2)
                    sp.dma_start(D["x_d"][:, cols].rearrange("(k p) t -> p k t", p=P), xc[:, :, :]).then_inc(stored, 16)
                    for u in range(4):
                        sp.wait_ge(qparts_ready, it * 4 + u + 1)
                        dst = QKD[u // 2][b, :, (u % 2) * P:(u % 2 + 1) * P, bass.ds(n * CH, CH)]
                        sp.dma_start(dst.rearrange("s p t -> p s t"), qparts[:, :, :]).then_inc(qparts_stored, 16)
                    sp.wait_ge(vb_sb, it * 2 + 2)
                    sp.wait_ge(qparts_stored, it * 64 + 64)
                    sp.dma_start(D["vb_d"][b, bass.ds(n * CH, CH), :].rearrange("(k p) n -> p k n", p=P),
                                 vb[:, :, :, :].rearrange("p k h d -> p k (h d)")).then_inc(stored, 16)
            sp.wait_ge(stored, 16 * PAD_STORES + 16 * STORES * NG)

        @block.gpsimd
        def _(pool):
            pool.memset(wo[:, :, :], 0.0)
            pool.memset(ones[:, :], 1.0 / C).then_inc(filled, 1)
            pool.memset(vnew[:, :, :, :], 0.0).then_inc(filled, 1)
            pool.memset(kT[:, :, 0:PAD], 0.0)
            pool.memset(eps[:, :], EPS)
            pool.memset(far[:, :, :], 0.0)
            pool.memset(sj[:, :, :], 0.0).then_inc(filled, 1)
            pool.memset(vb[:, :, :, :], 0.0).then_inc(filled, 1)
            pool.wait_ge(filled, 4)
            pool.memset(vb[:, :, :, HD:HD + 1], 1.0).then_inc(filled, 1)
            pool.wait_ge(const_ld, 16 * N_CONST)
            pool.tensor_scalar(se_w[:, :], se_t[:, :], HD ** -0.5, HD ** -0.5, ALU.mult, ALU.add).then_inc(made, 1)
            pool.wait_ge(made, 1)
            for r in range(4):
                view = sj[:, :, :].rearrange("p (a r) (s h) -> p a r s h", r=4, s=4)[:, :, r, r, :]
                w = se_w[:, :].rearrange("p (a r) -> p a r", r=4)[:, :, r]
                pool.tensor_tensor(view, w.unsqueeze(2).broadcast_to([P, J // 4, 8]),
                                   hmask[:, :].unsqueeze(1).broadcast_to([P, J // 4, 8]), ALU.mult).then_inc(made, 1)
            with pool.Fori(0, BATCH) as b:
                with pool.Fori(0, NCH) as n:
                    it = b * NCH + n
                    chunk_start(pool, it)
                    pool.wait_ge(qk_sb, it * 4 + 4)
                    k = 0
                    for m, (c, bank, r, g) in enumerate(PRODUCTS):
                        if ON_POOL[m]:
                            if k >= RING:
                                pool.wait_ge(prod_p_used, it * N_POOL + (k - RING + 1))
                            off = OFFSETS[BANK_J * bank + 4 * g + r]
                            pool.tensor_tensor(prod_p[:, k % RING, :], qT[:, c, :],
                                               kT[:, c, bass.ds(n * CH + (PAD - off), CH)], ALU.mult).then_inc(prod_p_ready, 1)
                            k += 1
                    pool.wait_ge(v_ld, it * 32 + 32)
                    for u in range(TILES):
                        t = it * TILES + u
                        pool.wait_ge(attn_ready, t + 1)
                        if u:
                            pool.wait_ge(pv_ps, t)
                        for f, src in enumerate((v7[:, u + 2], v96[:, u], v7[:, u])):
                            w = attn[:, :, NEAR + f:NEAR + f + 1].broadcast_to([P, H, HD])
                            dst = far[:, :, 0:HD] if f == 0 else fart[:, :, :]
                            pool.tensor_tensor(dst, w, src[:, :, 0:HD], ALU.mult).then_inc(far_step, 1)
                            if f:
                                pool.wait_ge(far_step, t * 5 + 2 * f)
                                i = pool.tensor_tensor(far[:, :, 0:HD], far[:, :, 0:HD], fart[:, :, :], ALU.add)
                                i.then_inc(far_step, 1)
                                pool.wait_ge(far_step, t * 5 + 2 * f + 1)
                        pool.sem_inc(far_ready, 1)

        @block.tensor
        def _(pe):
            pe.wait_ge(filled, 5)
            pe.wait_ge(const_ld, 16 * N_CONST)
            pe.wait_ge(made, 5)
            with pe.Fori(0, BATCH) as b:
                with pe.Fori(0, NCH) as n:
                    it = b * NCH + n
                    chunk_start(pe, it)
                    pe.wait_ge(chunk_ld, it * 80 + 80)
                    ln_pe(pe, it, 0)
                    xn_pe(pe, it, 0)
                    for u in range(4):
                        for k in range(KC):
                            mm = pe.matmul(PS[:, u, :], wqkv[:, k, u * P:(u + 1) * P], xn[:, k, :],
                                           start=(k == 0), stop=(k == KC - 1))
                        mm.then_inc(qk_ps, 1)
                    for s in range(TILES):
                        for k in range(KC):
                            mm = pe.matmul(PS[:, 6 + s // 2, (s % 2) * C:(s % 2 + 1) * C], xn[:, k, s * P:(s + 1) * P],
                                           wqkv[:, k, 2 * C:3 * C], start=(k == 0), stop=(k == KC - 1))
                        mm.then_inc(v_ps, 1)
                    kd = kp = 0
                    for m, (c, bank, r, g) in enumerate(PRODUCTS):
                        unit = c * len(BANKS) + bank
                        if r == 0 and g == 0 and unit >= 2:
                            pe.wait_ge(sc_sb, it * 6 + (unit - 1))
                        if ON_POOL[m]:
                            pe.wait_ge(prod_p_ready, it * N_POOL + (kp + 1))
                            rhs, used = prod_p[:, kp % RING, :], prod_p_used
                            kp += 1
                        else:
                            pe.wait_ge(prod_d_ready, it * N_DVE + (kd + 1))
                            rhs, used = prod_d[:, kd % RING, :], prod_d_used
                            kd += 1
                        j = BANK_J * bank + 4 * g + r
                        pe.matmul(PS[SLOT * g:SLOT * (g + 1), unit % 2, :], sj[:, j, :], rhs,
                                  start=(r == 0), stop=(r == 3)).then_inc(used, 1)
                    for u in range(TILES):
                        t = it * TILES + u
                        for c in range(KC):
                            pe.wait_ge(sc_sb, it * 6 + 3 * (c + 1))
                            if u or c:
                                pe.wait_ge(lg_ready, t * 2 + c)
                            for bank, nj in enumerate(BANKS):
                                mrows = 8 * nj
                                tr = pe.transpose(PS[:, 2, bank * P:bank * P + mrows],
                                                  sc[0:mrows, 3 * c + bank, u * P:(u + 1) * P], ident[0:mrows, 0:mrows])
                            tr.then_inc(l_ps, 1)
                        pe.wait_ge(parts_ready, t + 1)
                        for half in range(2):
                            if u or half:
                                pe.wait_ge(tp_sb, t * 2 + half)
                            for h in range(8):
                                tr = pe.transpose(TP[0:PARTS * NEAR, h, :],
                                                  parts[:, 8 * half + h].rearrange("p s j -> p (s j)"), identb[:, :])
                            tr.then_inc(tp_ps, 1)
                        pe.wait_ge(tp_sb, t * 2 + 2)
                        for q in range(6):
                            if q >= 3:
                                pe.wait_ge(a_sb, t * 6 + (q - 2))
                            first = 32 * q if q < 4 else 32 * (q - 4)
                            for tt in range(first, min(first + 32, P if q < 4 else NEAR - 1)):
                                a = (2 * P - 1 - tt) if q < 4 else (P - 1 - tt)
                                mm = pe.matmul(PS[:, 4 + q % 3, (tt - first) * H:(tt - first + 1) * H],
                                               band[:, a:a + P], parts_t[:, :, tt], start=True, stop=True)
                            mm.then_inc(sp_ps, 1)
                        pe.wait_ge(a_sb, t * 6 + 6)
                        pe.wait_ge(v_ld, it * 32 + 32)
                        pe.wait_ge(far_ready, t + 1)
                        if u:
                            pe.wait_ge(o_sb, t)
                        for g in range(HG):
                            for step in range(3):
                                for jh in range(GRP):
                                    h = GRP * g + jh
                                    out = PS[SLOT * jh:SLOT * (jh + 1), 7, g * P:(g + 1) * P]
                                    if step == 0:
                                        pe.matmul(out, v7[:, u + 3, h, :], a0[:, h, :], start=True, stop=False)
                                    elif step == 1:
                                        pe.matmul(out[:, 0:NEAR - 1], v7[:, u + 2, h, :], a1[:, h, :], start=False, stop=False)
                                    else:
                                        mm = pe.matmul(out, far[:, h, :], ident[:, :], start=False, stop=True)
                        mm.then_inc(pv_ps, 1)
                    pe.wait_ge(o_sb, it * TILES + TILES)
                    for m in range(KC):
                        for g in range(HG):
                            mm = pe.matmul(PS[:, m, :], wo[:, g, m * P:(m + 1) * P], oT[:, g, :],
                                           start=(g == 0), stop=(g == HG - 1))
                        mm.then_inc(y_ps, 1)
                    pe.wait_ge(x_updated, it * 2 + 1)
                    ln_pe(pe, it, 1)
                    xn_pe(pe, it, 1)
                    for m in range(KC):
                        for k in range(KC):
                            mm = pe.matmul(PS[:, 2 + m, :], mtc[:, k, m * P:(m + 1) * P], xn[:, k, :],
                                           start=(k == 0), stop=(k == KC - 1))
                        mm.then_inc(ffn_ps, 1)
                    pe.wait_ge(x_updated, it * 2 + 2)
                    ln_pe(pe, it, 2)
                    xn_pe(pe, it, 2)
                    for u in range(4):
                        if u >= 2:
                            pe.wait_ge(qkb_read, it * 4 + (u - 1))
                        for w, bank in ((wqkv_b, 2 * (u % 2)), (wrot, 2 * (u % 2) + 1)):
                            for k in range(KC):
                                mm = pe.matmul(PS[:, bank, :], w[:, k, u * P:(u + 1) * P], xn[:, k, :],
                                               start=(k == 0), stop=(k == KC - 1))
                        mm.then_inc(qkb_ps, 1)
                    for s in range(TILES):
                        for k in range(KC):
                            mm = pe.matmul(PS[:, 6 + s // 2, (s % 2) * C:(s % 2 + 1) * C], xn[:, k, s * P:(s + 1) * P],
                                           wqkv_b[:, k, 2 * C:3 * C], start=(k == 0), stop=(k == KC - 1))
                        mm.then_inc(vb_ps, 1)

        @block.scalar
        def _(act):
            act.wait_ge(filled, 5)
            with act.Fori(0, BATCH) as b:
                with act.Fori(0, NCH) as n:
                    it = b * NCH + n
                    chunk_start(act, it)
                    ln_act(act, it, 0)
                    for u in range(4):
                        act.wait_ge(qk_ps, it * 4 + (u + 1))
                        dst = qT[:, u, :] if u < 2 else kT[:, u - 2, bass.ds(n * CH + PAD, CH)]
                        act.copy(dst, PS[:, u, :]).then_inc(qk_sb, 1)
                    for s in range(2):
                        act.wait_ge(v_ps, it * 4 + (2 * s + 2))
                        act.copy(vnew[:, 2 * s:2 * s + 2, :, 0:HD],
                                 PS[:, 6 + s, :].rearrange("p (s h d) -> p s h d", s=2, d=HD)).then_inc(v_sb, 1)
                    for unit in range(2 * len(BANKS)):
                        act.wait_ge(prod_d_used, it * N_DVE + SUMMED[unit][0])
                        act.wait_ge(prod_p_used, it * N_POOL + SUMMED[unit][1])
                        rows = 8 * BANKS[unit % 3]
                        act.copy(sc[0:rows, unit, :], PS[0:rows, unit % 2, :]).then_inc(sc_sb, 1)
                    for u in range(TILES):
                        t = it * TILES + u
                        act.wait_ge(lg_shifted, t + 1)
                        for c in range(KC):
                            e = act.activation(attn[:, 8 * c:8 * c + 8, :], lg[:, c].rearrange("p j h -> p h j"), ACT.Exp)
                        e.then_inc(exp_ready, 1)
                        act.wait_ge(attn_ready, t + 1)
                        act.copy(parts[:, :, 0, :], attn[:, :, 0:NEAR]).then_inc(part_cast, 1)
                        act.wait_ge(rest_ready, t + 1)
                        act.copy(parts[:, :, 1, :], rest[:, :, :]).then_inc(part_cast, 1)
                        for q in range(6):
                            act.wait_ge(sp_ps, t * 6 + (q + 1))
                            nt = 32 if q < 5 else NEAR - 1 - 32
                            dst = a0[:, :, 32 * q:32 * q + 32] if q < 4 else a1[:, :, 32 * (q - 4):32 * (q - 4) + nt]
                            act.copy(dst, PS[:, 4 + q % 3, 0:nt * H].rearrange("p (t h) -> p h t", h=H)).then_inc(a_sb, 1)
                    ln_act(act, it, 1)
                    ln_act(act, it, 2)
                    for u in range(4):
                        act.wait_ge(rope_rest, it * 8 + 2 * u + 1)
                        act.copy(qparts[:, 0, :], rope_q[:, :]).then_inc(rope_cast, 1)
                        act.wait_ge(rope_rest, it * 8 + 2 * u + 2)
                        act.copy(qparts[:, 1, :], rope_r[:, :]).then_inc(rope_cast, 1)
                    for s in range(2):
                        act.wait_ge(vb_ps, it * 4 + (2 * s + 2))
                        act.copy(vb[:, 2 * s:2 * s + 2, :, 0:HD],
                                 PS[:, 6 + s, :].rearrange("p (s h d) -> p s h d", s=2, d=HD)).then_inc(vb_sb, 1)

        STEPS = TILES * 6 + 4 * 2

        @block.vector
        def _(dve):
            dve.wait_ge(filled, 5)
            dve.wait_ge(const_ld, 16 * N_CONST)
            with dve.Fori(0, BATCH) as b:
                with dve.Fori(0, NCH) as n:
                    it = b * NCH + n
                    count = [0]

                    def then(ins):
                        count[0] += 1
                        ins.then_inc(dve_step, 1)
                        dve.wait_ge(dve_step, it * STEPS + count[0])

                    chunk_start(dve, it)
                    dve.wait_ge(chunk_ld, it * 80 + 80)
                    ln_dve(dve, it, 0)
                    dve.wait_ge(qk_sb, it * 4 + 4)
                    k = 0
                    for m, (c, bank, r, g) in enumerate(PRODUCTS):
                        if not ON_POOL[m]:
                            if k >= RING:
                                dve.wait_ge(prod_d_used, it * N_DVE + (k - RING + 1))
                            off = OFFSETS[BANK_J * bank + 4 * g + r]
                            dve.tensor_tensor(prod_d[:, k % RING, :], qT[:, c, :],
                                              kT[:, c, bass.ds(n * CH + (PAD - off), CH)], ALU.mult).then_inc(prod_d_ready, 1)
                            k += 1
                    for u in range(TILES):
                        t = it * TILES + u
                        for c in range(KC):
                            dve.wait_ge(l_ps, t * 2 + (c + 1))
                            dve.tensor_tensor(lg[:, c].rearrange("p j h -> p (j h)"), PS[:, 2, 0:8 * J],
                                              pbias[:, c].rearrange("p j h -> p (j h)"), ALU.add).then_inc(lg_ready, 1)
                        dve.wait_ge(lg_ready, t * 2 + 2)
                        mask = vmask[:, bass.ds(n * TILES + u, 1), :].rearrange("p a j -> p (a j)") \
                            .unsqueeze(2).broadcast_to([P, J, 8])
                        for c in range(KC):
                            i = dve.tensor_tensor(lg[:, c], lg[:, c], mask, ALU.add)
                        then(i)
                        for c in range(KC):
                            i = dve.tensor_reduce(red[:, 0, 8 * c:8 * c + 8], lg[:, c].rearrange("p j h -> p h j"), AX_X, ALU.max)
                        then(i)
                        for c in range(KC):
                            i = dve.tensor_tensor(lg[:, c], lg[:, c],
                                                  red[:, 0, 8 * c:8 * c + 8].unsqueeze(1).broadcast_to([P, J, 8]), ALU.subtract)
                        i.then_inc(lg_shifted, 1)
                        dve.wait_ge(exp_ready, t + 1)
                        then(dve.tensor_reduce(red[:, 1, :], attn[:, :, :], AX_X, ALU.add))
                        then(dve.reciprocal(red[:, 2, :], red[:, 1, :]))
                        then(dve.tensor_tensor(red[:, 3, :], red[:, 2, :], gain[:, :], ALU.mult))
                        i = dve.tensor_tensor(attn[:, :, :], attn[:, :, :], red[:, 3, :].unsqueeze(2).broadcast_to([P, H, J]), ALU.mult)
                        i.then_inc(attn_ready, 1)
                        dve.wait_ge(part_cast, t * 2 + 1)
                        dve.tensor_tensor(rest[:, :, :], attn[:, :, 0:NEAR], parts[:, :, 0, :], ALU.subtract).then_inc(rest_ready, 1)
                        dve.wait_ge(part_cast, t * 2 + 2)
                        dve.tensor_tensor(parts[:, :, 2, :], rest[:, :, :], parts[:, :, 1, :], ALU.subtract).then_inc(parts_ready, 1)
                        for half in range(2):
                            dve.wait_ge(tp_ps, t * 2 + (half + 1))
                            dve.tensor_copy(parts_t[:, 8 * half:8 * half + 8, :], TP[0:PARTS * NEAR]).then_inc(tp_sb, 1)
                        dve.wait_ge(pv_ps, t + 1)
                        dve.tensor_copy(oT[:, :, u * P:(u + 1) * P],
                                        PS[:, 7, :].rearrange("p (g t) -> p g t", g=HG)).then_inc(o_sb, 1)
                        then(dve.engine_nop())
                    dve.wait_ge(y_ps, it * 2 + 2)
                    dve.tensor_tensor(xc[:, :, :], xc[:, :, :], PS[:, 0:KC, :], ALU.add).then_inc(x_updated, 1)
                    ln_dve(dve, it, 1)
                    dve.wait_ge(ffn_ps, it * 2 + 2)
                    for m in range(KC):
                        i = dve.scalar_tensor_tensor(out=xc[:, m, :], in0=PS[:, 2 + m, :], scalar=bcc[:, m:m + 1],
                                                     in1=xc[:, m, :], op0=ALU.add, op1=ALU.add)
                    i.then_inc(x_updated, 1)
                    ln_dve(dve, it, 2)
                    for u in range(4):
                        dve.wait_ge(qkb_ps, it * 4 + (u + 1))
                        dve.tensor_tensor(rope_a[:, :], PS[:, 2 * (u % 2), :], cosc[:, :], ALU.mult)
                        i = dve.tensor_tensor(rope_b[:, :], PS[:, 2 * (u % 2) + 1, :], sinc[:, :], ALU.mult)
                        i.then_inc(qkb_read, 1)
                        dve.wait_ge(qkb_read, it * 4 + (u + 1))
                        dve.tensor_tensor(rope_q[:, :], rope_a[:, :], rope_b[:, :], ALU.add).then_inc(dve_step, 1)
                        count[0] += 1
                        dve.wait_ge(dve_step, it * STEPS + count[0])
                        if u:
                            dve.wait_ge(qparts_stored, it * 64 + 16 * u)
                        dve.sem_inc(rope_rest, 1)
                        dve.wait_ge(rope_cast, it * 8 + (2 * u + 1))
                        dve.tensor_tensor(rope_r[:, :], rope_q[:, :], qparts[:, 0, :], ALU.subtract).then_inc(rope_rest, 1)
                        dve.wait_ge(rope_cast, it * 8 + (2 * u + 2))
                        dve.tensor_tensor(qparts[:, 2, :], rope_r[:, :], qparts[:, 1, :], ALU.subtract).then_inc(qparts_ready, 1)
                        then(dve.engine_nop())
                    assert count[0] == STEPS, count


def full_attention(nc, D):
    KT = T // P
    NGROUP = BATCH * HG
    ITERS = NGROUP * NCH
    MAXU = GRP * TILES * NCH
    PER_STEP = MAXU // KT
    AHEAD = 4
    CARRY = AHEAD * PER_STEP
    QK_LOADS = 16 * 6 * (1 + NCH)

    LOOP = []
    for kk in range(KT):
        ahead = kk >= KT - AHEAD
        first = (kk - (KT - AHEAD)) * PER_STEP if ahead else CARRY + kk * PER_STEP
        LOOP.append([("max", int(ahead), u) for u in range(first, first + PER_STEP)])
    LOOP[2].append(("sum", 0))
    LOOP[4].append(("sum", 1))
    LOOP[KT - AHEAD + 1].append(("rows",))
    LAST = [[op for op in step if op[0] == "sum"] for step in LOOP]
    FIRST = [[("max", 0, u) for u in range(n * PER_STEP, (n + 1) * PER_STEP)] for n in range(KT)]
    FIRST[2].append(("sum", 0))
    FIRST[4].append(("sum", 1))
    FIRST += [[("max", 1, u)] for u in range(CARRY)]
    FIRST[KT + 6].append(("rows",))
    BANKS_OF = sum(map(len, LOOP))
    SKIPPED = (BANKS_OF - sum(map(len, FIRST))) % 3
    BANKS_FIRST = SKIPPED + sum(map(len, FIRST))
    assert BANKS_OF % 3 == 1

    with ExitStack() as ctx:
        sb = lambda n, s, d: ctx.enter_context(nc.sbuf_tensor(n, s, d))
        sem = lambda n: ctx.enter_context(nc.semaphore(n))
        ps_s = ctx.enter_context(nc.psum_tensor("ps_s", [P, 2, 2, CH], F32))
        ps_m = ctx.enter_context(nc.psum_tensor("ps_m", [P, 3, CH], F32))
        ps_o = ctx.enter_context(nc.psum_tensor("ps_o", [P, CH], F32))
        qs = sb("qs", [KROWS + PARTS, HG * NCH, GRP, CH], BF16)
        ks = sb("ks", [KROWS + PARTS, HG, GRP, T], BF16)
        vg = sb("vg", [P, KT, GRP, SLOT], F32)
        pr = sb("pr", [P, 2, GRP, CH], F32)
        mx = sb("mx", [P, GRP * TILES, NCH], F32)
        nm = sb("nm", [P, GRP * TILES], F32)
        nmr = sb("nmr", [P, GRP * TILES], F32)
        nmp = sb("nmp", [P, P // 16, GRP * TILES], BF16)
        nmt = sb("nmt", [PARTS * GRP * TILES, P], BF16)
        identb = sb("identb2", [P, P], BF16)
        sel = sb("sel", [P, SLOT], F32)
        spread = sb("spread2", [P, TILES, P], F32)
        ou = sb("ou", [P, CH], F32)
        orc = sb("orc", [P, P], F32)
        on = sb("on", [P, CH], F32)
        (const_ld, filled, qk_ld, qk_ready, va_ld, vb_ld, vc_ld, s_ps, p_ready, pv_done, m_ps, m_read, nm_step,
         nmp_ready, nmt_sb, neg_ld, o_ps, o_sb, orc_ready, on_ready, o_stored) = (sem("c_" + n) for n in (
             "const_ld", "filled", "qk_ld", "qk_ready", "va_ld", "vb_ld", "vc_ld", "s_ps", "p_ready", "pv_done", "m_ps",
             "m_read", "nm_step", "nmp_ready", "nmt_sb", "neg_ld", "o_ps", "o_sb", "orc_ready", "on_ready",
             "o_stored"))
        block = ctx.enter_context(nc.Block())

        def taken(x):
            return 0 if isinstance(x, int) and x == 0 else x * BANKS_OF + (BANKS_FIRST - BANKS_OF)

        def unit_place(u):
            return u // (TILES * NCH), u // NCH % TILES, u % NCH

        @block.sync
        def _(sp):
            sp.dma_start(identb[:, :], D["identb"]).then_inc(const_ld, 16)
            sp.dma_start(sel[:, :], D["sel"]).then_inc(const_ld, 16)
            sp.dma_start(spread[:, :, :], D["spread"]).then_inc(const_ld, 16)

            with sp.Fori(0, BATCH) as b:
                with sp.Fori(0, HG * NCH) as q:
                    sp.wait_ge(nmt_sb, b * (HG * NCH) + q + 1)
                    sp.dma_start(qs[KROWS:KROWS + PARTS, bass.ds(q, 1), :, :].rearrange("a n j t -> a (n j t)"),
                                 nmt[:, :]).then_inc(neg_ld, 16)

        @block.gpsimd
        def _(pool):
            pool.memset(ks[KROWS:KROWS + PARTS, :, :, :], 1.0).then_inc(filled, 1)
            pool.wait_ge(filled, 1)
            pool.memset(ou[:, :], 1.0).then_inc(filled, 1)
            pool.memset(pr[:, 1, :, :], 1.0).then_inc(filled, 1)
            pool.memset(nmp[:, :, :], 0.0).then_inc(filled, 1)
            pool.wait_ge(filled, 4)

            def load_qk(b, g, G):
                rows = bass.ds(g * (GRP * HD), GRP * HD)
                for i in range(6):
                    r = slice(HD * i, HD * (i + 1))
                    pool.dma_start(ks[r, bass.ds(g, 1), :, :].rearrange("p a j t -> p (a j) t"),
                                   D["k_d"][b, K_STACK[i], rows, :].rearrange("(j d) t -> d j t", d=HD)).then_inc(qk_ld, 16)
                    for n in range(NCH):
                        pool.dma_start(qs[r, bass.ds(g * NCH + n, 1), :, :].rearrange("p a j t -> p (a j) t"),
                                       D["q_d"][b, Q_STACK[i], rows, n * CH:(n + 1) * CH].rearrange("(j d) t -> d j t", d=HD)
                                       ).then_inc(qk_ld, 16)
                pool.wait_ge(qk_ld, G * QK_LOADS + QK_LOADS)
                pool.sem_inc(qk_ready, 1)

            def load_v(b, g, first, last, loaded):
                pool.dma_start(vg[:, first:last, :, :].rearrange("p k j d -> p k (j d)"),
                               D["vb_d"][b, first * P:last * P, bass.ds(g * (GRP * SLOT), GRP * SLOT)]
                               .rearrange("(k p) n -> p k n", p=P)).then_inc(loaded, 16)

            def outs(x):
                pool.wait_ge(on_ready, x + 1)
                pool.dma_start(D["o_d"][x], on[:, :]).then_inc(o_stored, 16)

            def group(G, more_qk, more_v):
                outs(G * NCH + 1)
                if more_qk:
                    n = G + 3
                    load_qk(pool.snap(n // HG), pool.snap(n % HG), n)
                for i in range(1, NCH):
                    outs(G * NCH + (i + 1))
                if more_v:
                    n = G + 1
                    b, g = pool.snap(n // HG), pool.snap(n % HG)
                    for first, last, loaded in ((0, 8, va_ld), (8, KT - 1, vb_ld), (KT - 1, KT, vc_ld)):
                        pool.wait_ge(pv_done, G * (NCH * KT) + ((NCH - 1) * KT + (last - 1) + 3))
                        load_v(b, g, first, last, loaded)

            load_qk(0, 0, 0)
            for first, last, loaded in ((0, 8, va_ld), (8, KT - 1, vb_ld), (KT - 1, KT, vc_ld)):
                load_v(0, 0, first, last, loaded)
            outs(0)
            for g in range(1, 4):
                load_qk(0, g, g)
            with pool.Fori(0, 1) as G:
                group(G, False, True)
            with pool.Fori(1, NGROUP - 3) as G:
                group(G, True, True)
            pool.sem_inc(qk_ready, 1)
            with pool.Fori(NGROUP - 3, NGROUP - 1) as G:
                group(G, False, True)
            with pool.Fori(NGROUP - 1, NGROUP) as G:
                group(G, False, False)
            outs(ITERS + 1)
            pool.wait_ge(o_stored, 16 * (ITERS + 2))

        @block.tensor
        def _(pe):
            pe.wait_ge(const_ld, 48)
            pe.wait_ge(filled, 4)
            pe.sem_inc(pv_done, 1)

            def bank_free(x, u):
                pe.wait_ge(m_read, taken(x) + (u + 1 if u >= 3 else (3, 1, 2)[u]))

            def max_unit(x, u, pos, nq, nslot):
                j, qt, kc = unit_place(u)
                bank_free(x, pos)
                pe.matmul(ps_m[:, pos % 3, :], qs[0:KROWS, bass.ds(nq, 1), j, qt * P:(qt + 1) * P].rearrange("p a t -> p (a t)"),
                          ks[0:KROWS, bass.ds(nslot, 1), j, kc * CH:(kc + 1) * CH].rearrange("p a t -> p (a t)"),
                          start=True, stop=True).then_inc(m_ps, 1)

            def sums(x, pos, part, n=None):
                bank_free(x, pos)
                if part == 0:
                    pe.wait_ge(o_sb, (x if n is None else n) + 1)
                    for q in range(TILES):
                        mm = pe.matmul(ps_m[SLOT * q:SLOT * (q + 1), pos % 3, 0:P], sel[:, :], ou[:, q * P:(q + 1) * P],
                                       start=True, stop=True)
                else:
                    pe.wait_ge(orc_ready, (x if n is None else n) + 1)
                    for q in range(TILES):
                        mm = pe.matmul(ps_m[:, pos % 3, q * P:(q + 1) * P], spread[:, q, :], orc[:, :],
                                       start=True, stop=True)
                mm.then_inc(m_ps, 1)

            def max_rows(x, pos):
                bank_free(x, pos)
                pe.wait_ge(nmp_ready, x + 1)
                pe.transpose(ps_m[:, pos % 3, 0:P // 2].bitcast(BF16),
                             nmp[:, :, :].rearrange("p s n -> p (s n)"), identb[:, :]).then_inc(m_ps, 1)

            def weigh(kt, ready):
                pe.wait_ge(p_ready, ready)
                for j in range(GRP):
                    mm = pe.matmul(ps_o[SLOT * j:SLOT * (j + 1), :], vg[:, kt, j, :], pr[:, kt % 2, j, :],
                                   start=(kt == 0), stop=(kt == KT - 1), skip_group_check=True)
                mm.then_inc(pv_done, 1)
                return mm

            def fill(x, pos, op, sets):
                if op[0] == "max":
                    max_unit(x, op[2], pos, *sets[op[1]])
                elif op[0] == "sum":
                    sums(x, pos, op[1])
                else:
                    max_rows(x, pos)

            def iteration(x, plan, q, slot, group, sets, groups):
                pos = 0
                pe.wait_ge(neg_ld, x * 16)
                for kk in range(KT):
                    ops = list(plan[kk])
                    if sets and kk == 0:
                        pe.wait_ge(qk_ready, groups[0] + 1)
                    if sets and kk == KT - AHEAD:
                        pe.wait_ge(qk_ready, groups[1] + 1)

                    def fills(n):
                        nonlocal pos
                        for op in ops[:n]:
                            fill(x, pos, op, sets)
                            pos += 1
                        del ops[:n]

                    for pair in range(2):
                        pe.wait_ge(p_ready, x * (2 * KT) + (2 * kk + pair + 1 - 2 * KT))
                        for jj in range(2):
                            j = 2 * pair + jj
                            mm = pe.matmul(ps_s[:, pair, jj, :],
                                           ks[:, bass.ds(slot, 1), j, kk * P:(kk + 1) * P].rearrange("p a t -> p (a t)"),
                                           qs[:, bass.ds(q, 1), j, :].rearrange("p a t -> p (a t)"),
                                           start=True, stop=True)
                        mm.then_inc(s_ps, 1)
                        if len(ops) > 1:
                            fills(1)
                    if kk == 1:
                        pe.wait_ge(va_ld, group * 16 + 16)
                        pe.wait_ge(o_sb, x + 1)
                    if kk == 9:
                        pe.wait_ge(vb_ld, group * 16 + 16)
                    if kk == KT - 1:
                        pe.wait_ge(vc_ld, group * 16 + 16)
                    weigh((kk - 1) % KT, x * (2 * KT) + (2 * kk + 2 - 2 * KT))
                    fills(len(ops))

            pe.wait_ge(qk_ready, 1)
            for pos, op in enumerate((op for step in FIRST for op in step), SKIPPED):
                fill(0, pos, op, ((0, 0), (1, 0)))
            pe.wait_ge(vc_ld, 16)
            for j in range(GRP):
                pe.matmul(ps_o[SLOT * j:SLOT * (j + 1), :], vg[:, KT - 1, j, :], pr[:, 1, j, :],
                          start=True, stop=False, skip_group_check=True)
            with pe.Fori(1, ITERS) as x:
                group = [pe.snap((x + d) >> (NCH.bit_length() - 1)) for d in (-1, 0, 1)]
                q = [pe.snap((x + d) & (HG * NCH - 1)) for d in (-1, 0, 1)]
                slot = [pe.snap(g & (HG - 1)) for g in group]
                iteration(x, LOOP, q[0], slot[0], group[0], ((q[1], slot[1]), (q[2], slot[2])), group[1:])
            iteration(ITERS, LAST, HG * NCH - 1, HG - 1, NGROUP - 1, None, None)
            weigh(KT - 1, 2 * KT * ITERS + 2)
            for part in range(2):
                sums(ITERS, 2 + part, part, ITERS + 1)

        @block.scalar
        def _(act):
            act.wait_ge(filled, 4)
            act.sem_inc(p_ready, 2)

            def take_output(x):
                act.wait_ge(pv_done, x * KT + (2 - KT))
                act.wait_ge(on_ready, x)
                act.copy(ou[:, :], ps_o[:, :]).then_inc(o_sb, 1)

            with act.Fori(0, ITERS) as i:
                for kk in range(KT):
                    act.wait_ge(pv_done, i * KT + (kk + 1))
                    for pair in range(2):
                        act.wait_ge(s_ps, i * (2 * KT) + (2 * kk + pair + 1))
                        act.activation(pr[:, kk % 2, 2 * pair:2 * pair + 2, :], ps_s[:, pair, :, :], ACT.Exp,
                                       scale=HD ** -0.5).then_inc(p_ready, 1)
                    if kk == 0:
                        take_output(i + 1)
            take_output(ITERS + 1)

        @block.vector
        def _(dve):
            dve.wait_ge(filled, 4)
            dve.sem_inc(m_read, 3 + SKIPPED)
            dve.sem_inc(m_ps, SKIPPED)
            dve.sem_inc(o_sb, 1)

            def max_unit(x, u, pos):
                dve.wait_ge(m_ps, taken(x) + (pos + 1))
                j, qt, kc = unit_place(u)
                return dve.tensor_reduce(mx[:, j * TILES + qt, kc:kc + 1], ps_m[:, pos % 3, :], AX_X, ALU.max).then_inc(m_read, 1)

            def sums(x, pos, part, n=None):
                dve.wait_ge(m_ps, taken(x) + (pos + 1))
                if part == 0:
                    dve.reciprocal(orc[:, :], ps_m[:, pos % 3, 0:P]).then_inc(m_read, 1)
                    dve.wait_ge(m_read, taken(x) + (pos + 4))
                    dve.sem_inc(orc_ready, 1)
                else:
                    n = x if n is None else n
                    if not isinstance(n, int) or n:
                        dve.wait_ge(o_stored, n * 16)
                    dve.tensor_tensor(on[:, :], ou[:, :], ps_m[:, pos % 3, :], ALU.mult).then_inc(m_read, 1)
                    dve.wait_ge(m_read, taken(x) + (pos + 4))
                    dve.sem_inc(on_ready, 1)

            def max_parts(x, pos):
                NS = 5

                def after(n):
                    dve.wait_ge(nm_step, x * NS + n)

                dve.wait_ge(m_read, taken(x) + (pos + 3))
                dve.tensor_reduce(nm[:, :], mx[:, :, :], AX_X, ALU.max, negate=True).then_inc(nm_step, 1)
                after(1)
                yield
                dve.tensor_copy(nmp[:, 0, :], nm[:, :]).then_inc(nm_step, 1)
                yield
                after(2)
                dve.tensor_tensor(nmr[:, :], nm[:, :], nmp[:, 0, :], ALU.subtract).then_inc(nm_step, 1)
                yield
                after(3)
                dve.tensor_copy(nmp[:, 1, :], nmr[:, :]).then_inc(nm_step, 1)
                yield
                after(4)
                dve.tensor_tensor(nmp[:, 2, :], nmr[:, :], nmp[:, 1, :], ALU.subtract).then_inc(nm_step, 1)
                yield
                after(5)
                dve.sem_inc(nmp_ready, 1)

            def max_rows(x, pos):
                dve.wait_ge(m_ps, taken(x) + (pos + 1))
                if not (isinstance(x, int) and x == 0):
                    dve.wait_ge(neg_ld, x * 16)
                dve.tensor_copy(nmt[:, :], ps_m[0:PARTS * 16, pos % 3, 0:P // 2].bitcast(BF16)).then_inc(m_read, 1)
                dve.wait_ge(m_read, taken(x) + (pos + 4))
                dve.sem_inc(nmt_sb, 1)

            def iteration(x, plan, pos=0):
                steps = iter(())
                for op in (op for step in plan for op in step):
                    if op[0] == "max":
                        max_unit(x, op[2], pos)
                        next(steps, None)
                    elif op[0] == "sum":
                        sums(x, pos, op[1])
                    else:
                        max_rows(x, pos)
                    pos += 1
                    if op[0] == "max" and op[2] == MAXU - 1:
                        steps = max_parts(x, pos)
                        next(steps)

            iteration(0, FIRST, SKIPPED)
            with dve.Fori(1, ITERS) as x:
                iteration(x, LOOP)
            iteration(ITERS, LAST)
            for part in range(2):
                sums(ITERS, 2 + part, part, ITERS + 1)


def final_stage(nc, I, D, out):
    with ExitStack() as ctx:
        sb = lambda n, s, d: ctx.enter_context(nc.sbuf_tensor(n, s, d))
        sem = lambda n: ctx.enter_context(nc.semaphore("f_" + n))
        PS = ctx.enter_context(nc.psum_tensor("PSf", [P, 8, CH], F32))
        ones = sb("f_ones", [P, P], F32)
        spread = sb("f_spread", [P, TILES, P], F32)
        eps = sb("f_eps", [P, 1], F32)
        wo = sb("f_wo", [P, HG, C], F32)
        xc = sb("f_xc", [P, KC, CH], F32)
        oT = sb("f_oT", [P, HG, CH], F32)
        mtc = sb("f_mtc", [P, KC, C], F32)
        bcc = sb("f_bcc", [P, KC], F32)
        filled, const_ld, chunk_ld, y_ps, ffn_ps, x_updated, stored = (
            sem(n) for n in ("filled", "const_ld", "chunk_ld", "y_ps", "ffn_ps", "x_updated", "stored"))
        fsb = lambda n, s, d: sb("f_" + n, s, d)
        xn, ln_pe, ln_act, ln_dve, xn_pe = layer_norm(nc, ctx, fsb, sem, PS, 4, 5, ones, spread, eps, xc, 1)
        block = ctx.enter_context(nc.Block())
        LOADS = 16 * (HG + 3)

        @block.sync
        def _(sp):
            sp.dma_start(spread[:, :, :], I["spread"]).then_inc(const_ld, 16)
            sp.wait_ge(filled, 2)
            for j in range(GRP):
                for g in range(HG):
                    sp.dma_start(wo[SLOT * j:SLOT * j + HD, g, :],
                                 I["wo_b"][HD * (GRP * g + j):HD * (GRP * g + j + 1), :]).then_inc(const_ld, 16)
            with sp.Fori(0, BATCH) as b:
                with sp.Fori(0, NCH) as n:
                    it = b * NCH + n
                    sp.wait_ge(stored, it * 16 + 16)
                    cols = bass.ds(it * CH, CH)
                    for g in range(HG):
                        sp.dma_start(oT[:, g, :], D["o_d"][b * (HG * NCH) + n + (2 + g * NCH)]).then_inc(chunk_ld, 16)
                    sp.dma_start(xc[:, :, :], D["x_d"][:, cols].rearrange("(k p) t -> p k t", p=P)).then_inc(chunk_ld, 16)
                    sp.dma_start(mtc[:, :, :], D["mt_d"][it].rearrange("(k p) n -> p k n", p=P)).then_inc(chunk_ld, 16)
                    sp.dma_start(bcc[:, :], D["bc_d"][it].rearrange("(k p) -> p k", p=P),
                                 allow_slow_non_contiguous=True).then_inc(chunk_ld, 16)
                    sp.wait_ge(x_updated, it * 2 + 2)
                    sp.dma_start(out[:, cols].rearrange("(k p) t -> p k t", p=P), xc[:, :, :]).then_inc(stored, 16)
            sp.wait_ge(stored, 16 * NG + 16)

        @block.gpsimd
        def _(pool):
            pool.memset(wo[:, :, :], 0.0).then_inc(filled, 1)
            pool.memset(eps[:, :], EPS).then_inc(filled, 1)
            pool.memset(ones[:, :], 1.0 / C).then_inc(filled, 1)
            pool.sem_inc(stored, 16)

        @block.tensor
        def _(pe):
            pe.wait_ge(filled, 3)
            pe.wait_ge(const_ld, 16 * (GRP * HG + 1))
            with pe.Fori(0, NG) as it:
                pe.wait_ge(chunk_ld, it * LOADS + LOADS)
                for m in range(KC):
                    for g in range(HG):
                        mm = pe.matmul(PS[:, m, :], wo[:, g, m * P:(m + 1) * P], oT[:, g, :],
                                       start=(g == 0), stop=(g == HG - 1))
                    mm.then_inc(y_ps, 1)
                pe.wait_ge(x_updated, it * 2 + 1)
                ln_pe(pe, it, 0)
                xn_pe(pe, it, 0)
                for m in range(KC):
                    for k in range(KC):
                        mm = pe.matmul(PS[:, 2 + m, :], mtc[:, k, m * P:(m + 1) * P], xn[:, k, :],
                                       start=(k == 0), stop=(k == KC - 1))
                    mm.then_inc(ffn_ps, 1)

        @block.scalar
        def _(act):
            act.wait_ge(filled, 3)
            with act.Fori(0, NG) as it:
                ln_act(act, it, 0)

        @block.vector
        def _(dve):
            with dve.Fori(0, NG) as it:
                dve.wait_ge(chunk_ld, it * LOADS + LOADS)
                dve.wait_ge(y_ps, it * 2 + 2)
                dve.tensor_tensor(xc[:, :, :], xc[:, :, :], PS[:, 0:KC, :], ALU.add).then_inc(x_updated, 1)
                dve.wait_ge(x_updated, it * 2 + 1)
                ln_dve(dve, it, 0)
                dve.wait_ge(ffn_ps, it * 2 + 2)
                for m in range(KC):
                    i = dve.scalar_tensor_tensor(out=xc[:, m, :], in0=PS[:, 2 + m, :], scalar=bcc[:, m:m + 1],
                                                 in1=xc[:, m, :], op0=ALU.add, op1=ALU.add)
                i.then_inc(x_updated, 1)


def build(nc, I, out):
    dram = lambda n, s, d: nc.dram_tensor(n, s, d, kind="Internal").ap()
    D = {
        "mt_d": dram("mt_d", (NG, C, C), F32),
        "bc_d": dram("bc_d", (NG, C), F32),
        "v_d": dram("v_d", (BATCH, PAD + T, H * SLOT), F32),
        "vb_d": dram("vb_d", (BATCH, T, H * SLOT), F32),
        "x_d": dram("x_d", (C, BATCH * T), F32),
        "q_d": dram("q_d", (BATCH, PARTS, C, T), BF16),
        "k_d": dram("k_d", (BATCH, PARTS, C, T), BF16),
        "o_d": dram("o_d", (2 + BATCH * HG * NCH, P, CH), F32),
        "identb": I["identb"],
        "sel": I["sel"],
        "spread": I["spread"],
    }
    fold_ffn(nc, I["W1"], I["W2T"], I["b1"], I["b2"], D["mt_d"], D["bc_d"])
    local_stage(nc, I, D)
    full_attention(nc, D)
    final_stage(nc, I, D, out)


def constants():
    bf = mybir.dt.np(BF16)
    f = np.float32
    inv = (f(1.0) / f(10000.0) ** (np.arange(0, HD, 2, dtype=f) / f(HD))).astype(f)
    ang = np.outer(np.arange(T, dtype=f), inv).astype(f)
    d = np.arange(P) % HD
    sign = np.where(d < HD // 2, -1.0, 1.0).astype(f)[:, None]
    cosT = np.cos(ang).astype(f).T[d % (HD // 2)]
    sinT = np.sin(ang).astype(f).T[d % (HD // 2)] * sign
    t = np.arange(T).reshape(T // P, P)
    vmask = np.where(t.T[:, :, None] >= np.array(OFFSETS)[None, None, :], f(0), np.finfo(f).min).astype(f)
    j = np.tile(np.arange(NEAR), PARTS)
    band = (np.arange(EBW)[None, :] == (2 * P - 1 - j)[:, None]).astype(bf)
    p = np.arange(P)
    return {
        "cosT": np.ascontiguousarray(cosT), "sinT": np.ascontiguousarray(sinT.astype(f)), "vmask": vmask,
        "band": band, "ident": np.eye(P, dtype=f), "identb": np.eye(P).astype(bf),
        "hmask": (p[:, None] // HD == np.arange(8)[None, :]).astype(f),
        "sel": (p[:, None] == (np.arange(SLOT)[None, :] // 8 * SLOT + HD)).astype(f),
        "spread": (p[:, None, None] == (SLOT * np.arange(TILES)[None, :, None] + 8 * (p[None, None, :] // SLOT))).astype(f),
    }


def kernel(**inputs):
    import concourse.bacc as bacc
    from concourse.bass_utils import run_bass_kernel_spmd

    a = {k[3:]: np.asarray(v) for k, v in inputs.items()}
    tokens = BATCH * T
    wqkv_b = a["attn_b_Wqkv"]
    turned = (np.arange(2 * C) // HD) * HD + (np.arange(2 * C) + HD // 2) % HD
    arrays = {
        "xT": a["attn_a_x"].reshape(tokens, C).T,
        "wqkv": a["attn_a_w_qkv"], "wo": a["attn_a_w_out"], "pos_bias": a["attn_a_pos_bias"],
        "se_t": a["attn_a_scale_embed"].T, "gain": a["attn_a_if_gain"],
        "wqkv_b": wqkv_b, "wrot": wqkv_b[:, turned], "wo_b": a["attn_b_Wo"],
        "W1": a["ffn_W1"], "W2T": a["ffn_W2"].transpose(0, 2, 1), "b1": a["ffn_b1"].reshape(NG, INTER // P, P).transpose(0, 2, 1), "b2": a["ffn_b2"],
        **constants(),
    }
    arrays = {n: np.ascontiguousarray(v) for n, v in arrays.items()}
    nc = bacc.Bacc("TRN2", target_bir_lowering=False, num_devices=1)
    I = {n: nc.dram_tensor("in_" + n, v.shape, mybir.dt.from_np(v.dtype), kind="ExternalInput").ap()
         for n, v in arrays.items()}
    out = nc.dram_tensor("out_T", (C, tokens), F32, kind="ExternalOutput").ap()
    build(nc, I, out)
    r = run_bass_kernel_spmd(nc, [{"in_" + n: v for n, v in arrays.items()}], core_ids=[0])
    return r.results[0]["out_T"].T.reshape(BATCH, T, C)
```

```python
from contextlib import ExitStack

import numpy as np
import concourse.bass as bass
from concourse import mybir

F32 = mybir.dt.float32
BF16 = mybir.dt.bfloat16
ALU = mybir.AluOpType
ACT = mybir.ActivationFunctionType
AX_X = mybir.AxisListType.X

P = 128
BATCH, T, C = 2, 2048, 256
H, HD = 16, 16
KC = C // P
CH = 512
NCH = T // CH
TILES = CH // P
OFFSETS = list(range(41)) + [128, 96, 384]
J = len(OFFSETS)
NEAR = 41
PAD = 384
GRP, HG = 4, H // 4
SLOT = 32
INTER = 1024
NG = 8
EPS = 1e-5
PARTS = 3
BANK_J = 16
BANKS = [min(BANK_J, J - BANK_J * k) for k in range((J + BANK_J - 1) // BANK_J)]
EBW = 3 * P - 1
Q_STACK = [0, 0, 0, 1, 1, 2]
K_STACK = [0, 1, 2, 0, 1, 0]
KROWS = 6 * HD


PRODUCTS = [(c, bank, r, g) for c in range(KC) for bank in range(len(BANKS)) for r in range(4)
            for g in range(BANKS[bank] // 4)]
POOL_SHARE = 36
ON_POOL = [(k * POOL_SHARE) % len(PRODUCTS) < POOL_SHARE for k in range(len(PRODUCTS))]
N_DVE, N_POOL = ON_POOL.count(False), ON_POOL.count(True)
RING = 8
SUMMED = []
for _unit in range(KC * len(BANKS)):
    _n = sum(1 for c, bank, _, _ in PRODUCTS if c * len(BANKS) + bank <= _unit)
    SUMMED.append((ON_POOL[:_n].count(False), ON_POOL[:_n].count(True)))

END = len(PRODUCTS)
PE_TAIL = [(0, "y", 0), (1, "y", 1), (2, "y", 2), (3, "y", 3), (4, "y", 4), (5, "y", 5), (6, "y", 6),
           (7, "y", 7), (19, "mean", 0), (26, "var", 0), (28, "back", 0), (33, "ffn", 0), (35, "ffn", 1),
           (37, "ffn", 2), (39, "ffn", 3), (44, "mean", 1), (50, "var", 1), (54, "back", 1), (57, "qk", 0),
           (59, "qk", 1), (61, "qk", 2), (63, "qk", 3), (66, "qk", 4), (68, "qk", 5), (70, "qk", 6),
           (72, "qk", 7), (75, "qk", 8), (77, "qk", 9), (79, "qk", 10), (81, "qk", 11), (END, "qk", 12),
           (END, "qk", 13), (END, "qk", 14), (END, "qk", 15), (END, "v", 0), (END, "v", 1), (END, "v", 2),
           (END, "v", 3)]
DVE_TAIL = [(17, "add", 0), (24, "center", 0), (29, "inverse", 0), (33, "normalise", 0), (43, "update", 0),
            (48, "center", 1), (54, "inverse", 1), (56, "normalise", 1), (74, "rope", 0), (80, "rope", 1),
            (87, "rope", 2), (END, "rope", 3)]
ACT_TAIL = [(16, "scores", 0), (26, "square", 0), (28, "root", 0), (32, "scores", 1), (44, "scores", 2),
            (51, "square", 1), (53, "root", 1), (60, "scores", 3), (75, "cast", 0), (76, "scores", 4),
            (81, "store", 0), (83, "cast", 1), (87, "scores", 5), (87, "store", 1), (87, "cast", 2)]


def steps_at(table, m):
    return [(step, i) for pos, step, i in table if pos == m]


def fold_ffn(nc, W1, W2T, b1, b2, mt_d, bc_d):
    OC = INTER // P
    with ExitStack() as ctx:
        sb = lambda n, s, d: ctx.enter_context(nc.sbuf_tensor(n, s, d))
        sem = lambda n: ctx.enter_context(nc.semaphore(n))
        w1 = sb("w1", [P, 2, OC, C], F32)
        w2 = sb("w2", [P, 2, OC, C], F32)
        b1s = sb("b1s", [P, 2, OC], F32)
        b2s = sb("b2s", [1, 2, C], F32)
        mt = sb("mt", [P, 2, KC, C], F32)
        bc = sb("bc", [1, 2, C], F32)
        acc = sb("acc", [P, 2, C], F32)
        column = sb("column", [P, 1], F32)
        ps = ctx.enter_context(nc.psum_tensor("fold_ps", [P, 2, 4, CH], F32))
        loaded = [sem("fold_loaded0"), sem("fold_loaded1")]
        mm_done, evac, stored = sem("fold_mm"), sem("fold_evac"), sem("fold_stored")
        start, weighted, acc_step = sem("fold_start"), sem("fold_weighted"), sem("fold_acc_step")
        block = ctx.enter_context(nc.Block())

        @block.sync
        def _(sp):
            with sp.Fori(0, NG // 2) as i:
                for s in range(2):
                    g = i * 2 + s
                    sp.wait_ge(evac, i * 2 + s + 1)
                    sp.dma_start(w1[:, s], W1[g].rearrange("(k p) n -> p k n", p=P)).then_inc(loaded[s], 16)
                    sp.dma_start(w2[:, s], W2T[g].rearrange("(k p) n -> p k n", p=P)).then_inc(loaded[s], 16)
                    sp.dma_start(b1s[:, s], b1[g]).then_inc(loaded[s], 16)
                    sp.dma_start(b2s[:, s], b2[g].unsqueeze(0)).then_inc(loaded[s], 16)

        @block.tensor
        def _(pe):
            pe.wait_ge(start, 1)
            pe.sem_inc(mm_done, 2)
            with pe.Fori(0, NG // 2) as i:
                for s in range(2):
                    pe.wait_ge(loaded[s], i * 64 + 64)
                    pe.wait_ge(evac, i * 2 + s + 1)
                    for m in range(KC):
                        for k in range(OC):
                            pe.matmul(ps[:, s, m, 0:C], w1[:, s, k, m * P:(m + 1) * P], w2[:, s, k, :],
                                      start=(k == 0), stop=(k == OC - 1))
                    pe.wait_ge(weighted, i * 2 + s + 1)
                    pe.matmul(ps[0:1, s, 2, 0:C], column[:, :], acc[:, s, :], start=True, stop=True).then_inc(mm_done, 1)

        @block.vector
        def _(dve):
            dve.memset(column[:, :], 1.0).then_inc(start, 1)
            dve.sem_inc(evac, 2)
            dve.sem_inc(stored, 64)
            with dve.Fori(0, NG // 2) as i:
                for s in range(2):
                    dve.wait_ge(loaded[s], i * 64 + 64)
                    for k in range(OC):
                        if k == 0:
                            step = dve.tensor_scalar(acc[:, s, :], w2[:, s, k, :], b1s[:, s, k:k + 1], None, ALU.mult)
                        else:
                            step = dve.scalar_tensor_tensor(out=acc[:, s, :], in0=w2[:, s, k, :], scalar=b1s[:, s, k:k + 1],
                                                            in1=acc[:, s, :], op0=ALU.mult, op1=ALU.add)
                        if k < OC - 1:
                            step.then_inc(acc_step, 1)
                            dve.wait_ge(acc_step, (i * 2 + s) * (OC - 1) + (k + 1))
                    step.then_inc(weighted, 1)
                    dve.wait_ge(mm_done, i * 2 + s + 3)
                    dve.wait_ge(stored, i * 64 + 64)
                    dve.tensor_copy(mt[:, s], ps[:, s, 0:KC, 0:C])
                    dve.tensor_tensor(bc[:, s], ps[0:1, s, 2, 0:C], b2s[:, s], ALU.add).then_inc(evac, 1)

        @block.scalar
        def _(act):
            with act.Fori(0, NG // 2) as i:
                for s in range(2):
                    g = i * 2 + s
                    act.wait_ge(evac, i * 2 + s + 3)
                    act.dma_start(mt_d[g + 1].rearrange("(k p) n -> p k n", p=P), mt[:, s]).then_inc(stored, 16)
                    act.dma_start(bc_d[g + 1].unsqueeze(0), bc[:, s]).then_inc(stored, 16)
            act.dma_start(mt_d[0].rearrange("(k p) n -> p k n", p=P), mt[:, 1]).then_inc(stored, 16)
            act.dma_start(bc_d[0].unsqueeze(0), bc[:, 1]).then_inc(stored, 16)
            act.wait_ge(stored, 64 + 32 * NG + 32)


class LayerNorm:

    def __init__(self, sb, sem, PS, ones, spread, eps):
        self.PS, self.ones, self.spread, self.eps = PS, ones, spread, eps
        self.xm = sb("xm", [P, KC, CH], F32)
        self.sq = sb("sq", [P, KC, CH], F32)
        self.sd = sb("sd", [P, P], F32)
        self.rs = sb("rs", [P, P], F32)
        self.xn = sb("xn", [P, KC, CH], F32)
        (self.mean_ps, self.centered, self.squared, self.var_ps, self.sd_ready, self.rs_ready, self.rs_ps,
         self.xn_ready) = (sem(n) for n in ("mean_ps", "centered", "squared", "var_ps", "sd_ready", "rs_ready",
                                            "rs_ps", "xn_ready"))

    def wide(self, bank):
        return self.PS[:, bank, :].unsqueeze(1).broadcast_to([P, KC, CH])

    def mean(self, pe, banks, x):
        for k in range(KC):
            mm = pe.matmul(self.PS[:, banks[0], :], self.ones[:, :], x[:, k, :], start=(k == 0), stop=(k == KC - 1))
        mm.then_inc(self.mean_ps, 1)

    def center(self, dve, n, banks, x):
        dve.wait_ge(self.mean_ps, n)
        dve.tensor_tensor(self.xm[:, :, :], x[:, :, :], self.wide(banks[0]), ALU.subtract).then_inc(self.centered, 1)

    def square(self, act, n):
        act.wait_ge(self.centered, n)
        act.activation(self.sq[:, :, :], self.xm[:, :, :], ACT.Square).then_inc(self.squared, 1)

    def var(self, pe, n, banks):
        pe.wait_ge(self.squared, n)
        for k in range(KC):
            for q in range(TILES):
                mm = pe.matmul(self.PS[SLOT * q:SLOT * (q + 1), banks[1], 0:P], self.ones[:, 0:SLOT],
                               self.sq[:, k, q * P:(q + 1) * P], start=(k == 0), stop=(k == KC - 1))
        mm.then_inc(self.var_ps, 1)

    def root(self, act, n, banks):
        act.wait_ge(self.var_ps, n)
        act.activation(self.sd[:, :], self.PS[:, banks[1], 0:P], ACT.Sqrt, bias=self.eps[:, 0:1]).then_inc(self.sd_ready, 1)

    def inverse(self, dve, n):
        dve.wait_ge(self.sd_ready, n)
        dve.reciprocal(self.rs[:, :], self.sd[:, :]).then_inc(self.rs_ready, 1)

    def back(self, pe, n, banks):
        pe.wait_ge(self.rs_ready, n)
        for q in range(TILES):
            mm = pe.matmul(self.PS[:, banks[0], q * P:(q + 1) * P], self.spread[:, q, :], self.rs[:, :],
                           start=True, stop=True)
        mm.then_inc(self.rs_ps, 1)

    def normalise(self, dve, n, banks):
        dve.wait_ge(self.rs_ps, n)
        dve.tensor_tensor(self.xn[:, :, :], self.xm[:, :, :], self.wide(banks[0]), ALU.mult).then_inc(self.xn_ready, 1)


def local_stage(nc, I, D):
    with ExitStack() as ctx:
        sb = lambda n, s, d: ctx.enter_context(nc.sbuf_tensor(n, s, d))
        sem = lambda n: ctx.enter_context(nc.semaphore(n))
        PS = ctx.enter_context(nc.psum_tensor("PSa", [P, 8, CH], F32))
        TP = PS[:, 3, :].bitcast(BF16).rearrange("p (h t) -> p h t", h=8)

        ones = sb("ones", [P, P], F32)
        spread = sb("spread", [P, TILES, P], F32)
        eps = sb("eps", [P, 1], F32)
        ident = sb("ident", [P, P], F32)
        identb = sb("identb", [P, P], BF16)
        band = sb("band", [PARTS * NEAR, EBW], BF16)
        wqkv = sb("wqkv", [P, KC, 3 * C], F32)
        wo = sb("wo", [P, HG, C], F32)
        wqkv_b = sb("wqkv_b", [P, KC, 3 * C], F32)
        wrot = sb("wrot", [P, KC, 2 * C], F32)
        hmask = sb("hmask", [P, 8], F32)
        se_t = sb("se_t", [P, J], F32)
        se_w = sb("se_w", [P, J], F32)
        sj = sb("sj", [P, J, SLOT], F32)
        pbias = sb("pbias", [P, KC, J, 8], F32)
        vmask = sb("vmask", [P, T // P, J], F32)
        bias = sb("bias", [P, KC, J, 8], F32)
        gain = sb("gain", [P, H], F32)
        xh = sb("xh", [P, KC, CH], F32)
        xc = sb("xc", [P, KC, CH], F32)
        cosc = sb("cosc", [P, CH], F32)
        sinc = sb("sinc", [P, CH], F32)
        mtc = sb("mtc", [P, KC, C], F32)
        bcc = sb("bcc", [P, KC], F32)
        qT = sb("qT", [P, KC, CH], F32)
        kT = sb("kT", [P, KC, PAD + T], F32)
        prod_d = sb("prod_d", [P, RING, CH], F32)
        prod_p = sb("prod_p", [P, RING, CH], F32)
        sc = sb("sc", [P, 2 * len(BANKS), CH], F32)
        lg = sb("lg", [P, KC, J, 8], F32)
        red = sb("red", [P, 4, H], F32)
        attn = sb("attn", [P, H, J], F32)
        rest = sb("rest", [P, H, NEAR], F32)
        parts = sb("parts", [P, H, PARTS, NEAR], BF16)
        parts_t = sb("parts_t", [PARTS * NEAR, H, P], BF16)
        a0 = sb("a0", [P, H, P], F32)
        a1 = sb("a1", [P, H, NEAR - 1], F32)
        vnew = sb("vnew", [P, TILES, H, HD], F32)
        v7 = sb("v7", [P, TILES + 3, H, HD], F32)
        v96 = sb("v96", [P, TILES, H, HD], F32)
        far = sb("far", [P, 2, H, HD], F32)
        fart = sb("fart", [P, H, HD], F32)
        oT = sb("oT", [P, HG, CH], F32)
        rope_a = sb("rope_a", [P, CH], F32)
        rope_b = sb("rope_b", [P, CH], F32)
        rope_q = sb("rope_q", [P, CH], F32)
        qparts = sb("qparts", [P, 2, PARTS, CH], BF16)
        vb = sb("vb", [P, TILES, H, SLOT], F32)

        first_ld = sem("first_ld")
        const_ld, filled, made = sem("const_ld"), sem("filled"), sem("made")
        pad_stored = sem("pad_stored")
        head_ld, tail_ld, v_stored, v_ld = sem("head_ld"), sem("tail_ld"), sem("v_stored"), sem("v_ld")
        bias_ready, rope_done = sem("bias_ready"), sem("rope_done")
        x_stored, vb_stored = sem("x_stored"), sem("vb_stored")
        qk_ps, qk_sb, v_ps, v_sb = sem("qk_ps"), sem("qk_sb"), sem("v_ps"), sem("v_sb")
        prod_d_ready, prod_d_used = sem("prod_d_ready"), sem("prod_d_used")
        prod_p_ready, prod_p_used = sem("prod_p_ready"), sem("prod_p_used")
        sc_sb, l_ps, lg_ready = sem("sc_sb"), sem("l_ps"), sem("lg_ready")
        lg_shifted, exp_ready, attn_ready = sem("lg_shifted"), sem("exp_ready"), sem("attn_ready")
        part_cast, rest_ready, parts_ready = sem("part_cast"), sem("rest_ready"), sem("parts_ready")
        tp_ps, tp_sb, sp_ps, a_sb = sem("tp_ps"), sem("tp_sb"), sem("sp_ps"), sem("a_sb")
        far_step, far_ready, pv_ps, o_sb = sem("far_step"), sem("far_ready"), sem("pv_ps"), sem("o_sb")
        y_ps, ffn_ps, x_updated, dve_step = sem("y_ps"), sem("ffn_ps"), sem("x_updated"), sem("dve_step")
        qkb_ps, qkb_read, rope_cast, rope_rest, qparts_ready = (
            sem("qkb_ps"), sem("qkb_read"), sem("rope_cast"), sem("rope_rest"), sem("qparts_ready"))
        qparts_stored = [sem("qparts_stored0"), sem("qparts_stored1")]
        vb_ps, vb_sb = sem("vb_ps"), sem("vb_sb")

        ln = LayerNorm(sb, sem, PS, ones, spread, eps)
        xn, xn_ready = ln.xn, ln.xn_ready
        HEAD_BANKS, TAIL_BANKS = (0, 1), (4, 5)
        head_ln = lambda h: h * 3 + 1
        tail_ln = lambda s, l: s * 3 + (l + 2)
        block = ctx.enter_context(nc.Block())
        TAIL_LOADS = 16 * 5
        N_CONST = 10 + 8 + 1

        @block.sync
        def _(sp):
            def const(dst, src):
                sp.dma_start(dst, src).then_inc(const_ld, 16)
            sp.dma_start(xh[:, :, :], I["xT"][:, CH:2 * CH].rearrange("(k p) t -> p k t", p=P)).then_inc(head_ld, 16)
            sp.dma_start(spread[:, :, :], I["spread"]).then_inc(first_ld, 16)
            sp.dma_start(wqkv[:, :, :], I["wqkv"].rearrange("(k p) n -> p k n", p=P)).then_inc(first_ld, 16)
            const(hmask[:, :], I["hmask"])
            const(ident[:, :], I["ident"])
            const(identb[:, :], I["identb"])
            const(band[:, :], I["band"])
            const(wqkv_b[:, :, :], I["wqkv_b"].rearrange("(k p) n -> p k n", p=P))
            const(wrot[:, :, :], I["wrot"].rearrange("(k p) n -> p k n", p=P))
            const(vmask[:, :, :], I["vmask"])
            const(wo[:, :, :], I["wo"].rearrange("g p n -> p g n"))
            const(gain[:, :], I["gain"].partition_broadcast(P))
            for c in range(KC):
                const(pbias[:, c], I["pos_bias"][:, 8 * c:8 * c + 8].partition_broadcast(P))
            sp.wait_ge(filled, 1)
            for h in range(8):
                const(se_t[HD * h:HD * (h + 1), :], I["se_t"])
            sp.wait_ge(filled, 2)
            for b in range(BATCH):
                sp.dma_start(D["v_d"][b, 0:PAD, :].rearrange("(k p) n -> p k n", p=P),
                             vnew[:, 0:3].rearrange("p k h d -> p k (h d)")).then_inc(pad_stored, 16)

            def tail_loads(s):
                cols = bass.ds(s * CH, CH)
                sp.wait_ge(x_stored, s * 16 + 16)
                sp.dma_start(xc[:, :, :], I["xT"][:, cols].rearrange("(k p) t -> p k t", p=P)).then_inc(tail_ld, 16)
                sp.dma_start(cosc[:, :], I["cosT"][:, cols]).then_inc(tail_ld, 16)
                sp.dma_start(sinc[:, :], I["sinT"][:, cols]).then_inc(tail_ld, 16)
                sp.dma_start(mtc[:, :, :], D["mt_d"][s].rearrange("(k p) n -> p k n", p=P)).then_inc(tail_ld, 16)
                sp.dma_start(bcc[:, :], D["bc_d"][s].rearrange("(k p) -> p k", p=P),
                             allow_slow_non_contiguous=True).then_inc(tail_ld, 16)

            def tail_stores(s):
                cols = bass.ds(s * CH, CH)
                sp.wait_ge(x_updated, s * 2 + 2)
                sp.dma_start(D["x_d"][:, cols].rearrange("(k p) t -> p k t", p=P), xc[:, :, :]).then_inc(x_stored, 16)
                sp.wait_ge(vb_sb, s * 2 + 2)
                sp.dma_start(D["vb_d"][cols, :].rearrange("(k p) n -> p k n", p=P),
                             vb[:, :, :, :].rearrange("p k h d -> p k (h d)")).then_inc(vb_stored, 16)

            with sp.Fori(0, BATCH) as b:
                with sp.Fori(0, NCH) as n:
                    it = b * NCH + n
                    sp.wait_ge(v_sb, it * 2 + 2)
                    tail_loads(it)
                    sp.dma_start(D["v_d"][b, bass.ds(n * CH + PAD, CH), :].rearrange("(k p) n -> p k n", p=P),
                                 vnew[:, :, :, :].rearrange("p k h d -> p k (h d)")).then_inc(v_stored, 16)
                    sp.wait_ge(v_stored, it * 16 + 16)
                    sp.dma_start(v7[:, :, :, :].rearrange("p k h d -> p k (h d)"),
                                 D["v_d"][b, bass.ds(n * CH, CH + PAD), :].rearrange("(k p) n -> p k n", p=P)).then_inc(v_ld, 16)
                    sp.dma_start(v96[:, :, :, :].rearrange("p k h d -> p k (h d)"),
                                 D["v_d"][b, bass.ds(n * CH + PAD - 96, CH), :].rearrange("(k p) n -> p k n", p=P)).then_inc(v_ld, 16)
                    sp.wait_ge(ln.centered, head_ln(it))
                    sp.dma_start(xh[:, :, :], I["xT"][:, bass.ds(it * CH + 2 * CH, CH)]
                                 .rearrange("(k p) t -> p k t", p=P)).then_inc(head_ld, 16)
                    tail_stores(it)
            sp.wait_ge(v_sb, NG * 2 + 2)
            tail_loads(NG)
            tail_stores(NG)
            sp.wait_ge(pad_stored, 16 * BATCH)
            sp.wait_ge(x_stored, 16 * (NG + 1) + 16)
            for u in range(2):
                sp.wait_ge(qparts_stored[u], 32 * (NG + 1))
            sp.wait_ge(vb_stored, 16 * (NG + 1))

        @block.gpsimd
        def _(pool):
            pool.memset(ones[:, :], 1.0 / C).then_inc(filled, 1)
            pool.memset(vnew[:, :, :, :], 0.0).then_inc(filled, 1)
            pool.memset(kT[:, :, 0:PAD], 0.0)
            pool.memset(eps[:, :], EPS)
            pool.memset(oT[:, :, :], 0.0)
            pool.memset(sj[:, :, :], 0.0).then_inc(filled, 1)
            pool.memset(vb[:, :, :, :], 0.0).then_inc(filled, 1)
            pool.wait_ge(filled, 4)
            pool.memset(vb[:, :, :, HD:HD + 1], 1.0).then_inc(filled, 1)
            pool.wait_ge(const_ld, 16 * N_CONST)
            pool.tensor_scalar(se_w[:, :], se_t[:, :], HD ** -0.5, HD ** -0.5, ALU.mult, ALU.add).then_inc(made, 1)
            pool.wait_ge(made, 1)
            for r in range(4):
                view = sj[:, :, :].rearrange("p (a r) (s h) -> p a r s h", r=4, s=4)[:, :, r, r, :]
                w = se_w[:, :].rearrange("p (a r) -> p a r", r=4)[:, :, r]
                pool.tensor_tensor(view, w.unsqueeze(2).broadcast_to([P, J // 4, 8]),
                                   hmask[:, :].unsqueeze(1).broadcast_to([P, J // 4, 8]), ALU.mult).then_inc(made, 1)

            def bias_of(t, tile):
                pool.wait_ge(lg_ready, t * 2)
                for c in range(KC):
                    mask = vmask[:, bass.ds(tile, 1), :].rearrange("p a j -> p (a j)").unsqueeze(2).broadcast_to([P, J, 8])
                    pool.tensor_tensor(bias[:, c], pbias[:, c], mask, ALU.add).then_inc(bias_ready, 1)

            with pool.Fori(0, BATCH) as b:
                with pool.Fori(0, NCH) as n:
                    it = b * NCH + n
                    bias_of(it * TILES, n * TILES)
                    pool.wait_ge(qk_sb, it * 4 + 4)
                    k = 0
                    for m, (c, bank, r, g) in enumerate(PRODUCTS):
                        if ON_POOL[m]:
                            if k >= RING:
                                pool.wait_ge(prod_p_used, it * N_POOL + (k - RING + 1))
                            off = OFFSETS[BANK_J * bank + 4 * g + r]
                            pool.tensor_tensor(prod_p[:, k % RING, :], qT[:, c, :],
                                               kT[:, c, bass.ds(n * CH + (PAD - off), CH)], ALU.mult).then_inc(prod_p_ready, 1)
                            k += 1
                    pool.wait_ge(v_ld, it * 32 + 32)
                    for u in range(TILES):
                        t = it * TILES + u
                        if u < TILES - 1:
                            bias_of(t + 1, n * TILES + (u + 1))
                        pool.wait_ge(attn_ready, t + 1)
                        if u >= 2:
                            pool.wait_ge(pv_ps, t - 1)
                        for f, src in enumerate((v7[:, u + 2], v96[:, u], v7[:, u])):
                            w = attn[:, :, NEAR + f:NEAR + f + 1].broadcast_to([P, H, HD])
                            dst = far[:, u % 2, :, :] if f == 0 else fart[:, :, :]
                            pool.tensor_tensor(dst, w, src[:, :, :], ALU.mult).then_inc(far_step, 1)
                            if f:
                                pool.wait_ge(far_step, t * 5 + 2 * f)
                                i = pool.tensor_tensor(far[:, u % 2, :, :], far[:, u % 2, :, :], fart[:, :, :], ALU.add)
                                i.then_inc(far_step, 1)
                                pool.wait_ge(far_step, t * 5 + 2 * f + 1)
                        pool.sem_inc(far_ready, 1)

        @block.tensor
        def _(pe):
            pe.wait_ge(filled, 5)
            pe.wait_ge(first_ld, 32)

            def head_qk(h, u):
                if u == 0:
                    pe.wait_ge(xn_ready, head_ln(h))
                if u >= 2:
                    pe.wait_ge(qk_sb, h * 4 + (u - 1))
                for k in range(KC):
                    mm = pe.matmul(PS[:, u % 2, :], wqkv[:, k, u * P:(u + 1) * P], xn[:, k, :],
                                   start=(k == 0), stop=(k == KC - 1))
                mm.then_inc(qk_ps, 1)

            def head_v(h, s):
                if s % 2 == 0:
                    pe.wait_ge(qk_sb, h * 4 + (3 + s // 2))
                for k in range(KC):
                    mm = pe.matmul(PS[:, s // 2, (s % 2) * C:(s % 2 + 1) * C], xn[:, k, s * P:(s + 1) * P],
                                   wqkv[:, k, 2 * C:3 * C], start=(k == 0), stop=(k == KC - 1))
                mm.then_inc(v_ps, 1)

            def tail(s, step, i):
                if step == "y":
                    if i == 0:
                        pe.wait_ge(o_sb, s * TILES)
                    m, g = i // HG, i % HG
                    mm = pe.matmul(PS[:, 2 + m, :], wo[:, g, m * P:(m + 1) * P], oT[:, g, :],
                                   start=(g == 0), stop=(g == HG - 1))
                    if g == HG - 1:
                        mm.then_inc(y_ps, 1)
                elif step == "mean":
                    pe.wait_ge(x_updated, s * 2 + (1 + i))
                    ln.mean(pe, TAIL_BANKS, xc)
                elif step == "var":
                    ln.var(pe, tail_ln(s, i), TAIL_BANKS)
                elif step == "back":
                    ln.back(pe, tail_ln(s, i), TAIL_BANKS)
                elif step == "ffn":
                    if i == 0:
                        pe.wait_ge(xn_ready, tail_ln(s, 0))
                    m, k = i // KC, i % KC
                    mm = pe.matmul(PS[:, 2 + m, :], mtc[:, k, m * P:(m + 1) * P], xn[:, k, :],
                                   start=(k == 0), stop=(k == KC - 1))
                    if k == KC - 1:
                        mm.then_inc(ffn_ps, 1)
                elif step == "qk":
                    u, half, k = i // 4, i // 2 % 2, i % 2
                    if i == 0:
                        pe.wait_ge(xn_ready, tail_ln(s, 1))
                    if u >= 2 and i % 4 == 0:
                        pe.wait_ge(qkb_read, s * 4 + (u - 1))
                    mm = pe.matmul(PS[:, (2, 4, 2, 0)[u] + half, :], (wqkv_b, wrot)[half][:, k, u * P:(u + 1) * P], xn[:, k, :],
                                   start=(k == 0), stop=(k == KC - 1))
                    if i % 4 == 3:
                        mm.then_inc(qkb_ps, 1)
                else:
                    if i == 2:
                        pe.wait_ge(vb_sb, s * 2 + 1)
                    for k in range(KC):
                        mm = pe.matmul(PS[:, 6, (i % 2) * C:(i % 2 + 1) * C], xn[:, k, i * P:(i + 1) * P],
                                       wqkv_b[:, k, 2 * C:3 * C], start=(k == 0), stop=(k == KC - 1))
                    mm.then_inc(vb_ps, 1)

            def scores_to_tokens(it, u, c):
                if c == 0 and u == 0:
                    pe.wait_ge(sc_sb, it * 6 + 6)
                    pe.wait_ge(qkb_read, it * 4 + 3)
                else:
                    pe.wait_ge(lg_ready, (it * TILES + u) * 2 + c)
                for bank, nj in enumerate(BANKS):
                    mrows = 8 * nj
                    tr = pe.transpose(PS[:, 2, bank * P:bank * P + mrows],
                                      sc[0:mrows, 3 * c + bank, u * P:(u + 1) * P], ident[0:mrows, 0:mrows])
                tr.then_inc(l_ps, 1)

            def weights_to_offsets(t, half):
                if half == 0:
                    pe.wait_ge(parts_ready, t + 1)
                pe.wait_ge(tp_sb, t * 2 + half)
                for h in range(8):
                    tr = pe.transpose(TP[0:PARTS * NEAR, h, :],
                                      parts[:, 8 * half + h].rearrange("p s j -> p (s j)"), identb[:, :])
                tr.then_inc(tp_ps, 1)

            def head(h):
                ln.mean(pe, HEAD_BANKS, xh)
                ln.var(pe, head_ln(h), HEAD_BANKS)
                ln.back(pe, head_ln(h), HEAD_BANKS)
                for u in range(4):
                    head_qk(h, u)
                for s in range(TILES):
                    head_v(h, s)

            pe.wait_ge(head_ld, 16)
            head(0)
            pe.wait_ge(const_ld, 16 * N_CONST)
            pe.wait_ge(made, 5)
            with pe.Fori(0, BATCH) as b:
                with pe.Fori(0, NCH) as n:
                    it = b * NCH + n
                    kd = kp = 0
                    for m, (c, bank, r, g) in enumerate(PRODUCTS):
                        unit = c * len(BANKS) + bank
                        if r == 0 and g == 0:
                            if unit >= 2:
                                pe.wait_ge(sc_sb, it * 6 + (unit - 1))
                            else:
                                pe.wait_ge(v_sb, it * 2 + (unit + 1))
                        if ON_POOL[m]:
                            pe.wait_ge(prod_p_ready, it * N_POOL + (kp + 1))
                            rhs, used = prod_p[:, kp % RING, :], prod_p_used
                            kp += 1
                        else:
                            pe.wait_ge(prod_d_ready, it * N_DVE + (kd + 1))
                            rhs, used = prod_d[:, kd % RING, :], prod_d_used
                            kd += 1
                        j = BANK_J * bank + 4 * g + r
                        pe.matmul(PS[SLOT * g:SLOT * (g + 1), unit % 2, :], sj[:, j, :], rhs,
                                  start=(r == 0), stop=(r == 3)).then_inc(used, 1)
                        for step, i in steps_at(PE_TAIL, m):
                            tail(it, step, i)
                    for c in range(KC):
                        scores_to_tokens(it, 0, c)
                    for step, i in steps_at(PE_TAIL, END):
                        tail(it, step, i)
                    for u in range(TILES):
                        t = it * TILES + u
                        for half in range(2):
                            weights_to_offsets(t, half)
                            if u < TILES - 1:
                                scores_to_tokens(it, u + 1, half)
                        if u == TILES - 1:
                            ln.back(pe, head_ln(it + 1), HEAD_BANKS)
                        pe.wait_ge(tp_sb, t * 2 + 2)
                        for q in range(6):
                            if q >= 3:
                                pe.wait_ge(a_sb, t * 6 + (q - 2))
                            elif u == 0 and q == 2:
                                pe.wait_ge(vb_sb, it * 2 + 2)
                            first = 32 * q if q < 4 else 32 * (q - 4)
                            for tt in range(first, min(first + 32, P if q < 4 else NEAR - 1)):
                                a = (2 * P - 1 - tt) if q < 4 else (P - 1 - tt)
                                mm = pe.matmul(PS[:, 4 + q % 3, (tt - first) * H:(tt - first + 1) * H],
                                               band[:, a:a + P], parts_t[:, :, tt], start=True, stop=True)
                            mm.then_inc(sp_ps, 1)
                        if u == 0:
                            pe.wait_ge(head_ld, it * 16 + 32)
                            pe.wait_ge(qkb_read, it * 4 + 4)
                            ln.mean(pe, HEAD_BANKS, xh)
                        elif u == 1:
                            ln.var(pe, head_ln(it + 1), HEAD_BANKS)
                        elif u == TILES - 1:
                            for i in range(4):
                                head_qk(it + 1, i)
                        pe.wait_ge(a_sb, t * 6 + 6)
                        if u == 0:
                            pe.wait_ge(v_ld, it * 32 + 32)
                        pe.wait_ge(far_ready, t + 1)
                        pe.wait_ge(o_sb, t)
                        for g in range(HG):
                            for step in range(3):
                                for jh in range(GRP):
                                    h = GRP * g + jh
                                    out = PS[SLOT * jh:SLOT * jh + HD, 7, g * P:(g + 1) * P]
                                    if step == 0:
                                        pe.matmul(out, v7[:, u + 3, h, :], a0[:, h, :], start=True, stop=False)
                                    elif step == 1:
                                        pe.matmul(out[:, 0:NEAR - 1], v7[:, u + 2, h, :], a1[:, h, :], start=False, stop=False)
                                    else:
                                        mm = pe.matmul(out, far[:, u % 2, h, :], ident[:, :], start=False, stop=True)
                        mm.then_inc(pv_ps, 1)
                        if u == TILES - 1:
                            for s in range(TILES):
                                head_v(it + 1, s)
            for m in range(END + 1):
                for step, i in steps_at(PE_TAIL, m):
                    tail(NG, step, i)

        @block.scalar
        def _(act):
            act.wait_ge(filled, 5)
            QKD = [D["q_d"], D["k_d"]]

            def head_out(h, col, u):
                act.wait_ge(qk_ps, h * 4 + (u + 1))
                dst = qT[:, u, :] if u < 2 else kT[:, u - 2, bass.ds(col, CH)]
                act.copy(dst, PS[:, u % 2, :]).then_inc(qk_sb, 1)

            def head_v_out(h, s):
                act.wait_ge(v_ps, h * 4 + (2 * s + 2))
                act.copy(vnew[:, 2 * s:2 * s + 2, :, :],
                         PS[:, s, :].rearrange("p (s h d) -> p s h d", s=2, d=HD)).then_inc(v_sb, 1)

            def scores_out(it, unit):
                act.wait_ge(prod_d_used, it * N_DVE + SUMMED[unit][0])
                act.wait_ge(prod_p_used, it * N_POOL + SUMMED[unit][1])
                rows = 8 * BANKS[unit % 3]
                act.copy(sc[0:rows, unit, :], PS[0:rows, unit % 2, :]).then_inc(sc_sb, 1)

            def cast_part(s, i, part):
                act.wait_ge(rope_rest, s * 8 + (2 * i + 1 + part))
                act.copy(qparts[:, i % 2, part, :], (rope_q, rope_a)[part][:, :]).then_inc(rope_cast, 1)

            def tail(s, step, i):
                if step == "square":
                    ln.square(act, tail_ln(s, i))
                elif step == "root":
                    ln.root(act, tail_ln(s, i), TAIL_BANKS)
                elif step == "cast":
                    for part in range(2):
                        cast_part(s, i, part)
                elif step == "store":
                    act.wait_ge(qparts_ready, s * 4 + i + 1)
                    dst = QKD[i // 2][:, (i % 2) * P:(i % 2 + 1) * P, bass.ds(s * CH, CH)]
                    act.dma_start(dst.rearrange("s p t -> p s t"), qparts[:, i % 2, :, :]).then_inc(qparts_stored[i % 2], 16)

            def values_out(s, i):
                act.wait_ge(vb_stored, s * 16)
                act.wait_ge(vb_ps, s * 4 + (2 * i + 2))
                act.copy(vb[:, 2 * i:2 * i + 2, :, 0:HD],
                         PS[:, 6, :].rearrange("p (s h d) -> p s h d", s=2, d=HD)).then_inc(vb_sb, 1)

            def exponentials(t):
                act.wait_ge(lg_shifted, t + 1)
                act.wait_ge(far_ready, t)
                for c in range(KC):
                    e = act.activation(attn[:, 8 * c:8 * c + 8, :], lg[:, c].rearrange("p j h -> p h j"), ACT.Exp)
                e.then_inc(exp_ready, 1)

            def casts(t):
                act.wait_ge(attn_ready, t + 1)
                act.wait_ge(tp_ps, t * 2)
                act.copy(parts[:, :, 0, :], attn[:, :, 0:NEAR]).then_inc(part_cast, 1)
                act.wait_ge(rest_ready, t + 1)
                act.copy(parts[:, :, 1, :], rest[:, :, :]).then_inc(part_cast, 1)

            def band_out(t, q):
                act.wait_ge(sp_ps, t * 6 + (q + 1))
                nt = 32 if q < 5 else NEAR - 1 - 32
                dst = a0[:, :, 32 * q:32 * q + 32] if q < 4 else a1[:, :, 32 * (q - 4):32 * (q - 4) + nt]
                act.copy(dst, PS[:, 4 + q % 3, 0:nt * H].rearrange("p (t h) -> p h t", h=H)).then_inc(a_sb, 1)

            ln.square(act, 1)
            ln.root(act, 1, HEAD_BANKS)
            for u in range(4):
                head_out(0, PAD, u)
            act.wait_ge(pad_stored, 16 * BATCH)
            for s in range(2):
                head_v_out(0, s)
            with act.Fori(0, BATCH) as b:
                with act.Fori(0, NCH) as n:
                    it = b * NCH + n
                    next_col = act.snap(((n + 1) & (NCH - 1)) * CH + PAD)
                    for m in range(END):
                        for step, i in steps_at(ACT_TAIL, m):
                            if step == "scores":
                                scores_out(it, i)
                            else:
                                tail(it, step, i)
                    exponentials(it * TILES)
                    values_out(it, 0)
                    casts(it * TILES)
                    tail(it, "store", 2)
                    values_out(it, 1)
                    for u in range(TILES):
                        t = it * TILES + u
                        for q in range(6):
                            band_out(t, q)
                            if q == 1 and u < TILES - 1:
                                exponentials(t + 1)
                        if u < TILES - 1:
                            casts(t + 1)
                        if u < 2:
                            cast_part(it, 3, u)
                        elif u == 2:
                            tail(it, "store", 3)
                        if u == 0:
                            ln.square(act, head_ln(it + 1))
                        elif u == TILES - 2:
                            ln.root(act, head_ln(it + 1), HEAD_BANKS)
                        elif u == TILES - 1:
                            for i in range(4):
                                head_out(it + 1, next_col, i)
                        act.wait_ge(pv_ps, t + 1)
                        act.wait_ge(y_ps, it * 2 + 2)
                        act.copy(oT[:, :, u * P:(u + 1) * P],
                                 PS[:, 7, :].rearrange("p (g t) -> p g t", g=HG)).then_inc(o_sb, 1)
                    act.wait_ge(v_stored, it * 16 + 16)
                    for s in range(2):
                        head_v_out(it + 1, s)
            for m in range(END):
                for step, i in steps_at(ACT_TAIL, m):
                    tail(NG, step, i)
            tail(NG, "store", 2)
            values_out(NG, 0)
            tail(NG, "cast", 3)
            values_out(NG, 1)
            tail(NG, "store", 3)

        STEPS = TILES * 4

        @block.vector
        def _(dve):
            dve.wait_ge(filled, 5)

            def normalise_head(h):
                if not (isinstance(h, int) and h == 0):
                    dve.wait_ge(vb_ps, h * 4)
                ln.normalise(dve, head_ln(h), HEAD_BANKS)

            def tail(s, step, i):
                if step == "add":
                    dve.wait_ge(tail_ld, s * TAIL_LOADS + TAIL_LOADS)
                    dve.wait_ge(y_ps, s * 2 + 2)
                    dve.tensor_tensor(xc[:, :, :], xc[:, :, :], PS[:, 2:2 + KC, :], ALU.add).then_inc(x_updated, 1)
                elif step == "center":
                    ln.center(dve, tail_ln(s, i), TAIL_BANKS, xc)
                elif step == "inverse":
                    ln.inverse(dve, tail_ln(s, i))
                elif step == "normalise":
                    if i == 0:
                        dve.wait_ge(v_ps, s * 4 + 4)
                    ln.normalise(dve, tail_ln(s, i), TAIL_BANKS)
                elif step == "update":
                    dve.wait_ge(ffn_ps, s * 2 + 2)
                    for m in range(KC):
                        last = dve.scalar_tensor_tensor(out=xc[:, m, :], in0=PS[:, 2 + m, :], scalar=bcc[:, m:m + 1],
                                                        in1=xc[:, m, :], op0=ALU.add, op1=ALU.add)
                    last.then_inc(x_updated, 1)
                else:
                    for _ in rotation(s, i):
                        pass

            def rotation(s, i):
                bank = (2, 4, 2, 0)[i]
                dve.wait_ge(qkb_ps, s * 4 + (i + 1))
                dve.wait_ge(qparts_ready, s * 4 + i)
                dve.tensor_tensor(rope_a[:, :], PS[:, bank, :], cosc[:, :], ALU.mult)
                dve.tensor_tensor(rope_b[:, :], PS[:, bank + 1, :], sinc[:, :], ALU.mult).then_inc(qkb_read, 1)
                dve.wait_ge(qkb_read, s * 4 + (i + 1))
                dve.tensor_tensor(rope_q[:, :], rope_a[:, :], rope_b[:, :], ALU.add).then_inc(rope_done, 1)
                dve.wait_ge(rope_done, s * 4 + (i + 1))
                dve.wait_ge(qparts_stored[i % 2], s * 32 + 16 * (i // 2))
                dve.sem_inc(rope_rest, 1)
                yield
                dve.wait_ge(rope_cast, s * 8 + (2 * i + 1))
                dve.tensor_tensor(rope_a[:, :], rope_q[:, :], qparts[:, i % 2, 0, :], ALU.subtract).then_inc(rope_rest, 1)
                yield
                dve.wait_ge(rope_cast, s * 8 + (2 * i + 2))
                dve.tensor_tensor(qparts[:, i % 2, 2, :], rope_a[:, :], qparts[:, i % 2, 1, :], ALU.subtract).then_inc(qparts_ready, 1)

            def add_bias(t, c):
                dve.wait_ge(l_ps, t * 2 + (c + 1))
                dve.wait_ge(bias_ready, t * 2 + (c + 1))
                dve.tensor_tensor(lg[:, c].rearrange("p j h -> p (j h)"), PS[:, 2, 0:8 * J],
                                  bias[:, c].rearrange("p j h -> p (j h)"), ALU.add).then_inc(lg_ready, 1)

            def softmax(t, then, meanwhile=iter(())):
                dve.wait_ge(lg_ready, t * 2 + 2)
                for c in range(KC):
                    i = dve.tensor_reduce(red[:, 0, 8 * c:8 * c + 8], lg[:, c].rearrange("p j h -> p h j"), AX_X, ALU.max)
                then(i)
                for c in range(KC):
                    i = dve.tensor_tensor(lg[:, c], lg[:, c],
                                          red[:, 0, 8 * c:8 * c + 8].unsqueeze(1).broadcast_to([P, J, 8]), ALU.subtract)
                i.then_inc(lg_shifted, 1)
                next(meanwhile, None)
                dve.wait_ge(exp_ready, t + 1)
                then(dve.tensor_reduce(red[:, 1, :], attn[:, :, :], AX_X, ALU.add))
                then(dve.reciprocal(red[:, 2, :], red[:, 1, :]))
                then(dve.tensor_tensor(red[:, 3, :], red[:, 2, :], gain[:, :], ALU.mult))
                i = dve.tensor_tensor(attn[:, :, :], attn[:, :, :], red[:, 3, :].unsqueeze(2).broadcast_to([P, H, J]), ALU.mult)
                i.then_inc(attn_ready, 1)
                dve.wait_ge(part_cast, t * 2 + 1)
                i = dve.tensor_tensor(rest[:, :, :], attn[:, :, 0:NEAR], parts[:, :, 0, :], ALU.subtract)
                i.then_inc(rest_ready, 1)
                dve.wait_ge(part_cast, t * 2 + 2)
                i = dve.tensor_tensor(parts[:, :, 2, :], rest[:, :, :], parts[:, :, 1, :], ALU.subtract)
                i.then_inc(parts_ready, 1)
                dve.wait_ge(parts_ready, t + 1)

            dve.sem_inc(x_stored, 16)
            dve.memset(PS[:, 7, :], 0.0)
            dve.wait_ge(head_ld, 16)
            ln.center(dve, 1, HEAD_BANKS, xh)
            ln.inverse(dve, 1)
            normalise_head(0)
            dve.wait_ge(const_ld, 16 * N_CONST)
            with dve.Fori(0, BATCH) as b:
                with dve.Fori(0, NCH) as n:
                    it = b * NCH + n
                    count = [0]

                    def then(ins):
                        count[0] += 1
                        ins.then_inc(dve_step, 1)
                        dve.wait_ge(dve_step, it * STEPS + count[0])

                    dve.wait_ge(qk_sb, it * 4 + 4)
                    k = 0
                    for m, (c, bank, r, g) in enumerate(PRODUCTS):
                        if not ON_POOL[m]:
                            if k >= RING:
                                dve.wait_ge(prod_d_used, it * N_DVE + (k - RING + 1))
                            off = OFFSETS[BANK_J * bank + 4 * g + r]
                            dve.tensor_tensor(prod_d[:, k % RING, :], qT[:, c, :],
                                              kT[:, c, bass.ds(n * CH + (PAD - off), CH)], ALU.mult).then_inc(prod_d_ready, 1)
                            k += 1
                        for step, i in steps_at(DVE_TAIL, m):
                            tail(it, step, i)
                    for c in range(KC):
                        add_bias(it * TILES, c)
                    softmax(it * TILES, then)
                    last_rotation = rotation(it, 3)
                    for u in range(TILES):
                        t = it * TILES + u
                        for half in range(2):
                            dve.wait_ge(tp_ps, t * 2 + (half + 1))
                            dve.wait_ge(sp_ps, t * 6)
                            dve.tensor_copy(parts_t[:, 8 * half:8 * half + 8, :], TP[0:PARTS * NEAR]).then_inc(tp_sb, 1)
                            if u < TILES - 1:
                                add_bias(t + 1, half)
                        if u < TILES - 1:
                            softmax(t + 1, then, last_rotation)
                        if u == 0:
                            ln.center(dve, head_ln(it + 1), HEAD_BANKS, xh)
                        elif u == TILES - 2:
                            ln.inverse(dve, head_ln(it + 1))
                        elif u == TILES - 1:
                            normalise_head(it + 1)
                    assert count[0] == STEPS, count
            for m in range(END + 1):
                for step, i in steps_at(DVE_TAIL, m):
                    tail(NG, step, i)


def full_attention(nc, D):
    KT = T // P
    NGROUP = BATCH * HG
    ITERS = NGROUP * NCH
    MAXU = GRP * TILES * NCH
    PER_STEP = MAXU // KT
    AHEAD = 4
    CARRY = AHEAD * PER_STEP
    QK_LOADS = 16 * 6 * (1 + NCH)

    LOOP = []
    for kk in range(KT):
        ahead = kk >= KT - AHEAD
        first = (kk - (KT - AHEAD)) * PER_STEP if ahead else CARRY + kk * PER_STEP
        LOOP.append([("max", int(ahead), u) for u in range(first, first + PER_STEP)])
    LOOP[2].append(("sum", 0))
    LOOP[6].append(("sum", 1))
    LOOP[KT - AHEAD + 2].insert(1, ("rows",))
    PLAN = [op for step in LOOP for op in step]
    START = [("max", 0, u) for u in range(CARRY)]
    LAST = [[("sum", 0)] if kk == 2 else [("sum", 1)] if kk == 6 else [] for kk in range(KT)]
    END_PLAN = [("sum", 0), ("sum", 1)] * 2
    assert len(PLAN) % 3 == 1 and len(START) % 3 == 1

    with ExitStack() as ctx:
        sb = lambda n, s, d: ctx.enter_context(nc.sbuf_tensor(n, s, d))
        sem = lambda n: ctx.enter_context(nc.semaphore(n))
        ps_s = ctx.enter_context(nc.psum_tensor("ps_s", [P, 2, 2, CH], F32))
        ps_m = ctx.enter_context(nc.psum_tensor("ps_m", [P, 3, CH], F32))
        ps_o = ctx.enter_context(nc.psum_tensor("ps_o", [P, CH], F32))
        qs = sb("qs", [KROWS + PARTS, HG * NCH, GRP, CH], BF16)
        ks = sb("ks", [KROWS + PARTS, HG, GRP, T], BF16)
        vg = sb("vg", [P, KT, GRP, SLOT], F32)
        pr = sb("pr", [P, 2, GRP, CH], F32)
        mx = sb("mx", [P, GRP * TILES, NCH], F32)
        nm = sb("nm", [P, GRP * TILES], F32)
        nmr = sb("nmr", [P, GRP * TILES], F32)
        nmp = sb("nmp", [P, P // 16, GRP * TILES], BF16)
        nmt = sb("nmt", [PARTS * GRP * TILES, P], BF16)
        identb = sb("identb2", [P, P], BF16)
        sel = sb("sel", [P, SLOT], F32)
        spread = sb("spread2", [P, TILES, P], F32)
        ou = sb("ou", [P, CH], F32)
        orc = sb("orc", [P, P], F32)
        on = sb("on", [P, CH], F32)
        k0_ld, q0_ld = sem("c_k0_ld"), sem("c_q0_ld")
        (const_ld, filled, qk_ld, qk_ready, va_ld, vb_ld, vc_ld, s_ps, p_ready, pv_done, m_ps, m_read, nm_step,
         nmp_ready, nmt_sb, neg_ld, o_sb, orc_ready, on_ready, o_stored) = (sem("c_" + n) for n in (
             "const_ld", "filled", "qk_ld", "qk_ready", "va_ld", "vb_ld", "vc_ld", "s_ps", "p_ready", "pv_done", "m_ps",
             "m_read", "nm_step", "nmp_ready", "nmt_sb", "neg_ld", "o_sb", "orc_ready", "on_ready",
             "o_stored"))
        block = ctx.enter_context(nc.Block())

        def taken(x):
            return x * len(PLAN) + len(START)

        def maxima(x):
            return x * MAXU + CARRY

        def unit_place(u):
            return u // (TILES * NCH), u // NCH % TILES, u % NCH

        def first_k(eng, stack):
            for i in stack:
                eng.dma_start(ks[HD * i:HD * (i + 1), 0, :, :],
                              D["k_d"][K_STACK[i], 0:GRP * HD, CH:CH + T].rearrange("(j d) t -> d j t", d=HD)).then_inc(k0_ld, 16)

        def first_q(eng, chunks, loaded):
            for n in chunks:
                for i in range(6):
                    eng.dma_start(qs[HD * i:HD * (i + 1), n, :, :],
                                  D["q_d"][Q_STACK[i], 0:GRP * HD, (1 + n) * CH:(2 + n) * CH]
                                  .rearrange("(j d) t -> d j t", d=HD)).then_inc(loaded, 16)

        @block.sync
        def _(sp):
            first_k(sp, range(3))
            sp.dma_start(identb[:, :], D["identb"]).then_inc(const_ld, 16)
            sp.dma_start(sel[:, :], D["sel"]).then_inc(const_ld, 16)
            sp.dma_start(spread[:, :, :], D["spread"]).then_inc(const_ld, 16)
            first_q(sp, range(1, NCH), q0_ld)
            sp.dma_start(ks[KROWS:KROWS + PARTS, :, :, :].rearrange("a g j t -> a (g j t)"), D["one_rows"]).then_inc(q0_ld, 16)
            with sp.Fori(0, BATCH) as b:
                with sp.Fori(0, HG * NCH) as q:
                    sp.wait_ge(nmt_sb, b * (HG * NCH) + q + 1)
                    sp.dma_start(qs[KROWS:KROWS + PARTS, bass.ds(q, 1), :, :].rearrange("a n j t -> a (n j t)"),
                                 nmt[:, :]).then_inc(neg_ld, 16)

        @block.gpsimd
        def _(pool):
            pool.memset(ou[:, :], 1.0).then_inc(filled, 1)
            pool.memset(pr[:, 1, :, :], 1.0).then_inc(filled, 1)
            pool.memset(nmp[:, :, :], 0.0).then_inc(filled, 1)
            pool.wait_ge(filled, 3)

            def load_qk(b, g, G):
                rows = bass.ds(g * (GRP * HD), GRP * HD)
                for i in range(6):
                    r = slice(HD * i, HD * (i + 1))
                    pool.dma_start(ks[r, bass.ds(g, 1), :, :].rearrange("p a j t -> p (a j) t"),
                                   D["k_d"][K_STACK[i], rows, bass.ds(b * T + CH, T)].rearrange("(j d) t -> d j t", d=HD)).then_inc(qk_ld, 16)
                    for n in range(NCH):
                        pool.dma_start(qs[r, bass.ds(g * NCH + n, 1), :, :].rearrange("p a j t -> p (a j) t"),
                                       D["q_d"][Q_STACK[i], rows, bass.ds(b * T + (1 + n) * CH, CH)].rearrange("(j d) t -> d j t", d=HD)
                                       ).then_inc(qk_ld, 16)
                pool.wait_ge(qk_ld, G * QK_LOADS)
                pool.sem_inc(qk_ready, 1)

            def load_v(b, g, first, last, loaded):
                pool.dma_start(vg[:, first:last, :, :].rearrange("p k j d -> p k (j d)"),
                               D["vb_d"][bass.ds(b * T + (CH + first * P), (last - first) * P), bass.ds(g * (GRP * SLOT), GRP * SLOT)]
                               .rearrange("(k p) n -> p k n", p=P)).then_inc(loaded, 16)

            def outs(x):
                pool.wait_ge(on_ready, x + 1)
                pool.dma_start(D["o_d"][x], on[:, :]).then_inc(o_stored, 16)

            def group(G, more_qk, more_v):
                outs(G * NCH + 1)
                if more_qk:
                    n = G + 3
                    load_qk(pool.snap(n // HG), pool.snap(n % HG), n)
                for i in range(1, NCH):
                    outs(G * NCH + (i + 1))
                if more_v:
                    n = G + 1
                    b, g = pool.snap(n // HG), pool.snap(n % HG)
                    for first, last, loaded in ((0, 8, va_ld), (8, KT - 1, vb_ld), (KT - 1, KT, vc_ld)):
                        pool.wait_ge(pv_done, G * (NCH * KT) + ((NCH - 1) * KT + (last - 1) + 3))
                        load_v(b, g, first, last, loaded)

            for first, last, loaded in ((0, 8, va_ld), (8, KT - 1, vb_ld), (KT - 1, KT, vc_ld)):
                load_v(0, 0, first, last, loaded)
            outs(0)
            for g in range(1, 4):
                load_qk(0, g, g)
            with pool.Fori(0, 1) as G:
                group(G, False, True)
            with pool.Fori(1, NGROUP - 3) as G:
                group(G, True, True)
            pool.sem_inc(qk_ready, 1)
            with pool.Fori(NGROUP - 3, NGROUP - 1) as G:
                group(G, False, True)
            with pool.Fori(NGROUP - 1, NGROUP) as G:
                group(G, False, False)
            outs(ITERS + 1)
            pool.wait_ge(o_stored, 16 * (ITERS + 2))

        @block.tensor
        def _(pe):
            pe.wait_ge(const_ld, 48)
            pe.wait_ge(filled, 3)
            pe.sem_inc(pv_done, 1)

            def bank_free(x, plan, pos):
                if pos < 3:
                    pe.wait_ge(m_read, maxima(x) - (0, 2, 1)[pos])
                elif plan[pos - 3][0] == "max":
                    pe.wait_ge(m_read, maxima(x) + sum(op[0] == "max" for op in plan[:pos - 2]))
                elif plan[pos - 3] == ("sum", 0):
                    pe.wait_ge(orc_ready, x + 1)
                elif plan[pos - 3] == ("sum", 1):
                    pe.wait_ge(on_ready, x + 1)
                else:
                    pe.wait_ge(nmt_sb, x + 1)

            def max_unit(x, u, pos, nq, nslot):
                j, qt, kc = unit_place(u)
                pe.matmul(ps_m[:, pos % 3, :], qs[0:KROWS, bass.ds(nq, 1), j, qt * P:(qt + 1) * P].rearrange("p a t -> p (a t)"),
                          ks[0:KROWS, bass.ds(nslot, 1), j, kc * CH:(kc + 1) * CH].rearrange("p a t -> p (a t)"),
                          start=True, stop=True).then_inc(m_ps, 1)

            def sums(x, pos, part, n=None):
                if part == 0:
                    pe.wait_ge(o_sb, (x if n is None else n) + 1)
                    for q in range(TILES):
                        mm = pe.matmul(ps_m[SLOT * q:SLOT * (q + 1), pos % 3, 0:P], sel[:, :], ou[:, q * P:(q + 1) * P],
                                       start=True, stop=True)
                else:
                    pe.wait_ge(orc_ready, (x if n is None else n) + 1)
                    for q in range(TILES):
                        mm = pe.matmul(ps_m[:, pos % 3, q * P:(q + 1) * P], spread[:, q, :], orc[:, :],
                                       start=True, stop=True)
                mm.then_inc(m_ps, 1)

            def max_rows(x, pos):
                pe.wait_ge(nmp_ready, x + 1)
                pe.transpose(ps_m[:, pos % 3, 0:P // 2].bitcast(BF16),
                             nmp[:, :, :].rearrange("p s n -> p (s n)"), identb[:, :]).then_inc(m_ps, 1)

            def weigh(kt, ready):
                pe.wait_ge(p_ready, ready)
                for j in range(GRP):
                    mm = pe.matmul(ps_o[SLOT * j:SLOT * (j + 1), :], vg[:, kt, j, :], pr[:, kt % 2, j, :],
                                   start=(kt == 0), stop=(kt == KT - 1), skip_group_check=True)
                mm.then_inc(pv_done, 1)
                return mm

            def fill(x, plan, pos, sets):
                op = plan[pos]
                bank_free(x, plan, pos)
                if op[0] == "max":
                    max_unit(x, op[2], pos, *sets[op[1]])
                elif op[0] == "sum":
                    sums(x, pos, op[1])
                else:
                    max_rows(x, pos)

            def iteration(x, steps, plan, q, slot, group, sets, groups):
                pos = 0
                pe.wait_ge(neg_ld, x * 16)
                for kk in range(KT):
                    left = len(steps[kk])
                    if sets and kk == 0:
                        pe.wait_ge(qk_ready, groups[0])
                    if sets and kk == KT - AHEAD:
                        pe.wait_ge(qk_ready, groups[1])
                    for pair in range(2):
                        pe.wait_ge(p_ready, x * (2 * KT) + (2 * kk + pair + 1 - 2 * KT))
                        for jj in range(2):
                            j = 2 * pair + jj
                            mm = pe.matmul(ps_s[:, pair, jj, :],
                                           ks[:, bass.ds(slot, 1), j, kk * P:(kk + 1) * P].rearrange("p a t -> p (a t)"),
                                           qs[:, bass.ds(q, 1), j, :].rearrange("p a t -> p (a t)"),
                                           start=True, stop=True)
                        mm.then_inc(s_ps, 1)
                        if left > 1:
                            fill(x, plan, pos, sets)
                            pos, left = pos + 1, left - 1
                    if kk == 1:
                        pe.wait_ge(va_ld, group * 16 + 16)
                        pe.wait_ge(o_sb, x + 1)
                    if kk == 9:
                        pe.wait_ge(vb_ld, group * 16 + 16)
                    if kk == KT - 1:
                        pe.wait_ge(vc_ld, group * 16 + 16)
                    weigh((kk - 1) % KT, x * (2 * KT) + (2 * kk + 2 - 2 * KT))
                    for _ in range(left):
                        fill(x, plan, pos, sets)
                        pos += 1

            pe.wait_ge(k0_ld, 16 * 12)
            for pos in range(CARRY):
                if pos >= 3:
                    pe.wait_ge(m_read, pos - 2)
                max_unit(0, pos, pos, 0, 0)
            for pos, op in enumerate(PLAN):
                if op == ("max", 1, 0):
                    pe.wait_ge(q0_ld, 16 * (6 * (NCH - 1) + 1))
                fill(0, PLAN, pos, ((0, 0), (1, 0)))
            pe.wait_ge(vc_ld, 16)
            for j in range(GRP):
                pe.matmul(ps_o[SLOT * j:SLOT * (j + 1), :], vg[:, KT - 1, j, :], pr[:, 1, j, :],
                          start=True, stop=False, skip_group_check=True)
            with pe.Fori(1, ITERS) as x:
                group = [pe.snap((x + d) >> (NCH.bit_length() - 1)) for d in (-1, 0, 1)]
                q = [pe.snap((x + d) & (HG * NCH - 1)) for d in (-1, 0, 1)]
                slot = [pe.snap(g & (HG - 1)) for g in group]
                iteration(x, LOOP, PLAN, q[0], slot[0], group[0], ((q[1], slot[1]), (q[2], slot[2])), group[1:])
            iteration(ITERS, LAST, END_PLAN, HG * NCH - 1, HG - 1, NGROUP - 1, None, None)
            weigh(KT - 1, 2 * KT * ITERS + 2)
            for pos in (2, 3):
                bank_free(ITERS, END_PLAN, pos)
                sums(ITERS, pos, pos - 2, ITERS + 1)

        @block.scalar
        def _(act):
            first_k(act, range(3, 6))
            first_q(act, (0,), k0_ld)
            act.wait_ge(filled, 3)
            act.sem_inc(p_ready, 2)

            def take_output(x):
                act.wait_ge(pv_done, x * KT + (2 - KT))
                act.wait_ge(on_ready, x)
                act.copy(ou[:, :], ps_o[:, :]).then_inc(o_sb, 1)

            with act.Fori(0, NGROUP) as G:
                for d in range(NCH):
                    i = G * NCH + d
                    for kk in range(KT):
                        act.wait_ge(pv_done, i * KT + (kk + 1))
                        for pair in range(2):
                            act.wait_ge(s_ps, i * (2 * KT) + (2 * kk + pair + 1))
                            act.activation(pr[:, kk % 2, 2 * pair:2 * pair + 2, :], ps_s[:, pair, :, :], ACT.Exp,
                                           scale=HD ** -0.5).then_inc(p_ready, 1)
                        if kk == 0:
                            take_output(i + 1)
            take_output(ITERS + 1)

        @block.vector
        def _(dve):
            dve.wait_ge(filled, 3)
            dve.sem_inc(o_sb, 1)

            def max_unit(x, u, pos):
                dve.wait_ge(m_ps, taken(x) + (pos + 1))
                j, qt, kc = unit_place(u)
                return dve.tensor_reduce(mx[:, j * TILES + qt, kc:kc + 1], ps_m[:, pos % 3, :], AX_X, ALU.max).then_inc(m_read, 1)

            def sums(x, pos, part, n=None):
                dve.wait_ge(m_ps, taken(x) + (pos + 1))
                if part == 0:
                    dve.reciprocal(orc[:, :], ps_m[:, pos % 3, 0:P]).then_inc(orc_ready, 1)
                else:
                    n = x if n is None else n
                    if not isinstance(n, int) or n:
                        dve.wait_ge(o_stored, n * 16)
                    dve.tensor_tensor(on[:, :], ou[:, :], ps_m[:, pos % 3, :], ALU.mult).then_inc(on_ready, 1)

            def max_parts(x):
                NS = 5

                def after(n):
                    dve.wait_ge(nm_step, x * NS + n)

                dve.wait_ge(m_read, x * MAXU + MAXU)
                dve.tensor_reduce(nm[:, :], mx[:, :, :], AX_X, ALU.max, negate=True).then_inc(nm_step, 1)
                after(1)
                yield
                dve.tensor_copy(nmp[:, 0, :], nm[:, :]).then_inc(nm_step, 1)
                yield
                after(2)
                dve.tensor_tensor(nmr[:, :], nm[:, :], nmp[:, 0, :], ALU.subtract).then_inc(nm_step, 1)
                yield
                after(3)
                dve.tensor_copy(nmp[:, 1, :], nmr[:, :]).then_inc(nm_step, 1)
                yield
                after(4)
                dve.tensor_tensor(nmp[:, 2, :], nmr[:, :], nmp[:, 1, :], ALU.subtract).then_inc(nm_step, 1)
                yield
                after(5)
                dve.sem_inc(nmp_ready, 1)

            def max_rows(x, pos):
                dve.wait_ge(m_ps, taken(x) + (pos + 1))
                if not (isinstance(x, int) and x == 0):
                    dve.wait_ge(neg_ld, x * 16)
                dve.tensor_copy(nmt[:, :], ps_m[0:PARTS * 16, pos % 3, 0:P // 2].bitcast(BF16)).then_inc(nmt_sb, 1)

            def iteration(x, plan):
                steps = iter(())
                for pos, op in enumerate(plan):
                    if op[0] == "max":
                        max_unit(x, op[2], pos)
                        next(steps, None)
                    elif op[0] == "sum":
                        sums(x, pos, op[1])
                    else:
                        max_rows(x, pos)
                    if op[0] == "max" and op[2] == MAXU - 1:
                        steps = max_parts(x)
                        next(steps)

            for pos in range(CARRY):
                max_unit(-1, pos, pos + (len(PLAN) - CARRY))
            iteration(0, PLAN)
            with dve.Fori(1, ITERS) as x:
                iteration(x, PLAN)
            iteration(ITERS, END_PLAN[:2])
            for part in range(2):
                sums(ITERS, 2 + part, part, ITERS + 1)


def final_stage(nc, I, D, out):
    with ExitStack() as ctx:
        sb = lambda n, s, d: ctx.enter_context(nc.sbuf_tensor(n, s, d))
        sem = lambda n: ctx.enter_context(nc.semaphore("f_" + n))
        PS = ctx.enter_context(nc.psum_tensor("PSf", [P, 8, CH], F32))
        ones = sb("f_ones", [P, P], F32)
        spread = sb("f_spread", [P, TILES, P], F32)
        eps = sb("f_eps", [P, 1], F32)
        wo = sb("f_wo", [P, HG, C], F32)
        xc = sb("f_xc", [P, 2, KC, CH], F32)
        oT = sb("f_oT", [P, 2, HG, CH], F32)
        mtc = sb("f_mtc", [P, 2, KC, C], F32)
        bcc = sb("f_bcc", [P, 2, KC], F32)
        filled, const_ld, y_ps, x_added, ffn_ps, x_updated = (
            sem(n) for n in ("filled", "const_ld", "y_ps", "x_added", "ffn_ps", "x_updated"))
        o_ld, rest_ld, stored = ([sem(n + str(s)) for s in range(2)] for n in ("o_ld", "rest_ld", "stored"))
        ln = LayerNorm(lambda n, s, d: sb("f_" + n, s, d), sem, PS, ones, spread, eps)
        BANKS_LN = (4, 5)
        PAIRS = NG // 2
        block = ctx.enter_context(nc.Block())

        @block.sync
        def _(sp):
            sp.dma_start(wo[:, :, :], I["wo_b"].rearrange("g p n -> p g n")).then_inc(const_ld, 16)
            with sp.Fori(0, BATCH) as b:
                with sp.Fori(0, NCH // 2) as half:
                    for s in range(2):
                        i = b * (NCH // 2) + half
                        sp.wait_ge(y_ps, i * 4 + (2 * s + 2))
                        for g in range(HG):
                            sp.dma_start(oT[:, s, g, :], D["o_d"][b * (HG * NCH) + half * 2 + (2 + g * NCH + s)]).then_inc(o_ld[s], 16)
            for s in range(2):
                sp.wait_ge(stored[s], 16 * PAIRS)

        @block.gpsimd
        def _(pool):
            pool.memset(eps[:, :], EPS).then_inc(filled, 1)
            pool.memset(ones[:, :], 1.0 / C).then_inc(filled, 1)
            with pool.Fori(0, PAIRS) as i:
                for s in range(2):
                    it = i * 2 + s
                    pool.wait_ge(stored[s], i * 16)
                    pool.dma_start(xc[:, s], D["x_d"][:, bass.ds(it * CH + CH, CH)]
                                   .rearrange("(k p) t -> p k t", p=P)).then_inc(rest_ld[s], 16)
                    pool.dma_start(mtc[:, s], D["mt_d"][it + 1].rearrange("(k p) n -> p k n", p=P)).then_inc(rest_ld[s], 16)
                    pool.dma_start(bcc[:, s], D["bc_d"][it + 1].rearrange("(k p) -> p k", p=P),
                                   allow_slow_non_contiguous=True).then_inc(rest_ld[s], 16)

        @block.tensor
        def _(pe):
            pe.sem_inc(y_ps, 4)

            def project(i, s, m):
                if m == 0:
                    pe.wait_ge(o_ld[s], i * (16 * HG) + 16 * HG)
                for g in range(HG):
                    mm = pe.matmul(PS[:, 2 * s + m, :], wo[:, g, m * P:(m + 1) * P], oT[:, s, g, :],
                                   start=(g == 0), stop=(g == HG - 1))
                mm.then_inc(y_ps, 1)

            def pair(i, last):
                for s in range(2):
                    n = i * 2 + (s + 1)
                    more = not (last and s == 1)
                    i2 = i if s == 0 else i + 1
                    pe.wait_ge(x_added, n)
                    ln.mean(pe, BANKS_LN, xc[:, s])
                    if more:
                        project(i2, 1 - s, 0)
                    ln.var(pe, n, BANKS_LN)
                    if more:
                        project(i2, 1 - s, 1)
                    ln.back(pe, n, BANKS_LN)
                    pe.wait_ge(ln.xn_ready, n)
                    for m in range(KC):
                        for k in range(KC):
                            mm = pe.matmul(PS[:, 6 + m, :], mtc[:, s, k, m * P:(m + 1) * P], ln.xn[:, k, :],
                                           start=(k == 0), stop=(k == KC - 1))
                        mm.then_inc(ffn_ps, 1)

            pe.wait_ge(filled, 2)
            pe.wait_ge(const_ld, 32)
            for m in range(KC):
                project(0, 0, m)
            with pe.Fori(0, PAIRS - 1) as i:
                pair(i, False)
            pair(PAIRS - 1, True)

        @block.scalar
        def _(act):
            act.dma_start(spread[:, :, :], I["spread"]).then_inc(const_ld, 16)
            act.wait_ge(filled, 2)
            with act.Fori(0, PAIRS) as i:
                for s in range(2):
                    n = i * 2 + (s + 1)
                    ln.square(act, n)
                    ln.root(act, n, BANKS_LN)
                    act.wait_ge(x_updated, n)
                    act.dma_start(out[:, bass.ds(i * (2 * CH) + s * CH, CH)].rearrange("(k p) t -> p k t", p=P),
                                  xc[:, s]).then_inc(stored[s], 16)

        @block.vector
        def _(dve):
            def add(i, s):
                dve.wait_ge(rest_ld[s], i * 48 + 48)
                dve.wait_ge(y_ps, i * 4 + (2 * s + 6))
                dve.tensor_tensor(xc[:, s], xc[:, s], PS[:, 2 * s:2 * s + KC, :], ALU.add).then_inc(x_added, 1)

            def pair(i, last):
                for s in range(2):
                    n = i * 2 + (s + 1)
                    ln.center(dve, n, BANKS_LN, xc[:, s])
                    ln.inverse(dve, n)
                    ln.normalise(dve, n, BANKS_LN)
                    if not (last and s == 1):
                        add(i if s == 0 else i + 1, 1 - s)
                    dve.wait_ge(ffn_ps, i * 4 + (2 * s + 2))
                    for m in range(KC):
                        last_op = dve.scalar_tensor_tensor(out=xc[:, s, m, :], in0=PS[:, 6 + m, :], scalar=bcc[:, s, m:m + 1],
                                                           in1=xc[:, s, m, :], op0=ALU.add, op1=ALU.add)
                    last_op.then_inc(x_updated, 1)

            add(0, 0)
            with dve.Fori(0, PAIRS - 1) as i:
                pair(i, False)
            pair(PAIRS - 1, True)


def build(nc, I, out):
    dram = lambda n, s, d: nc.dram_tensor(n, s, d, kind="Internal").ap()
    D = {
        "mt_d": dram("mt_d", (1 + NG, C, C), F32),
        "bc_d": dram("bc_d", (1 + NG, C), F32),
        "v_d": dram("v_d", (BATCH, PAD + T, C), F32),
        "vb_d": dram("vb_d", (CH + BATCH * T, H * SLOT), F32),
        "x_d": dram("x_d", (C, CH + BATCH * T), F32),
        "q_d": dram("q_d", (PARTS, C, CH + BATCH * T), BF16),
        "k_d": dram("k_d", (PARTS, C, CH + BATCH * T), BF16),
        "o_d": dram("o_d", (2 + BATCH * HG * NCH, P, CH), F32),
        "identb": I["identb"],
        "one_rows": I["one_rows"],
        "sel": I["sel"],
        "spread": I["spread"],
    }
    fold_ffn(nc, I["W1"], I["W2T"], I["b1"], I["b2"], D["mt_d"], D["bc_d"])
    local_stage(nc, I, D)
    full_attention(nc, D)
    final_stage(nc, I, D, out)


def constants():
    bf = mybir.dt.np(BF16)
    f = np.float32
    inv = (f(1.0) / f(10000.0) ** (np.arange(0, HD, 2, dtype=f) / f(HD))).astype(f)
    ang = np.outer(np.arange(T, dtype=f), inv).astype(f)
    d = np.arange(P) % HD
    sign = np.where(d < HD // 2, -1.0, 1.0).astype(f)[:, None]
    cosT = np.cos(ang).astype(f).T[d % (HD // 2)]
    sinT = np.sin(ang).astype(f).T[d % (HD // 2)] * sign
    t = np.arange(T).reshape(T // P, P)
    vmask = np.where(t.T[:, :, None] >= np.array(OFFSETS)[None, None, :], f(0), np.finfo(f).min).astype(f)
    j = np.tile(np.arange(NEAR), PARTS)
    band = (np.arange(EBW)[None, :] == (2 * P - 1 - j)[:, None]).astype(bf)
    p = np.arange(P)
    chunk0 = np.zeros((P, CH), f)
    return {
        "cosT": np.concatenate([chunk0] + [cosT] * BATCH, axis=1),
        "sinT": np.concatenate([chunk0] + [sinT.astype(f)] * BATCH, axis=1), "vmask": vmask,
        "one_rows": np.ones((PARTS, HG * GRP * T), bf),
        "band": band, "ident": np.eye(P, dtype=f), "identb": np.eye(P).astype(bf),
        "hmask": (p[:, None] // HD == np.arange(8)[None, :]).astype(f),
        "sel": (p[:, None] == (np.arange(SLOT)[None, :] // 8 * SLOT + HD)).astype(f),
        "spread": (p[:, None, None] == (SLOT * np.arange(TILES)[None, :, None] + 8 * (p[None, None, :] // SLOT))).astype(f),
    }


def kernel(**inputs):
    import concourse.bacc as bacc
    from concourse.bass_utils import run_bass_kernel_spmd

    a = {k[3:]: np.asarray(v) for k, v in inputs.items()}
    tokens = BATCH * T
    wqkv_b = a["attn_b_Wqkv"]
    turned = (np.arange(2 * C) // HD) * HD + (np.arange(2 * C) + HD // 2) % HD
    tiled = lambda w: np.pad(w.reshape(HG, GRP, HD, C), ((0, 0), (0, 0), (0, SLOT - HD), (0, 0))).reshape(HG, P, C)
    arrays = {
        "xT": np.pad(a["attn_a_x"].reshape(tokens, C).T, ((0, 0), (CH, CH))),
        "wqkv": a["attn_a_w_qkv"], "wo": tiled(a["attn_a_w_out"]), "pos_bias": a["attn_a_pos_bias"],
        "se_t": a["attn_a_scale_embed"].T, "gain": a["attn_a_if_gain"],
        "wqkv_b": wqkv_b, "wrot": wqkv_b[:, turned], "wo_b": tiled(a["attn_b_Wo"]),
        "W1": a["ffn_W1"], "W2T": a["ffn_W2"].transpose(0, 2, 1), "b1": a["ffn_b1"].reshape(NG, INTER // P, P).transpose(0, 2, 1), "b2": a["ffn_b2"],
        **constants(),
    }
    arrays = {n: np.ascontiguousarray(v) for n, v in arrays.items()}
    nc = bacc.Bacc("TRN2", target_bir_lowering=False, num_devices=1)
    I = {n: nc.dram_tensor("in_" + n, v.shape, mybir.dt.from_np(v.dtype), kind="ExternalInput").ap()
         for n, v in arrays.items()}
    out = nc.dram_tensor("out_T", (C, tokens), F32, kind="ExternalOutput").ap()
    build(nc, I, out)
    r = run_bass_kernel_spmd(nc, [{"in_" + n: v for n, v in arrays.items()}], core_ids=[0])
    return r.results[0]["out_T"].T.reshape(BATCH, T, C)
```
